# Optimizing a Trainium2 kernel written in Bass

```python
import numpy as np
import jax
import jax.numpy as jnp

def _softmax(x, axis=-1):
    return jax.nn.softmax(x, axis=axis)

def _gelu(x):
    return jax.nn.gelu(x, approximate=True)

def _silu(x):
    return jax.nn.silu(x)

def _sigmoid(x):
    return jax.nn.sigmoid(x)

def _layernorm(x, axis=-1, eps=1e-05):
    m = jnp.mean(x, axis=axis, keepdims=True)
    v = jnp.var(x, axis=axis, keepdims=True)
    return (x - m) / jnp.sqrt(v + eps)

def _scatter_add(tgt, idx, src, axis=0):
    return tgt.at[idx].add(src)

def _segment_sum(src, seg, n):
    return jax.ops.segment_sum(src, seg, n)
kernel_name = 'mk_flamingo_gated_d4_seqx_r4_de1ee5'

def setup_inputs(seed: int=0):
    np.random.seed(seed)
    _w = jnp.asarray

    def _rec_inputs():
        import jax
        import jax.numpy as jnp
        _rk = jax.random.key(seed)
        x = 7.22e-05 + 1 * jax.random.normal(jax.random.fold_in(_rk, 1), (8, 256, 256), jnp.float32)
        _lenS = 256 - jax.random.randint(jax.random.fold_in(_rk, 7), (8,), 0, max(1, 256 // 4) + 1, jnp.int32)
        _lenS2 = 256 - jax.random.randint(jax.random.fold_in(_rk, 8), (8,), 0, max(1, 256 // 4) + 1, jnp.int32)
        _ctx_1024P = jax.random.normal(jax.random.fold_in(_rk, 11), (8, 16, 256), jnp.float32)
        _ctx_1024c = jax.random.dirichlet(jax.random.fold_in(_rk, 511), 0.3 * jnp.ones((16,), jnp.float32), (8, 256))
        _ctx_1024t = jnp.einsum('bsk,bkd->bsd', _ctx_1024c, _ctx_1024P)
        _ctx_1024t = _ctx_1024t * jax.lax.rsqrt(jnp.mean(jnp.square(_ctx_1024t)) + 1e-12) * 0.953939
        ctx_1024 = 4.13588e-05 + 0.999923 * (_ctx_1024t + 0.3 * jax.random.normal(jax.random.fold_in(_rk, 611), (8, 256, 256), jnp.float32))
        _validS = jnp.arange(256)[None, :] < _lenS[:, None]
        _validS2 = jnp.arange(256)[None, :] < _lenS2[:, None]
        _causal = jnp.tril(jnp.ones((256, 256), dtype=bool))
        mask_Bx1xSxS2_ik1 = jnp.where(jnp.broadcast_to(_validS2[:, None, None, :], (8, 1, 256, 256)), 1, 0).astype(jnp.int32)
        _g = jax.random.normal(jax.random.fold_in(_rk, 9001), (2, 4), jnp.float32)
        _g = jnp.sign(_g) * jnp.maximum(jnp.abs(_g), 1.0) + (_g == 0) * 1.0
        g_xattn = _g[0]
        g_ffn = _g[1]
        return (x, ctx_1024, mask_Bx1xSxS2_ik1, g_xattn, g_ffn)
    x, ctx_1024, mask_Bx1xSxS2_ik1, g_xattn, g_ffn = _rec_inputs()

    def _L0_xattn_setup():
        import jax, jax.numpy as jnp
        import numpy as np
        D_MODEL = 256
        N_HEADS = 16
        D_K = D_MODEL // N_HEADS
        NEG = -1000000000.0
        key = jax.random.key(seed)
        k1, k2, k3, k4 = jax.random.split(key, 4)
        B, S = (4, 512)
        query = jax.random.normal(k1, (B, S, D_MODEL), dtype=jnp.float32)
        key_t = jax.random.normal(k2, (B, S, D_MODEL), dtype=jnp.float32)
        value = jax.random.normal(k3, (B, S, D_MODEL), dtype=jnp.float32)
        mask = jax.random.randint(k4, (B, 1, S, S), 0, 2, dtype=jnp.int32)
        return {'query': query, 'key': key_t, 'value': value, 'mask': mask}
    _L0_xattn_all = _L0_xattn_setup()
    _L0_xattn_in = {k: v for k, v in _L0_xattn_all.items() if k in ()}
    del _L0_xattn_all

    def _L0_ffn_setup():
        import jax, jax.numpy as jnp
        import numpy as np
        DIM = 256
        NUM_HEAVY = 256
        N_ITERS = 50
        EPS = 1.0
        FETCH_K_RATIO = 9.0 / 8.0

        def rms_norm(x, gamma):
            norm = jnp.maximum(jnp.linalg.norm(x, axis=-1, keepdims=True), 1e-12)
            return x / norm * x.shape[-1] ** 0.5 * gamma

        def feed_forward(x, gamma, w1, b1, w2, b2):
            h = jax.nn.gelu(rms_norm(x, gamma) @ w1 + b1, approximate=False)
            return h @ w2 + b2

        def coor_descent(s, k, n_iters, eps):
            logk = jnp.log(jnp.asarray(k, dtype=s.dtype))

            def step(ab, _):
                a, b = ab
                sb = (s + b) / eps
                a = eps * (logk - jax.scipy.special.logsumexp(sb, axis=-1, keepdims=True))
                b = -jax.nn.relu(s + a)
                return ((a, b), None)
            a0 = jnp.zeros_like(s[..., :1])
            b0 = -s
            (a, b), _ = jax.lax.scan(step, (a0, b0), None, length=n_iters)
            return jnp.exp((s + a + b) / eps)
        key = jax.random.key(seed)
        ks = jax.random.split(key, 8)
        b, n, d = (4, 2048, DIM)
        dl, dh = (int(d * 0.5), d * 4)
        u = lambda k, shape, fan_in: jax.random.uniform(k, shape, jnp.float32, -1.0, 1.0) / np.sqrt(fan_in)
        return {'x': jax.random.normal(ks[0], (b, n, d), jnp.float32), 'routing_token': jax.random.normal(ks[1], (d,), jnp.float32), 'light_gamma': jnp.ones((d,), jnp.float32), 'light_w1': u(ks[2], (d, dl), d), 'light_b1': jnp.zeros((dl,), jnp.float32), 'light_w2': u(ks[3], (dl, d), dl), 'light_b2': jnp.zeros((d,), jnp.float32), 'heavy_gamma': jnp.ones((d,), jnp.float32), 'heavy_w1': u(ks[4], (d, dh), d), 'heavy_b1': jnp.zeros((dh,), jnp.float32), 'heavy_w2': u(ks[5], (dh, d), dh), 'heavy_b2': jnp.zeros((d,), jnp.float32)}
    _L0_ffn_all = _L0_ffn_setup()
    _L0_ffn_in = {k: v for k, v in _L0_ffn_all.items() if k in ('routing_token', 'light_gamma', 'light_w1', 'light_b1', 'light_w2', 'light_b2', 'heavy_gamma', 'heavy_w1', 'heavy_b1', 'heavy_w2', 'heavy_b2')}
    del _L0_ffn_all

    def _L1_xattn_setup():
        import jax, jax.numpy as jnp
        import numpy as np
        import math
        B, S, D, H = (4, 512, 256, 16)
        DK = D // H
        key = jax.random.key(seed)
        ks = jax.random.split(key, 11)
        mk = lambda k, shape: jax.random.normal(k, shape, dtype=jnp.float32)
        inp = {'query': mk(ks[0], (B, S, D)), 'key': mk(ks[1], (B, S, D)), 'value': mk(ks[2], (B, S, D)), 'Wq': mk(ks[3], (D, D)) * 0.02, 'bq': jnp.zeros((D,), jnp.float32), 'Wk': mk(ks[4], (D, D)) * 0.02, 'bk': jnp.zeros((D,), jnp.float32), 'Wv': mk(ks[5], (D, D)) * 0.02, 'bv': jnp.zeros((D,), jnp.float32), 'Wo': mk(ks[6], (D, D)) * 0.02, 'bo': jnp.zeros((D,), jnp.float32)}
        return inp
    _L1_xattn_all = _L1_xattn_setup()
    _L1_xattn_in = {k: v for k, v in _L1_xattn_all.items() if k in ('Wq', 'bq', 'Wk', 'bk', 'Wv', 'bv', 'Wo', 'bo')}
    del _L1_xattn_all

    def _L1_ffn_setup():
        import jax, jax.numpy as jnp
        import numpy as np
        DIM, E, K, H = (256, 8, 2, 1024)
        key = jax.random.key(seed)
        ks = jax.random.split(key, 5)
        s_in = 1.0 / np.sqrt(DIM)
        s_h = 1.0 / np.sqrt(H)
        return {'x': jax.random.normal(ks[0], (4, 512, DIM), dtype=jnp.float32), 'Wr': jax.random.normal(ks[1], (DIM, E), dtype=jnp.float32) * s_in, 'W1': jax.random.normal(ks[2], (E, DIM, H), dtype=jnp.float32) * s_in, 'b1': jnp.zeros((E, H), dtype=jnp.float32), 'W2': jax.random.normal(ks[3], (E, H, DIM), dtype=jnp.float32) * s_h, 'b2': jnp.zeros((E, DIM), dtype=jnp.float32)}
    _L1_ffn_all = _L1_ffn_setup()
    _L1_ffn_in = {k: v for k, v in _L1_ffn_all.items() if k in ('Wr', 'W1', 'b1', 'W2', 'b2')}
    del _L1_ffn_all

    def _L2_xattn_setup():
        import jax, jax.numpy as jnp
        import numpy as np
        EMBED = 256
        HEADS = 16
        HEAD_DIM = EMBED // HEADS
        key = jax.random.key(seed)
        ks = jax.random.split(key, 7)
        B, Sd, Se = (4, 512, 512)
        dec = jax.random.normal(ks[0], (B, Sd, EMBED), dtype=jnp.float32)
        enc = jax.random.normal(ks[1], (B, Se, EMBED), dtype=jnp.float32)
        scale = 1.0 / np.sqrt(EMBED)
        W_q = jax.random.normal(ks[2], (EMBED, EMBED), dtype=jnp.float32) * scale
        W_k = jax.random.normal(ks[3], (EMBED, EMBED), dtype=jnp.float32) * scale
        W_v = jax.random.normal(ks[4], (EMBED, EMBED), dtype=jnp.float32) * scale
        W_o = jax.random.normal(ks[5], (EMBED, EMBED), dtype=jnp.float32) * scale
        b_o = jax.random.normal(ks[6], (EMBED,), dtype=jnp.float32) * 0.01
        return {'decoder_input': dec, 'encoder_output': enc, 'W_q': W_q, 'W_k': W_k, 'W_v': W_v, 'W_o': W_o, 'b_o': b_o}
    _L2_xattn_all = _L2_xattn_setup()
    _L2_xattn_in = {k: v for k, v in _L2_xattn_all.items() if k in ('W_q', 'W_k', 'W_v', 'W_o', 'b_o')}
    del _L2_xattn_all

    def _L2_ffn_setup():
        import jax, jax.numpy as jnp
        import numpy as np
        D_MODEL, HIDDEN, N_EXPERTS, TOP_K = (256, 512, 8, 2)
        RMS_EPS = 1e-06
        key = jax.random.key(seed)
        ks = jax.random.split(key, 6)
        B, S = (4, 512)
        return {'x': jax.random.normal(ks[0], (B, S, D_MODEL), jnp.float32), 'norm_weight': jnp.ones((D_MODEL,), jnp.float32), 'gate_w': jax.random.normal(ks[1], (N_EXPERTS, D_MODEL), jnp.float32) * 0.02, 'w1': jax.random.normal(ks[2], (N_EXPERTS, HIDDEN, D_MODEL), jnp.float32) * 0.02, 'b1': jnp.zeros((N_EXPERTS, HIDDEN), jnp.float32), 'w2': jax.random.normal(ks[3], (N_EXPERTS, D_MODEL, HIDDEN), jnp.float32) * 0.02, 'b2': jnp.zeros((N_EXPERTS, D_MODEL), jnp.float32)}
    _L2_ffn_all = _L2_ffn_setup()
    _L2_ffn_in = {k: v for k, v in _L2_ffn_all.items() if k in ('norm_weight', 'gate_w', 'w1', 'b1', 'w2', 'b2')}
    del _L2_ffn_all

    def _L3_xattn_setup():
        import jax, jax.numpy as jnp
        import numpy as np
        EMBED = 256
        ATTN = 256
        HEADS = 16
        HEAD_DIM = ATTN // HEADS
        key = jax.random.key(seed)
        ks = jax.random.split(key, 8)
        s = 1.0 / np.sqrt(EMBED)
        sa = 1.0 / np.sqrt(ATTN)
        return {'queries': jax.random.normal(ks[0], (4, 128, EMBED), jnp.float32), 'context': jax.random.normal(ks[1], (4, 512, EMBED), jnp.float32), 'Wq': jax.random.normal(ks[2], (EMBED, ATTN), jnp.float32) * s, 'bq': jnp.zeros((ATTN,), jnp.float32), 'Wkv': jax.random.normal(ks[3], (EMBED, 2 * ATTN), jnp.float32) * s, 'bkv': jnp.zeros((2 * ATTN,), jnp.float32), 'Wo': jax.random.normal(ks[4], (ATTN, EMBED), jnp.float32) * sa, 'bo': jnp.zeros((EMBED,), jnp.float32)}
    _L3_xattn_all = _L3_xattn_setup()
    _L3_xattn_in = {k: v for k, v in _L3_xattn_all.items() if k in ('Wq', 'bq', 'Wkv', 'bkv', 'Wo', 'bo')}
    del _L3_xattn_all

    def _L3_ffn_setup():
        import jax, jax.numpy as jnp
        import numpy as np
        B, S, D_MODEL, D_HIDDEN = (4, 512, 256, 1024)

        def act_quant(x):
            scale = 127.0 / jnp.clip(jnp.max(jnp.abs(x), axis=-1, keepdims=True), 1e-05)
            return jnp.clip(jnp.round(x * scale), -128, 127) / scale

        def weight_quant(w):
            scale = 1.0 / jnp.clip(jnp.mean(jnp.abs(w)), 1e-05)
            return jnp.clip(jnp.round(w * scale), -1, 1) / scale

        def bit_linear(x, w):
            xq = x + jax.lax.stop_gradient(act_quant(x) - x)
            wq = w + jax.lax.stop_gradient(weight_quant(w) - w)
            return jnp.einsum('bsd,hd->bsh', xq, wq)

        def depthwise_conv1d(x_bcl, w, b):
            y = jax.lax.conv_general_dilated(x_bcl, w, window_strides=(1,), padding=[(1, 1)], dimension_numbers=('NCH', 'OIH', 'NCH'), feature_group_count=x_bcl.shape[1])
            return y + b[None, :, None]
        key = jax.random.key(seed)
        ks = jax.random.split(key, 5)
        lim1 = 1.0 / np.sqrt(D_MODEL)
        lim2 = 1.0 / np.sqrt(D_HIDDEN)
        limc = 1.0 / np.sqrt(3.0)
        return {'x': jax.random.normal(ks[0], (B, S, D_MODEL), dtype=jnp.float32), 'w1': jax.random.uniform(ks[1], (D_HIDDEN, D_MODEL), jnp.float32, -lim1, lim1), 'conv_w': jax.random.uniform(ks[2], (D_HIDDEN, 1, 3), jnp.float32, -limc, limc), 'conv_b': jax.random.uniform(ks[3], (D_HIDDEN,), jnp.float32, -limc, limc), 'w2': jax.random.uniform(ks[4], (D_MODEL, D_HIDDEN), jnp.float32, -lim2, lim2)}
    _L3_ffn_all = _L3_ffn_setup()
    _L3_ffn_in = {k: v for k, v in _L3_ffn_all.items() if k in ('w1', 'conv_w', 'conv_b', 'w2')}
    del _L3_ffn_all
    return {'x': x, 'ctx_1024': ctx_1024, 'mask_Bx1xSxS2_ik1': mask_Bx1xSxS2_ik1, 'g_xattn': g_xattn, 'g_ffn': g_ffn, 'L0_ffn_routing_token': _L0_ffn_in['routing_token'], 'L0_ffn_light_gamma': _L0_ffn_in['light_gamma'], 'L0_ffn_light_w1': _L0_ffn_in['light_w1'], 'L0_ffn_light_b1': _L0_ffn_in['light_b1'], 'L0_ffn_light_w2': _L0_ffn_in['light_w2'], 'L0_ffn_light_b2': _L0_ffn_in['light_b2'], 'L0_ffn_heavy_gamma': _L0_ffn_in['heavy_gamma'], 'L0_ffn_heavy_w1': _L0_ffn_in['heavy_w1'], 'L0_ffn_heavy_b1': _L0_ffn_in['heavy_b1'], 'L0_ffn_heavy_w2': _L0_ffn_in['heavy_w2'], 'L0_ffn_heavy_b2': _L0_ffn_in['heavy_b2'], 'L1_xattn_Wq': _L1_xattn_in['Wq'], 'L1_xattn_bq': _L1_xattn_in['bq'], 'L1_xattn_Wk': _L1_xattn_in['Wk'], 'L1_xattn_bk': _L1_xattn_in['bk'], 'L1_xattn_Wv': _L1_xattn_in['Wv'], 'L1_xattn_bv': _L1_xattn_in['bv'], 'L1_xattn_Wo': _L1_xattn_in['Wo'], 'L1_xattn_bo': _L1_xattn_in['bo'], 'L1_ffn_Wr': _L1_ffn_in['Wr'], 'L1_ffn_W1': _L1_ffn_in['W1'], 'L1_ffn_b1': _L1_ffn_in['b1'], 'L1_ffn_W2': _L1_ffn_in['W2'], 'L1_ffn_b2': _L1_ffn_in['b2'], 'L2_xattn_W_q': _L2_xattn_in['W_q'], 'L2_xattn_W_k': _L2_xattn_in['W_k'], 'L2_xattn_W_v': _L2_xattn_in['W_v'], 'L2_xattn_W_o': _L2_xattn_in['W_o'], 'L2_xattn_b_o': _L2_xattn_in['b_o'], 'L2_ffn_norm_weight': _L2_ffn_in['norm_weight'], 'L2_ffn_gate_w': _L2_ffn_in['gate_w'], 'L2_ffn_w1': _L2_ffn_in['w1'], 'L2_ffn_b1': _L2_ffn_in['b1'], 'L2_ffn_w2': _L2_ffn_in['w2'], 'L2_ffn_b2': _L2_ffn_in['b2'], 'L3_xattn_Wq': _L3_xattn_in['Wq'], 'L3_xattn_bq': _L3_xattn_in['bq'], 'L3_xattn_Wkv': _L3_xattn_in['Wkv'], 'L3_xattn_bkv': _L3_xattn_in['bkv'], 'L3_xattn_Wo': _L3_xattn_in['Wo'], 'L3_xattn_bo': _L3_xattn_in['bo'], 'L3_ffn_w1': _L3_ffn_in['w1'], 'L3_ffn_conv_w': _L3_ffn_in['conv_w'], 'L3_ffn_conv_b': _L3_ffn_in['conv_b'], 'L3_ffn_w2': _L3_ffn_in['w2']}

def reference(x, ctx_1024, mask_Bx1xSxS2_ik1, g_xattn, g_ffn, L0_ffn_routing_token, L0_ffn_light_gamma, L0_ffn_light_w1, L0_ffn_light_b1, L0_ffn_light_w2, L0_ffn_light_b2, L0_ffn_heavy_gamma, L0_ffn_heavy_w1, L0_ffn_heavy_b1, L0_ffn_heavy_w2, L0_ffn_heavy_b2, L1_xattn_Wq, L1_xattn_bq, L1_xattn_Wk, L1_xattn_bk, L1_xattn_Wv, L1_xattn_bv, L1_xattn_Wo, L1_xattn_bo, L1_ffn_Wr, L1_ffn_W1, L1_ffn_b1, L1_ffn_W2, L1_ffn_b2, L2_xattn_W_q, L2_xattn_W_k, L2_xattn_W_v, L2_xattn_W_o, L2_xattn_b_o, L2_ffn_norm_weight, L2_ffn_gate_w, L2_ffn_w1, L2_ffn_b1, L2_ffn_w2, L2_ffn_b2, L3_xattn_Wq, L3_xattn_bq, L3_xattn_Wkv, L3_xattn_bkv, L3_xattn_Wo, L3_xattn_bo, L3_ffn_w1, L3_ffn_conv_w, L3_ffn_conv_b, L3_ffn_w2):
    import jax
    import jax.numpy as jnp

    def _L0_xattn_ref(query, key, value, mask):
        import jax, jax.numpy as jnp
        import numpy as np
        D_MODEL = 256
        N_HEADS = 16
        D_K = D_MODEL // N_HEADS
        NEG = -1000000000.0
        B, S, _ = query.shape
        q = query.reshape(B, S, N_HEADS, D_K).transpose(0, 2, 1, 3)
        k = key.reshape(B, S, N_HEADS, D_K).transpose(0, 2, 1, 3)
        v = value.reshape(B, S, N_HEADS, D_K).transpose(0, 2, 1, 3)
        scale = jnp.asarray(np.sqrt(D_K), dtype=q.dtype)
        scores = jnp.einsum('bhqd,bhkd->bhqk', q, k) / scale
        scores = jnp.where(mask == 0, jnp.asarray(NEG, scores.dtype), scores)
        attn = jax.nn.softmax(scores, axis=-1)
        out = jnp.einsum('bhqk,bhkd->bhqd', attn, v)
        return out.transpose(0, 2, 1, 3).reshape(B, S, D_MODEL)

    def _L0_ffn_ref(x, routing_token, light_gamma, light_w1, light_b1, light_w2, light_b2, heavy_gamma, heavy_w1, heavy_b1, heavy_w2, heavy_b2):
        import jax, jax.numpy as jnp
        import numpy as np
        DIM = 256
        NUM_HEAVY = 256
        N_ITERS = 50
        EPS = 1.0
        FETCH_K_RATIO = 9.0 / 8.0

        def rms_norm(x, gamma):
            norm = jnp.maximum(jnp.linalg.norm(x, axis=-1, keepdims=True), 1e-12)
            return x / norm * x.shape[-1] ** 0.5 * gamma

        def feed_forward(x, gamma, w1, b1, w2, b2):
            h = jax.nn.gelu(rms_norm(x, gamma) @ w1 + b1, approximate=False)
            return h @ w2 + b2

        def coor_descent(s, k, n_iters, eps):
            logk = jnp.log(jnp.asarray(k, dtype=s.dtype))

            def step(ab, _):
                a, b = ab
                sb = (s + b) / eps
                a = eps * (logk - jax.scipy.special.logsumexp(sb, axis=-1, keepdims=True))
                b = -jax.nn.relu(s + a)
                return ((a, b), None)
            a0 = jnp.zeros_like(s[..., :1])
            b0 = -s
            (a, b), _ = jax.lax.scan(step, (a0, b0), None, length=n_iters)
            return jnp.exp((s + a + b) / eps)
        b, n, d = x.shape
        light_out = feed_forward(x, light_gamma, light_w1, light_b1, light_w2, light_b2)
        s = jnp.einsum('bnd,d->bn', x, routing_token)
        effective_k = min(NUM_HEAVY * FETCH_K_RATIO, n)
        scores = coor_descent(s, effective_k, N_ITERS, EPS)
        sel_scores, sel_idx = jax.lax.top_k(scores, NUM_HEAVY)
        sel_scores = sel_scores + jax.lax.stop_gradient(1.0 - sel_scores)
        routed = jnp.take_along_axis(x, sel_idx[..., None], axis=1)
        routed_out = feed_forward(routed, heavy_gamma, heavy_w1, heavy_b1, heavy_w2, heavy_b2)
        routed_out = routed_out * sel_scores[..., None]
        batch_idx = jnp.arange(b)[:, None]
        heavy_out = jnp.zeros_like(x).at[batch_idx, sel_idx].set(routed_out)
        return light_out + heavy_out

    def _L1_xattn_ref(query, key, value, Wq, bq, Wk, bk, Wv, bv, Wo, bo):
        import jax, jax.numpy as jnp
        import numpy as np
        import math
        B, S, D, H = (4, 512, 256, 16)
        DK = D // H
        b, s, d = query.shape
        scale = 1.0 / math.sqrt(DK)

        def proj(x, W, bias):
            return (x @ W.T + bias).reshape(b, s, H, DK).transpose(0, 2, 1, 3)
        q = proj(query, Wq, bq)
        k = proj(key, Wk, bk)
        v = proj(value, Wv, bv)
        scores = jnp.einsum('bhqd,bhkd->bhqk', q, k) * scale
        attn = jax.nn.softmax(scores, axis=-1)
        x = jnp.einsum('bhqk,bhkd->bhqd', attn, v)
        x = x.transpose(0, 2, 1, 3).reshape(b, s, d)
        return x @ Wo.T + bo

    def _L1_ffn_ref(x, Wr, W1, b1, W2, b2):
        import jax, jax.numpy as jnp
        import numpy as np
        DIM, E, K, H = (256, 8, 2, 1024)
        batch, seq, dim = x.shape
        x_flat = x.reshape(-1, dim)
        logits = x_flat @ Wr
        w, ind = jax.lax.top_k(logits, K)
        w = jax.nn.softmax(w, axis=-1)
        combine = jnp.einsum('tke,tk->te', jax.nn.one_hot(ind, E, dtype=x.dtype), w)

        def body(acc, params):
            W1e, b1e, W2e, b2e, ce = params
            h = jax.nn.gelu(x_flat @ W1e + b1e, approximate=False)
            y = h @ W2e + b2e
            return (acc + ce[:, None] * y, None)
        out0 = jnp.zeros_like(x_flat)
        out, _ = jax.lax.scan(body, out0, (W1, b1, W2, b2, combine.T))
        return out.reshape(batch, seq, dim)

    def _L2_xattn_ref(decoder_input, encoder_output, W_q, W_k, W_v, W_o, b_o):
        import jax, jax.numpy as jnp
        import numpy as np
        EMBED = 256
        HEADS = 16
        HEAD_DIM = EMBED // HEADS
        B, Sd, E = decoder_input.shape
        Se = encoder_output.shape[1]
        Q = (decoder_input @ W_q).reshape(B, Sd, HEADS, HEAD_DIM)
        K = (encoder_output @ W_k).reshape(B, Se, HEADS, HEAD_DIM)
        V = (encoder_output @ W_v).reshape(B, Se, HEADS, HEAD_DIM)
        scores = jnp.einsum('bqhd,bkhd->bhqk', Q, K) / jnp.sqrt(jnp.float32(HEAD_DIM))
        attn = jax.nn.softmax(scores, axis=-1)
        out = jnp.einsum('bhqk,bkhd->bqhd', attn, V).reshape(B, Sd, E)
        return out @ W_o + b_o

    def _L2_ffn_ref(x, norm_weight, gate_w, w1, b1, w2, b2):
        import jax, jax.numpy as jnp
        import numpy as np
        D_MODEL, HIDDEN, N_EXPERTS, TOP_K = (256, 512, 8, 2)
        RMS_EPS = 1e-06
        B, S, D = x.shape
        E = gate_w.shape[0]
        t = x * jax.lax.rsqrt(jnp.mean(x * x, axis=-1, keepdims=True) + RMS_EPS) * norm_weight
        tokens = t.reshape(-1, D)
        T = tokens.shape[0]
        gate_logits = tokens @ gate_w.T
        gate_scores, expert_idx = jax.lax.top_k(gate_logits, TOP_K)
        routing_weights = jax.nn.softmax(gate_scores, axis=-1)
        combine = jnp.zeros((T, E), tokens.dtype).at[jnp.arange(T)[:, None], expert_idx].add(routing_weights)

        def body(acc, params):
            W1, B1, W2, B2, c = params
            h = jax.nn.gelu(tokens @ W1.T + B1, approximate=False)
            o = h @ W2.T + B2
            return (acc + c[:, None] * o, None)
        out, _ = jax.lax.scan(body, jnp.zeros_like(tokens), (w1, b1, w2, b2, combine.T))
        return x + out.reshape(B, S, D)

    def _L3_xattn_ref(queries, context, Wq, bq, Wkv, bkv, Wo, bo):
        import jax, jax.numpy as jnp
        import numpy as np
        EMBED = 256
        ATTN = 256
        HEADS = 16
        HEAD_DIM = ATTN // HEADS
        B, Lq, _ = queries.shape
        Lk = context.shape[1]
        q = queries @ Wq + bq
        kv = context @ Wkv + bkv
        k, v = jnp.split(kv, 2, axis=-1)
        q = q.reshape(B, Lq, HEADS, HEAD_DIM)
        k = k.reshape(B, Lk, HEADS, HEAD_DIM)
        v = v.reshape(B, Lk, HEADS, HEAD_DIM)
        scale = 1.0 / np.sqrt(HEAD_DIM)
        scores = jnp.einsum('bqhd,bkhd->bhqk', q, k) * scale
        attn = jax.nn.softmax(scores, axis=-1)
        x = jnp.einsum('bhqk,bkhd->bqhd', attn, v).reshape(B, Lq, ATTN)
        return x @ Wo + bo

    def _L3_ffn_ref(x, w1, conv_w, conv_b, w2):
        import jax, jax.numpy as jnp
        import numpy as np
        B, S, D_MODEL, D_HIDDEN = (4, 512, 256, 1024)

        def act_quant(x):
            scale = 127.0 / jnp.clip(jnp.max(jnp.abs(x), axis=-1, keepdims=True), 1e-05)
            return jnp.clip(jnp.round(x * scale), -128, 127) / scale

        def weight_quant(w):
            scale = 1.0 / jnp.clip(jnp.mean(jnp.abs(w)), 1e-05)
            return jnp.clip(jnp.round(w * scale), -1, 1) / scale

        def bit_linear(x, w):
            xq = x + jax.lax.stop_gradient(act_quant(x) - x)
            wq = w + jax.lax.stop_gradient(weight_quant(w) - w)
            return jnp.einsum('bsd,hd->bsh', xq, wq)

        def depthwise_conv1d(x_bcl, w, b):
            y = jax.lax.conv_general_dilated(x_bcl, w, window_strides=(1,), padding=[(1, 1)], dimension_numbers=('NCH', 'OIH', 'NCH'), feature_group_count=x_bcl.shape[1])
            return y + b[None, :, None]
        h = bit_linear(x, w1)
        h = depthwise_conv1d(h.transpose(0, 2, 1), conv_w, conv_b)
        h = h.transpose(0, 2, 1)
        h = jax.nn.silu(h)
        return bit_linear(h, w2)
    x = x + jnp.tanh(g_xattn[0]) * _L0_xattn_ref(_layernorm(x, axis=-1), ctx_1024, ctx_1024, mask_Bx1xSxS2_ik1)
    x = x + jnp.tanh(g_ffn[0]) * _L0_ffn_ref(_layernorm(x, axis=-1), L0_ffn_routing_token, L0_ffn_light_gamma, L0_ffn_light_w1, L0_ffn_light_b1, L0_ffn_light_w2, L0_ffn_light_b2, L0_ffn_heavy_gamma, L0_ffn_heavy_w1, L0_ffn_heavy_b1, L0_ffn_heavy_w2, L0_ffn_heavy_b2)
    x = x + jnp.tanh(g_xattn[1]) * _L1_xattn_ref(_layernorm(x, axis=-1), ctx_1024, ctx_1024, L1_xattn_Wq, L1_xattn_bq, L1_xattn_Wk, L1_xattn_bk, L1_xattn_Wv, L1_xattn_bv, L1_xattn_Wo, L1_xattn_bo)
    x = x + jnp.tanh(g_ffn[1]) * _L1_ffn_ref(_layernorm(x, axis=-1), L1_ffn_Wr, L1_ffn_W1, L1_ffn_b1, L1_ffn_W2, L1_ffn_b2)
    x = x + jnp.tanh(g_xattn[2]) * _L2_xattn_ref(_layernorm(x, axis=-1), ctx_1024, L2_xattn_W_q, L2_xattn_W_k, L2_xattn_W_v, L2_xattn_W_o, L2_xattn_b_o)
    x = x + jnp.tanh(g_ffn[2]) * _L2_ffn_ref(_layernorm(x, axis=-1), L2_ffn_norm_weight, L2_ffn_gate_w, L2_ffn_w1, L2_ffn_b1, L2_ffn_w2, L2_ffn_b2)
    x = x + jnp.tanh(g_xattn[3]) * _L3_xattn_ref(_layernorm(x, axis=-1), ctx_1024, L3_xattn_Wq, L3_xattn_bq, L3_xattn_Wkv, L3_xattn_bkv, L3_xattn_Wo, L3_xattn_bo)
    x = x + jnp.tanh(g_ffn[3]) * _L3_ffn_ref(_layernorm(x, axis=-1), L3_ffn_w1, L3_ffn_conv_w, L3_ffn_conv_b, L3_ffn_w2)
    return x

_drawn_inputs = setup_inputs


def setup_inputs(seed=0):
    import zlib

    import numpy as np

    out = dict(_drawn_inputs(seed))
    spreads = {'L0_ffn_light_gamma': (1.0, 0.2),
     'L0_ffn_light_b1': (0.0, 0.1),
     'L0_ffn_light_b2': (0.0, 0.1),
     'L0_ffn_heavy_gamma': (1.0, 0.2),
     'L0_ffn_heavy_b1': (0.0, 0.1),
     'L0_ffn_heavy_b2': (0.0, 0.1),
     'L1_xattn_bq': (0.0, 0.8),
     'L1_xattn_bk': (0.0, 2.0),
     'L1_xattn_bv': (0.0, 0.1),
     'L1_xattn_bo': (0.0, 0.1),
     'L1_ffn_b1': (0.0, 0.1),
     'L1_ffn_b2': (0.0, 0.1),
     'L2_ffn_norm_weight': (1.0, 0.2),
     'L2_ffn_b1': (0.0, 0.422),
     'L2_ffn_b2': (0.0, 0.1),
     'L3_xattn_bq': (0.0, 0.358),
     'L3_xattn_bkv': (0.0, 0.1),
     'L3_xattn_bo': (0.0, 0.1)}
    factors = {'g_ffn': 27.824, 'L1_xattn_Wq': 4.759, 'L1_xattn_Wk': 4.273, 'L2_xattn_b_o': 5.821}
    for name, (base, spread) in spreads.items():
        noise = np.random.default_rng([zlib.crc32(name.encode()), seed]).standard_normal(out[name].shape)
        drawn = base * np.exp(spread * noise) if base else spread * noise
        out[name] = jnp.asarray(drawn.astype(out[name].dtype))
    for name, factor in factors.items():
        out[name] = (out[name] * factor).astype(out[name].dtype)
    return out
```

```python
from contextlib import ExitStack

import numpy as np

import concourse.bass as bass
from concourse import mybir

F32 = mybir.dt.float32
F32R = mybir.dt.float32r
BF16 = mybir.dt.bfloat16
I32 = mybir.dt.int32
U32 = mybir.dt.uint32
ALU = mybir.AluOpType
ACT = mybir.ActivationFunctionType
AX = mybir.AxisListType
ds = bass.ds

P = 128
B, S, D = 8, 256, 256
HEADS, DH = 16, 16
T = B * S
TILES = T // P
KC = D // P
GROUPS = T // 512
PAIRS = HEADS // 2
STEPS = B * PAIRS
QUADS = STEPS // 2
LAYERS = 4
EXPERTS = 8
SCALE = 1.0 / DH ** 0.5
LN_EPS = 1e-5
RMS_EPS = 1e-6
MASKED = -2.0 ** 100
MAGIC = 1.5 * 2.0 ** 23
NJ = {0: 9, 1: 8, 2: 4}
NE = {0: 1, 1: EXPERTS, 2: EXPERTS}
PREP = {0: 6, 1: 3, 2: 3}
WEIGHTS = {0: (0, 0), 1: (1, 0), 2: (1 + EXPERTS // 2, EXPERTS // 2)}
RMS = (1, 5)
LNV = [8, 17, 8, 8, 8, 18, 8, 14]
RMS_AT = 11
Q3P = 8
H3 = 1024
NJ3 = H3 // P

COLS = {}


def _columns():
    at = 0
    for name, n in [("gate", 8), ("bq1", 2), ("bk1", 2), ("bq3", 2), ("bk3", 2), ("gamma_l", 2), ("gamma_h", 2),
                    ("b1_0", 9), ("b1_1", 64), ("b1_2", 32), ("norm_w", 2), ("conv_w", 24), ("conv_b", 8),
                    ("iota", 8), ("low", 1)]:
        COLS[name] = (at, n)
        at += n
    return at


NCOL = _columns()


def build(nc, io, upto=8):
    ctx = ExitStack()
    with ctx:
        def sb(name, shape, dt=F32, stack=ctx):
            return stack.enter_context(nc.sbuf_tensor(name, shape, dt))

        def sem(name, n=None):
            if n is None:
                return ctx.enter_context(nc.semaphore(name))
            return [ctx.enter_context(nc.semaphore(f"{name}{i}")) for i in range(n)]

        x_res = sb("x_res", [P, TILES, D])
        wide = sb("wide", [P, KC * T])
        xnT = wide[:].rearrange("p (c t) -> p c t", c=KC)
        onat = wide[:].rearrange("p (t d) -> p t d", t=TILES)
        xng = sb("xng", [P, 2, 4, D])
        wslot = sb("wslot", [P, 2, 4096])
        wslots = wslot[:].rearrange("p s n -> p (s n)")
        wproj = sb("wproj", [P, 4, KC, D])
        sel = sb("sel", [P, 16, P], F32R)
        ident = sb("ident", [P, P])
        bar = sb("bar", [P, P], BF16)
        ones = sb("ones", [P, P])
        ones_r = sb("ones_r", [2, P], F32R)
        pick = sb("pick", [2, 2, P], F32R)
        cols = sb("cols", [P, NCOL])
        tg = sb("tg", [P, 8])
        st6 = sb("st6", [P, 2, 4, 6])
        mv = sb("mv", [P, 2, 4, 2])
        sml = sb("sml", [P, 2, 12, 4])
        s1 = sb("s1", [P, TILES])
        cw = sb("cw", [P, TILES, EXPERTS])
        bvb = sb("bvb", [P, D])
        bo_row = sb("bo_row", [1, D])
        wg = sb("wg", [P, KC, EXPERTS])
        gt = sb("gt", [P, 16, TILES])
        lgs = sb("lgs", [P, 2, 4, 8])
        mx8 = sb("mx8", [P, 2, 4, 8])
        ix8 = sb("ix8", [P, 2, 4, 8], U32)
        eq = sb("eq", [P, 2, TILES, 8])
        lgT = sb("lgT", [8, 512])
        b1cur = sb("b1cur", [P, 2, 8])

        def col(name, i=0, parts=P):
            return cols[0:parts, COLS[name][0] + i:COLS[name][0] + i + 1]

        at = ExitStack()
        q_hi = sb("q_hi", [P, KC, T], F32R, at)
        q_lo = sb("q_lo", [P, KC, T], F32R, at)
        k_hi = sb("k_hi", [P, KC, T], F32R, at)
        k_lo = sb("k_lo", [P, KC, T], F32R, at)
        vall = sb("vall", [P, TILES, D], F32, at)
        vbuf = sb("vbuf", [P, 2, 2, HEADS, 32], F32, at)
        qk = sb("qk", [P, 4, 512], F32R, at)
        probs = sb("probs", [P, 4, 512], F32, at)
        pvs = sb("pvs", [P, 2, 256], F32, at)
        nm = sb("nm", [P, 2, 2, 2], F32, at)
        nmT = sb("nmT", [2, 2, 256], F32R, at)
        rc = sb("rc", [P, 2, 2, 4], F32, at)
        ctxg = probs[:].rearrange("p (g c) t -> p g c t", g=2)
        oTs = probs
        at.close()
        ft = ExitStack()
        hT = sb("hT", [P, 2, 9, 512], F32, ft)
        b2f = sb("b2f", [2, EXPERTS, D], F32, ft)
        b2h = sb("b2h", [2, EXPERTS, D], F32R, ft)
        b2s = sb("b2s", [2, EXPERTS, D], F32R, ft)
        nT = sb("nT", [P, KC, T], BF16, ft)
        w1q = sb("w1q", [P, KC, H3], BF16, ft)
        w2q = sb("w2q", [P, NJ3, D], BF16, ft)
        bcast = sb("bcast", [P, 2, 512], F32, ft)
        n2 = sb("n2", [P, NJ3, 512], BF16, ft)
        q3 = sb("q3", [P, 16], F32, ft)
        q3g = sb("q3g", [P, 2, 4, 4], F32, ft)
        amx = sb("amx", [P, 512], F32, ft)
        ft.close()
        stage_i = wslots[:, 4608:4608 + 2048].bitcast(I32).rearrange("p (b m n) -> p b m n", b=2, m=2)
        mask_b = wslots[:, 6656:6656 + 1024].bitcast(BF16).rearrange("p (b m n) -> p b m n", b=2, m=2)

        PS = ctx.enter_context(nc.psum_tensor("PS", [P, 8, 512], F32))

        const_in = sem("const_in")
        x_in = sem("x_in")
        v0_in = sem("v0_in")
        consts = sem("consts")
        padded = sem("padded")
        gates = sem("gates")
        U = 2 * LAYERS
        ln_v, ln_a = sem("ln_v", U), sem("ln_a", U)
        xn_ready, xT_mm, xT_done = sem("xn_ready"), sem("xT_mm"), sem("xT_done", U)
        wproj_in, ctx_in = sem("wproj_in", LAYERS), sem("ctx_in", 2)
        k_mm, v_mm, q_mm = sem("k_mm", LAYERS), sem("v_mm", LAYERS), sem("q_mm", LAYERS)
        khi_done, klo_done = sem("khi_done"), sem("klo_done")
        qhi_done, qlo_done, v_done = sem("qhi_done"), sem("qlo_done"), sem("v_done", LAYERS)
        sel_mm, sel_done = sem("sel_mm"), sem("sel_done")
        nat_mm, max_done = sem("nat_mm"), sem("max_done")
        maxT_mm, maxT_done = sem("maxT_mm"), sem("maxT_done")
        sc_mm, exp_done = sem("sc_mm"), sem("exp_done")
        v_copied, pv_mm, pv_done = sem("v_copied"), sem("pv_mm"), sem("pv_done")
        oT_mm, rc_done, o_done = sem("oT_mm"), sem("rc_done"), sem("o_done")
        mask_in, mask_done = sem("mask_in", 2), sem("mask_done")
        o_staged, oTr_mm, oTr_done = sem("o_staged"), sem("oTr_mm"), sem("oTr_done")
        wo_mm, xo_done = sem("wo_mm"), sem("xo_done", LAYERS)
        lg_mm, lg_done = sem("lg_mm", LAYERS), sem("lg_done", LAYERS)
        lgn_mm, route_v, route_e = sem("lgn_mm", LAYERS), sem("route_v", LAYERS), sem("route_e", LAYERS)
        w_in, wg_in, b2_in, prep = sem("w_in", 2), sem("wg_in"), sem("b2_in", LAYERS), sem("prep", LAYERS)
        h_mm, h_done = sem("h_mm", LAYERS), sem("h_done", LAYERS)
        b1_done = sem("b1_done", LAYERS)
        y_mm, y_done = sem("y_mm", LAYERS), sem("y_done", LAYERS)
        w3_in = sem("w3_in")
        q3_mm, q3_v, q3_p = sem("q3_mm"), sem("q3_v"), sem("q3_p")
        mx3_mm, bc_done, tap_done, cv_v, cv_done = sem("mx3_mm"), sem("bc_done"), sem("tap_done"), sem("cv_v"), sem("cv_done")
        silu_done, n2_done = sem("silu_done"), sem("n2_done")
        out_done = sem("out_done")

        lo_l = [l for l in range(LAYERS) if 2 * l < upto]
        ffn = lambda l: 2 * l + 1 < upto

        def ln_ready(l, u):
            if u == 0:
                return x_in, 16
            if u % 2:
                return xo_done[l], (1 if l == 0 else B)
            return y_done[l - 1], 4 * GROUPS * NE[l - 1]

        block = ctx.enter_context(nc.Block())

        @block.sync
        def _(sp):
            sp.dma_start(x_res[:], io["x"].rearrange("(t p) d -> p t d", p=P)).then_inc(x_in, 16)
            for dst, name in ((xng[:].rearrange("p a b c -> p (a b c)"), "sel"), (ident[:], "ident"), (cols[:], "cols"),
                              (lgT[0:2, 0:256], "pick")):
                sp.dma_start(dst, io[name]).then_inc(const_in, 16)
            sp.dma_start(vall[:], io["ctx"].rearrange("(t p) d -> p t d", p=P)).then_inc(v0_in, 16)

            def load_feed(l):
                if l == 0:
                    sp.dma_start(wslots[:, 0:KC * NJ[0] * P].rearrange("p (c h) -> p c h", c=KC),
                                 io["W1_0"].rearrange("(c p) h -> p c h", p=P)).then_inc(w_in[0], 16)
                    sp.dma_start(wslots[:, 2304:2304 + NJ[0] * D].rearrange("p (j d) -> p j d", d=D),
                                 io["W2_0"].rearrange("(j p) d -> p j d", p=P)).then_inc(w_in[0], 16)

            def expert_slot(l, e):
                n = NJ[l] * P

                def load(slot, ex):
                    sp.dma_start(wslot[:, slot, 0:KC * n].rearrange("p (c h) -> p c h", c=KC),
                                 io[f"W1_{l}"][ds(ex * D, D), :].rearrange("(c p) h -> p c h", p=P)
                                 ).then_inc(w_in[slot], 16)
                    sp.dma_start(wslot[:, slot, KC * n:KC * n + NJ[l] * D].rearrange("p (j d) -> p j d", d=D),
                                 io[f"W2_{l}"][ds(ex * n, n), :].rearrange("(j p) d -> p j d", p=P)
                                 ).then_inc(w_in[slot], 16)
                return load

            for l in lo_l:
                if l >= 2:
                    sp.wait_ge(xo_done[l - 1], B)
                if l >= 1:
                    sp.dma_start(wproj[:], io[f"wproj_{l}"].rearrange("w (c p) n -> p w c n", p=P)
                                 ).then_inc(wproj_in[l], 16)
                    sp.dma_start(bo_row[:], io[f"bo_{l}"]).then_inc(wproj_in[l], 16)
                    if l != 2:
                        sp.dma_start(bvb[:], io[f"bv_{l}"]).then_inc(wproj_in[l], 16)
                if l == 0:
                    load_feed(0)
                if l in (1, 2):
                    sp.wait_ge(y_mm[l - 1], GROUPS * NE[l - 1])
                    if l == 1:
                        sp.wait_ge(mask_done, B)
                        sp.wait_ge(sc_mm, 2 * STEPS)
                    for e in range(2):
                        expert_slot(l, e)(e, e)
                    if l == 2:
                        sp.wait_ge(lg_mm[1], GROUPS)
                    sp.dma_start(wg[:], io[f"wg_{l}"].rearrange("(c p) e -> p c e", p=P)).then_inc(wg_in, 16)
                if l == 3:
                    sp.wait_ge(y_mm[2], GROUPS * NE[2])
                    sp.dma_start(wslot[:, 0, 0:2048].rearrange("p (c h) -> p c h", c=KC),
                                 io["W1_3"].rearrange("(c p) h -> p c h", p=P)).then_inc(w3_in, 16)
                    sp.dma_start(wslot[:, 1, 0:2048].rearrange("p (j d) -> p j d", d=D),
                                 io["W2_3"].rearrange("(j p) d -> p j d", p=P)).then_inc(w3_in, 16)
                if l >= 1:
                    sp.wait_ge(y_done[l - 1], 4 * GROUPS * NE[l - 1])
                for p in range(2):
                    sp.dma_start(ctxg[:, p], io["ctxT"][:, p * 512:(p + 1) * 512].rearrange("(c p) t -> p c t", p=P)
                                 ).then_inc(ctx_in[p], 16)
                with sp.Fori(1, GROUPS // 2) as i:
                    for p in range(2):
                        if l:
                            sp.wait_ge(v_mm[l], 2 * i + p - 1)
                        else:
                            sp.wait_ge(klo_done, 2 * i + p - 1)
                            sp.wait_ge(khi_done, 2 * i + p - 1)
                        sp.dma_start(ctxg[:, p], io["ctxT"][:, ds((2 * i + p) * 512, 512)].rearrange(
                            "(c p) t -> p c t", p=P)).then_inc(ctx_in[p], 16)
                if l == 0:
                    def load_mask(b, p):
                        for m, name in enumerate(("mask", "maskT")):
                            sp.dma_start(stage_i[:, p, m].rearrange("p (a n) -> p a n", a=2),
                                         io[name][ds(b * S, S), :].rearrange("(a p) n -> p a n", p=P)
                                         ).then_inc(mask_in[p], 16)
                    for p in range(2):
                        load_mask(p, p)
                    with sp.Fori(1, B // 2) as i:
                        for p in range(2):
                            sp.wait_ge(mask_done, 2 * i + p - 1)
                            load_mask(2 * i + p, p)
                if not ffn(l):
                    continue
                if l < 3:
                    sp.wait_ge(xo_done[l], 1 if l == 0 else B)
                    ne = 2 if l == 0 else EXPERTS
                    sp.dma_start(b2f[:, 0:ne, :], io[f"b2_{l}"]).then_inc(b2_in[l], 16)
                if l in (1, 2):
                    load = expert_slot(l, 0)
                    with sp.Fori(1, EXPERTS // 2) as i:
                        for p in range(2):
                            sp.wait_ge(y_mm[l], GROUPS * (2 * i + p - 1))
                            load(p, 2 * i + p)
            if upto == 8:
                for g in range(GROUPS):
                    sp.wait_ge(y_done[3], 4 * (g + 1))
                    sp.dma_start(io["out"].rearrange("(t p) d -> p t d", p=P)[:, 4 * g:4 * g + 4, :],
                                 x_res[:, 4 * g:4 * g + 4, :]).then_inc(out_done, 16)
                sp.wait_ge(out_done, 16 * GROUPS)
            else:
                if upto % 2:
                    sp.wait_ge(xo_done[upto // 2], 1 if upto == 1 else B)
                else:
                    sp.wait_ge(*ln_ready(upto // 2, upto))
                sp.dma_start(io["out"].rearrange("(t p) d -> p t d", p=P), x_res[:]).then_inc(out_done, 16)
                sp.wait_ge(out_done, 16)

        @block.gpsimd
        def _(pool):
            nc.gpsimd.memset(vbuf[:, :, :, :, DH:DH + 1], 1.0).then_inc(padded, 1)
            nc.gpsimd.memset(vbuf[:, :, :, :, DH + 1:32], 0.0).then_inc(padded, 1)
            for l in lo_l:
                if l:
                    pool.wait_ge(y_done[l - 1], 4 * GROUPS * NE[l - 1])
                    nc.gpsimd.memset(vbuf[:, :, :, :, DH:DH + 1], 1.0).then_inc(padded, 1)
                    nc.gpsimd.memset(vbuf[:, :, :, :, DH + 1:32], 0.0).then_inc(padded, 1)

                def copy_v(b, p):
                    nc.gpsimd.tensor_copy(
                        vbuf[:, p, :, :, 0:DH],
                        vall[:, ds(2 * b, 2), :].rearrange("p t (h d) -> p t h d", d=DH)).then_inc(v_copied, 1)

                if l:
                    pool.wait_ge(v_done[l], GROUPS)
                else:
                    pool.wait_ge(v0_in, 16)
                for p in range(2):
                    copy_v(p, p)
                with pool.Fori(1, B // 2) as i:
                    for p in range(2):
                        b = 2 * i + p
                        pool.wait_ge(pv_mm, STEPS * l + PAIRS * (b - 1))
                        copy_v(b, p)
                if l:
                    def stage_o(b, p):
                        nc.gpsimd.tensor_copy(xng[:, p, 0:2, :], onat[:, ds(2 * b, 2), :]).then_inc(o_staged, 1)
                    pool.wait_ge(o_done, QUADS * (l + 1))
                    for p in range(2):
                        stage_o(p, p)
                    with pool.Fori(1, B // 2) as i:
                        for p in range(2):
                            pool.wait_ge(oTr_mm, B * (l - 1) + 2 * i + p - 1)
                            stage_o(2 * i + p, p)
                if l in (1, 2) and ffn(l):
                    def stage_b1(e, slot):
                        nc.gpsimd.tensor_copy(b1cur[:, slot, 0:NJ[l]],
                                              cols[:, ds(COLS[f"b1_{l}"][0] + e * NJ[l], NJ[l])]).then_inc(b1_done[l], 1)
                    for e in range(2):
                        if l == 2:
                            pool.wait_ge(h_done[1], EXPERTS * GROUPS * NJ[1])
                        stage_b1(e, e)
                    with pool.Fori(1, EXPERTS // 2) as i:
                        for slot in range(2):
                            pool.wait_ge(h_done[l], NJ[l] * GROUPS * (2 * i + slot - 1))
                            stage_b1(2 * i + slot, slot)

        @block.tensor
        def _(pe):
            pe.wait_ge(const_in, 64)
            pe.wait_ge(consts, 4)

            def transposes(u, g, p):
                pe.wait_ge(xn_ready, GROUPS * u + g + 1)
                if not (isinstance(g, int) and g == 0):
                    pe.wait_ge(qlo_done if u == 0 else xT_done[u], g)
                for c in range(KC):
                    for t in range(4):
                        mm = pe.transpose(PS[:, c, t * P:(t + 1) * P], xng[:, p, t, c * P:(c + 1) * P], ident[:])
                mm.then_inc(xT_mm, 1)

            def project(l, g, p, turn=1):
                u = 2 * l
                first = isinstance(g, int) and g == 0
                if l:
                    pe.wait_ge(ctx_in[p], 16 * (2 * l + turn))
                    if first:
                        pe.wait_ge(y_done[l - 1], 4 * GROUPS * NE[l - 1])
                        pe.wait_ge(wproj_in[l], 32 if l == 2 else 48)
                    else:
                        pe.wait_ge(klo_done, GROUPS * l + g)
                    for oc in range(KC):
                        for kc in range(KC):
                            mm = pe.matmul(PS[:, 2 + oc, :], wproj[:, 1, kc, oc * P:(oc + 1) * P], ctxg[:, p, kc, :],
                                           start=(kc == 0), stop=(kc == KC - 1))
                    mm.then_inc(k_mm[l], 1)
                    if not first:
                        pe.wait_ge(v_done[l], g)
                    for t in range(4):
                        for kc in range(KC):
                            mm = pe.matmul(PS[:, 4 + t // 2, (t % 2) * D:(t % 2 + 1) * D],
                                           ctxg[:, p, kc, t * P:(t + 1) * P], wproj[:, 2, kc, :],
                                           start=(kc == 0), stop=(kc == KC - 1))
                    mm.then_inc(v_mm[l], 1)
                transposes(u, g, p)
                if l:
                    pe.wait_ge(xT_done[u], g + 1)
                    if not first:
                        pe.wait_ge(qlo_done, GROUPS * l + g)
                    for oc in range(KC):
                        for kc in range(KC):
                            mm = pe.matmul(PS[:, 6 + oc, :], wproj[:, 0, kc, oc * P:(oc + 1) * P],
                                           xnT[:, kc, ds(g * 512, 512)], start=(kc == 0), stop=(kc == KC - 1))
                    mm.then_inc(q_mm[l], 1)

            def attend(l, i):
                s0 = STEPS * l + 2 * PAIRS * i
                j0 = QUADS * l + PAIRS * i
                peeled = isinstance(i, int)
                for k in range(2 * PAIRS):
                    for stage, lag in ((select, 0), (scores_nat, 1), (max_rows, 2), (scores_key, 3), (times_v, 4),
                                       (back, 5)):
                        n = k - lag
                        if n >= 0 or not peeled:
                            stage(l, s0 + n, n % (2 * PAIRS), 2 * i + n // PAIRS, j0 + n // 2)

            def select(l, s, k, b, j):
                c = k % PAIRS
                oc, v = c // 4, c % 4
                if not (isinstance(s, int) and s == 0):
                    pe.wait_ge(sel_done, s)
                if isinstance(s, int) and s % STEPS == 0:
                    pe.wait_ge(qlo_done, GROUPS * (l + 1))
                    pe.wait_ge(klo_done, GROUPS * (l + 1))
                at = ds(b * S, S)
                pe.matmul(PS[:, 0, 0:256], sel[:, v, :], q_hi[:, oc, at], start=True, stop=False)
                pe.matmul(PS[:, 0, 0:256], sel[:, 4 + v, :], q_lo[:, oc, at], start=False, stop=True)
                pe.matmul(PS[:, 0, 256:512], sel[:, 8 + v, :], k_hi[:, oc, at], start=True, stop=False)
                pe.matmul(PS[:, 0, 256:512], sel[:, 12 + v, :], k_lo[:, oc, at], start=False, stop=True
                          ).then_inc(sel_mm, 1)

            def scores_nat(l, s, k, b, j):
                pe.wait_ge(sel_done, s + 1)
                if l == 0 and k % PAIRS == 0:
                    pe.wait_ge(mask_done, b + 1)
                for h in range(2):
                    rows = slice(64 * h, 64 * h + 3 * DH)
                    if not (isinstance(s, int) and s == 0):
                        pe.wait_ge(max_done, 2 * (s - 1) + h + 1)
                    for qt in range(2):
                        mm = pe.matmul(PS[:, 1 + h, qt * S:(qt + 1) * S], qk[rows, k % 4, qt * P:(qt + 1) * P],
                                       qk[rows, k % 4, 256:512], start=(l > 0 or qt == 0), stop=(l > 0),
                                       skip_group_check=(l == 0))
                    if l == 0:
                        mm = pe.matmul(PS[:, 1 + h, :], bar[:], mask_b[:, (k // PAIRS) % 2, 0], start=False,
                                       stop=True, skip_group_check=True)
                    mm.then_inc(nat_mm, 1)

            def max_rows(l, s, k, b, j):
                pe.wait_ge(max_done, 2 * s + 2)
                if not (isinstance(s, int) and s == 0):
                    pe.wait_ge(maxT_done, s)
                for qt in range(2):
                    mm = pe.transpose(PS[0:2, 6, qt * P:(qt + 1) * P], nm[:, k % 2, qt, :], ident[:])
                mm.then_inc(maxT_mm, 1)

            def scores_key(l, s, k, b, j):
                pe.wait_ge(maxT_done, s + 1)
                for h in range(2):
                    rows = slice(64 * h, 64 * h + 3 * DH)
                    if not (isinstance(s, int) and s == 0):
                        pe.wait_ge(exp_done, 2 * (s - 1) + h + 1)
                    for kt in range(2):
                        pe.matmul(PS[:, 3 + h, kt * S:(kt + 1) * S], qk[rows, k % 4, 256 + kt * P:256 + (kt + 1) * P],
                                  qk[rows, k % 4, 0:256], start=(kt == 0), stop=False, skip_group_check=True)
                    if l == 0:
                        pe.matmul(PS[:, 3 + h, :], bar[:], mask_b[:, (k // PAIRS) % 2, 1], start=False,
                                  stop=False, skip_group_check=True)
                    pe.matmul(PS[:, 3 + h, :], pick[:, h, :], nmT[:, k % 2, :].unsqueeze(1).broadcast_to([2, 2, 256]),
                              start=False, stop=True, skip_group_check=True).then_inc(sc_mm, 1)

            def times_v(l, s, k, b, j):
                pe.wait_ge(exp_done, 2 * s + 2)
                if k % PAIRS == 0:
                    pe.wait_ge(v_copied, B * l + b + 1)
                    if isinstance(s, int) and s % STEPS == 0:
                        pe.wait_ge(padded, 2 * (l + 1))
                if k % 2 == 0 and not (isinstance(s, int) and s < 2):
                    pe.wait_ge(pv_done, j)
                for h in range(2):
                    strip = 32 * (2 * (k % 2) + h)
                    head = 2 * (k % PAIRS) + h
                    for kt in range(2):
                        mm = pe.matmul(PS[strip:strip + 32, 5, 0:256],
                                       vbuf[:, (k // PAIRS) % 2, kt, head, :],
                                       probs[:, 2 * (k % 2) + h, kt * S:(kt + 1) * S],
                                       start=(kt == 0), stop=(kt == 1))
                mm.then_inc(pv_mm, 1)

            def back(l, s, k, b, j):
                if k % 2 == 0:
                    return
                pe.wait_ge(pv_done, j + 1)
                if not (isinstance(s, int) and s < 2):
                    pe.wait_ge(o_done, j)
                for qt in range(2):
                    mm = pe.transpose(PS[:, 7, qt * P:(qt + 1) * P], pvs[:, k // 2 % 2, qt * P:(qt + 1) * P],
                                      ident[:])
                mm.then_inc(oT_mm, 1)

            def out_project(l, b, p):
                first = isinstance(b, int)
                b0 = B * (l - 1) + b
                pe.wait_ge(o_staged, b0 + 1)
                if not first:
                    pe.wait_ge(oTr_done, b0 - 1)
                for kc in range(KC):
                    for qt in range(2):
                        mm = pe.transpose(PS[:, p, kc * 256 + qt * P:kc * 256 + (qt + 1) * P],
                                          xng[:, p, qt, kc * P:(kc + 1) * P], ident[:])
                mm.then_inc(oTr_mm, 1)
                pe.wait_ge(oTr_done, b0 + 1)
                if not first:
                    pe.wait_ge(xo_done[l], b - 1)
                for qt in range(2):
                    o = PS[:, 2 + p, qt * D:(qt + 1) * D]
                    pe.matmul(o, ones[0:1, :], bo_row[:], start=True, stop=False)
                    for kc in range(KC):
                        mm = pe.matmul(o, oTs[:, p, kc * 256 + qt * P:kc * 256 + (qt + 1) * P], wproj[:, 3, kc, :],
                                       start=False, stop=(kc == KC - 1))
                mm.then_inc(wo_mm, 1)

            def router(l, g, p):
                first = isinstance(g, int) and g == 0
                if first:
                    pe.wait_ge(wg_in, 16 * l)
                else:
                    pe.wait_ge(lg_done[l], g)
                pe.wait_ge(xT_done[2 * l + 1], g + 1)
                for kc in range(KC):
                    mm = pe.matmul(PS[0:8, 2, :], wg[:, kc, :], xnT[:, kc, ds(g * 512, 512)],
                                   start=(kc == 0), stop=(kc == KC - 1))
                mm.then_inc(lg_mm[l], 1)
                pe.wait_ge(lg_done[l], g + 1)
                if not first:
                    pe.wait_ge(route_v[l], 5 * (g - 1) + 1)
                for t in range(4):
                    mm = pe.transpose(PS[:, 3, 8 * t:8 * t + 8], lgT[:, t * P:(t + 1) * P], ident[0:8, 0:8])
                mm.then_inc(lgn_mm[l], 1)

            def hidden(l, n, e, g, slot, j, turn):
                nj = NJ[l]
                if j == 0:
                    pe.wait_ge(w_in[slot], 32 * (WEIGHTS[l][slot] + turn))
                at0 = isinstance(n, int) and n == 0
                if j >= 4:
                    pe.wait_ge(h_done[l], nj * n + j - 3)
                elif not at0:
                    last = max(x for x in range(nj) if x % 4 == j)
                    pe.wait_ge(h_done[l], nj * n - nj + last + 1)
                w1 = wslots[:, 0:KC * nj * P] if l == 0 else wslot[:, slot, 0:KC * nj * P]
                w1 = w1.rearrange("p (c h) -> p c h", c=KC)
                for kc in range(KC):
                    mm = pe.matmul(PS[:, 4 + j % 4, :], w1[:, kc, j * P:(j + 1) * P], xnT[:, kc, ds(g * 512, 512)],
                                   start=(kc == 0), stop=(kc == KC - 1))
                mm.then_inc(h_mm[l], 1)

            def outputs(l, n, e, p, slot, j):
                nj = NJ[l]
                pe.wait_ge(h_done[l], nj * n + j + 1)
                if j == 0 and not (isinstance(n, int) and n < 2):
                    pe.wait_ge(y_done[l], 4 * n - 4)
                base = KC * nj * P
                w2 = wslots[:, base:base + nj * D] if l == 0 else wslot[:, slot, base:base + nj * D]
                w2 = w2.rearrange("p (j d) -> p j d", d=D)
                for t in range(4):
                    o = PS[:, 2 * p + t // 2, (t % 2) * D:(t % 2 + 1) * D]
                    mm = pe.matmul(o, hT[:, p, j, t * P:(t + 1) * P], w2[:, j, :],
                                   start=(j == 0 and t % 2 == 0), stop=(j == nj - 1), skip_group_check=True)
                    if j == 0:
                        for r in range(2 if l == 0 else 1):
                            pe.matmul(o, ones_r[:], b2s[:, r, :] if l == 0 else b2s[:, ds(e, 1), :], start=False,
                                      stop=False, skip_group_check=True)
                if j == nj - 1:
                    mm.then_inc(y_mm[l], 1)

            def feed_pair(l, n, e, g, slot, turn=1):
                nj = NJ[l]
                todo = [(p, j) for p in range(2) for j in range(nj)]
                hidden(l, n, e, g, slot, 0, turn)
                for at, (p, j) in enumerate(todo):
                    if at + 1 < len(todo):
                        p1, j1 = todo[at + 1]
                        hidden(l, n + p1, e, g + p1, slot, j1, turn)
                    outputs(l, n + p, e, p, slot, j)

            for l in lo_l:
                u = 2 * l
                for p in range(2):
                    project(l, p, p)
                with pe.Fori(1, GROUPS // 2) as i:
                    for p in range(2):
                        project(l, 2 * i + p, p, i + 1)
                attend(l, 0)
                with pe.Fori(1, B // 2) as i:
                    attend(l, i)
                for k in range(5):
                    for stage, lag in ((scores_nat, 1), (max_rows, 2), (scores_key, 3), (times_v, 4), (back, 5)):
                        n = k - lag
                        if n < 0:
                            stage(l, STEPS * (l + 1) + n, n % (2 * PAIRS), B + n // PAIRS, QUADS * (l + 1) + n // 2)
                if l:
                    pe.wait_ge(o_done, QUADS * (l + 1))
                    for p in range(2):
                        out_project(l, p, p)
                    with pe.Fori(1, B // 2) as i:
                        for p in range(2):
                            out_project(l, 2 * i + p, p)
                if not ffn(l):
                    continue
                u += 1
                if l:
                    pe.wait_ge(xo_done[l], B)

                if l == 3:
                    pe.wait_ge(q3_v, 1)
                    pe.matmul(PS[:, 7, 0:2], ones[:], q3[:, 0:2], start=True, stop=True).then_inc(q3_mm, 1)

                def norm(g, p):
                    transposes(u, g, p)
                    if l in (1, 2):
                        router(l, g, p)
                for p in range(2):
                    norm(p, p)
                with pe.Fori(1, GROUPS // 2) as i:
                    for p in range(2):
                        norm(2 * i + p, p)
                if l < 3:
                    pe.wait_ge(xT_done[u], GROUPS)
                    pe.wait_ge(prep[l], PREP[l])
                    if l == 0:
                        feed_pair(0, 0, 0, 0, 0)
                        feed_pair(0, 2, 0, 2, 0)
                    else:
                        feed_pair(l, 0, 0, 0, 0)
                        feed_pair(l, 2, 0, 2, 0)
                        with pe.Fori(0, GROUPS // 2) as gg:
                            feed_pair(l, GROUPS + 2 * gg, 1, 2 * gg, 1)
                        with pe.Fori(1, EXPERTS // 2) as i:
                            for slot in range(2):
                                with pe.Fori(0, GROUPS // 2) as gg:
                                    feed_pair(l, (2 * i + slot) * GROUPS + 2 * gg, 2 * i + slot, 2 * gg, slot, i + 1)
                else:
                    def quantised(g, p):
                        first = isinstance(g, int) and g == 0
                        pe.wait_ge(q3_p, Q3P * g + 1)
                        for t in range(4):
                            mm = pe.transpose(PS[:, 2, t * P:(t + 1) * P],
                                              q3g[:, p, 0, t:t + 1].broadcast_to([P, P]), ident[:])
                        mm.then_inc(mx3_mm, 1)
                        for c in range(NJ3):
                            if c >= 4:
                                pe.wait_ge(h_done[3], NJ3 * g + c - 3)
                            elif not first:
                                pe.wait_ge(h_done[3], NJ3 * g + c - 3)
                            elif c == 0:
                                pe.wait_ge(xT_done[u], GROUPS)
                                pe.wait_ge(q3_v, 10)
                            for kc in range(KC):
                                mm = pe.matmul(PS[:, 4 + c % 4, :], w1q[:, kc, c * P:(c + 1) * P],
                                               nT[:, kc, ds(g * 512, 512)], start=(kc == 0), stop=(kc == KC - 1))
                            mm.then_inc(h_mm[3], 1)
                        pe.wait_ge(q3_p, Q3P * g + 2)
                        for t in range(4):
                            mm = pe.transpose(PS[:, 2, t * P:(t + 1) * P], amx[:, t * P:(t + 1) * P], ident[:])
                        mm.then_inc(mx3_mm, 1)
                        pe.wait_ge(q3_p, Q3P * g + 5)
                        for t in range(4):
                            mm = pe.transpose(PS[:, 3, t * P:(t + 1) * P],
                                              q3g[:, p, 2, t:t + 1].broadcast_to([P, P]), ident[:])
                        mm.then_inc(mx3_mm, 1)
                        pe.wait_ge(n2_done, g + 1)
                        if not first:
                            pe.wait_ge(y_done[3], 4 * g)
                        for t in range(4):
                            for c in range(NJ3):
                                mm = pe.matmul(PS[:, t // 2, (t % 2) * D:(t % 2 + 1) * D], n2[:, c, t * P:(t + 1) * P],
                                               w2q[:, c, :], start=(c == 0), stop=(c == NJ3 - 1))
                        mm.then_inc(y_mm[3], 1)
                    for p in range(2):
                        quantised(p, p)
                    with pe.Fori(1, GROUPS // 2) as i:
                        for p in range(2):
                            quantised(2 * i + p, p)

        @block.scalar
        def _(act):
            act.wait_ge(const_in, 64)
            nc.scalar.activation(tg[:], cols[:, COLS["gate"][0]:COLS["gate"][0] + 8], ACT.Tanh).then_inc(gates, 1)

            def roots(u, g, p):
                act.wait_ge(ln_v[u], LNV[u] * g + 3)
                nc.scalar.activation(sml[:, p, 1, :], sml[:, p, 0, :], ACT.Sqrt).then_inc(ln_a[u], 1)
                if u in RMS:
                    act.wait_ge(ln_v[u], LNV[u] * g + RMS_AT)
                    nc.scalar.activation(sml[:, p, 7, :], sml[:, p, 6, :], ACT.Sqrt).then_inc(ln_a[u], 1)

            def project(l, g, p, turn=1):
                u = 2 * l
                roots(u, g, p)
                at = ds(g * 512, 512)
                if l:
                    act.wait_ge(k_mm[l], g + 1)
                    for oc in range(KC):
                        ins = nc.scalar.activation(k_hi[:, oc, at], PS[:, 2 + oc, :], ACT.Identity,
                                                   bias=col(f"bk{l}", oc) if l != 2 else 0.0)
                    ins.then_inc(khi_done, 1)
                    act.wait_ge(xT_mm, GROUPS * u + g + 1)
                    for c in range(KC):
                        ins = nc.scalar.activation(xnT[:, c, at], PS[:, c, :], ACT.Identity)
                    ins.then_inc(xT_done[u], 1)
                    act.wait_ge(q_mm[l], g + 1)
                    for oc in range(KC):
                        ins = nc.scalar.activation(q_hi[:, oc, at], PS[:, 6 + oc, :], ACT.Identity,
                                                   bias=col(f"bq{l}", oc) if l != 2 else 0.0)
                    ins.then_inc(qhi_done, 1)
                else:
                    act.wait_ge(ctx_in[p], 16 * turn)
                    for c in range(KC):
                        ins = nc.scalar.activation(k_hi[:, c, at], ctxg[:, p, c, :], ACT.Identity)
                    ins.then_inc(khi_done, 1)
                    act.wait_ge(xT_mm, g + 1)
                    for c in range(KC):
                        ins = nc.scalar.activation(q_hi[:, c, at], PS[:, c, :], ACT.Identity)
                    ins.then_inc(qhi_done, 1)

            def take_stack(l, s, k):
                act.wait_ge(sel_mm, s + 1)
                if not (isinstance(s, int) and s < 4):
                    act.wait_ge(sc_mm, 2 * s - 6)
                nc.scalar.activation(qk[:, k % 4, :], PS[:, 0, :], ACT.Identity).then_inc(sel_done, 1)

            def exps(l, s, k):
                for h in range(2):
                    act.wait_ge(sc_mm, 2 * s + h + 1)
                    if h == 0 and not (isinstance(s, int) and s < 2):
                        act.wait_ge(pv_mm, s - 1)
                    nc.scalar.activation(probs[:, 2 * (k % 2) + h, :], PS[:, 3 + h, :], ACT.Exp, scale=SCALE
                                         ).then_inc(exp_done, 1)

            def attend(l, i):
                for k in range(2 * PAIRS):
                    take_stack(l, STEPS * l + 2 * PAIRS * i + k, k)
                    n = k - 3
                    if n >= 0 or not isinstance(i, int):
                        exps(l, STEPS * l + 2 * PAIRS * i + n, n % (2 * PAIRS))

            def take_oT(l, b, p):
                b0 = B * (l - 1) + b
                act.wait_ge(oTr_mm, b0 + 1)
                if not isinstance(b, int):
                    act.wait_ge(wo_mm, b0 - 1)
                nc.scalar.activation(oTs[:, p, :], PS[:, p, :], ACT.Identity).then_inc(oTr_done, 1)

            def norm(l, g, p):
                u = 2 * l + 1
                at = ds(g * 512, 512)
                act.wait_ge(xT_mm, GROUPS * u + g + 1)
                for c in range(KC):
                    ins = nc.scalar.activation(nT[:, c, at] if l == 3 else xnT[:, c, at], PS[:, c, :], ACT.Identity,
                                               scale=col("norm_w", c) if l == 2 else 1.0)
                ins.then_inc(xT_done[u], 1)
                if l in (1, 2):
                    act.wait_ge(lg_mm[l], g + 1)
                    if not (isinstance(g, int) and g == 0):
                        act.wait_ge(lgn_mm[l], g)
                    nc.scalar.activation(lgT[:], PS[0:8, 2, :], ACT.Identity).then_inc(lg_done[l], 1)

            def feed(l, n, e, p, slot=0):
                nj = NJ[l]
                for j in range(nj):
                    act.wait_ge(h_mm[l], nj * n + j + 1)
                    if j == 0:
                        if not (isinstance(n, int) and n < 2):
                            act.wait_ge(y_mm[l], n - 1)
                        if l:
                            act.wait_ge(b1_done[l], e + 1)
                    bias = col("b1_0", j) if l == 0 else b1cur[:, slot, j:j + 1]
                    nc.scalar.activation(hT[:, p, j, :], PS[:, 4 + j % 4, :], ACT.Gelu, bias=bias).then_inc(h_done[l], 1)

            for l in lo_l:
                for p in range(2):
                    project(l, p, p)
                with act.Fori(1, GROUPS // 2) as i:
                    for p in range(2):
                        project(l, 2 * i + p, p, i + 1)
                attend(l, 0)
                with act.Fori(1, B // 2) as i:
                    attend(l, i)
                for n in range(-3, 0):
                    exps(l, STEPS * (l + 1) + n, n % (2 * PAIRS))
                if l:
                    for p in range(2):
                        take_oT(l, p, p)
                    with act.Fori(1, B // 2) as i:
                        for p in range(2):
                            take_oT(l, 2 * i + p, p)
                if not ffn(l):
                    continue
                u = 2 * l + 1

                def norm_pair(g):
                    for p in range(2):
                        roots(u, g + p, p)
                    for p in range(2):
                        norm(l, g + p, p)
                norm_pair(0)
                with act.Fori(1, GROUPS // 2) as i:
                    norm_pair(2 * i)
                if l in (1, 2):
                    act.wait_ge(route_v[l], 5 * GROUPS)
                    nc.scalar.activation(gt[:, 3, :], gt[:, 2, :], ACT.Exp).then_inc(route_e[l], 1)
                if l == 0:
                    for n in range(GROUPS):
                        feed(0, n, 0, n % 2)
                elif l < 3:
                    for e in range(2):
                        for g in range(GROUPS):
                            feed(l, GROUPS * e + g, e, g % 2, e)
                    with act.Fori(1, EXPERTS // 2) as i:
                        for slot in range(2):
                            for g in range(GROUPS):
                                feed(l, GROUPS * (2 * i + slot) + g, 2 * i + slot, g % 2, slot)
                else:
                    def quantised(g, p):
                        act.wait_ge(mx3_mm, 3 * g + 1)
                        nc.scalar.activation(bcast[:, p, :], PS[:, 2, :], ACT.Identity).then_inc(bc_done, 1)
                        for c in range(NJ3 + 1):
                            if c < NJ3:
                                act.wait_ge(h_done[3], NJ3 * g + c + 1)
                                nc.scalar.activation(hT[:, 1, c, :], hT[:, 0, c, :], ACT.Identity,
                                                     scale=col("conv_w", NJ3 + c), bias=col("conv_b", c)
                                                     ).then_inc(tap_done, 1)
                            if c:
                                act.wait_ge(cv_done, NJ3 * g + c)
                                nc.scalar.activation(hT[:, 1, c - 1, :], hT[:, 1, c - 1, :], ACT.Silu
                                                     ).then_inc(silu_done, 1)
                        act.wait_ge(q3_p, Q3P * g + Q3P)
                        if not (isinstance(g, int) and g == 0):
                            act.wait_ge(y_mm[3], g)
                        nc.scalar.activation(n2[:].rearrange("p c t -> p (c t)"),
                                             hT[:, 0, 0:NJ3, :].rearrange("p c t -> p (c t)"), ACT.Identity,
                                             bias=-MAGIC).then_inc(n2_done, 1)
                    for p in range(2):
                        quantised(p, p)
                    with act.Fori(1, GROUPS // 2) as i:
                        for p in range(2):
                            quantised(2 * i + p, p)

        @block.vector
        def _(dve):
            dve.wait_ge(const_in, 64)
            nc.vector.tensor_copy(sel[:].rearrange("p a b -> p (a b)"), xng[:].rearrange("p a b c -> p (a b c)")
                                  ).then_inc(consts, 1)
            nc.vector.tensor_scalar(bar[:], ident[:], MASKED, None, ALU.mult).then_inc(consts, 1)
            nc.vector.tensor_copy(pick[:].rearrange("p a b -> p (a b)"), lgT[0:2, 0:256]).then_inc(consts, 1)
            nc.vector.memset(ones[:], 1.0)
            nc.vector.memset(ones_r[:].bitcast(F32), 1.0).then_inc(consts, 1)
            dve.wait_ge(consts, 4)
            dve.wait_ge(gates, 1)

            def rsqrt(u, g, p, k, v, root, r):
                q = lambda n: sml[:, p, n, :]

                def then(ins):
                    nonlocal k
                    k += 1
                    ins.then_inc(ln_v[u], 1)
                    dve.wait_ge(ln_v[u], LNV[u] * g + k)
                then(nc.vector.reciprocal(q(2), q(root)))
                then(nc.vector.tensor_tensor(q(3), q(2), q(2), ALU.mult))
                then(nc.vector.tensor_tensor(q(4), q(3), q(v), ALU.mult))
                then(nc.vector.tensor_scalar(q(5), q(4), -0.5, 1.5, ALU.mult, ALU.add))
                then(nc.vector.tensor_tensor(q(r), q(2), q(5), ALU.mult))
                return k

            def layernorm(l, u, g, p):
                q = lambda n: sml[:, p, n, :]
                first = isinstance(g, int) and g == 0
                k = 0

                def then(ins):
                    nonlocal k
                    k += 1
                    ins.then_inc(ln_v[u], 1)
                    dve.wait_ge(ln_v[u], LNV[u] * g + k)
                if first:
                    dve.wait_ge(*ln_ready(l, u))
                tile = lambda t: x_res[:, ds(4 * g + t, 1), :].rearrange("p a d -> p (a d)")
                for t in range(4):
                    ins = nc.vector.bn_stats(st6[:, p, t, :], tile(t))
                then(ins)
                for t in range(4):
                    ins = nc.vector.bn_aggr(mv[:, p, t, :], st6[:, p, t, :])
                then(ins)
                var = mv[:, p, :, 1]
                then(nc.vector.tensor_scalar(q(0), var, LN_EPS, None, ALU.add))
                dve.wait_ge(ln_a[u], (2 if u in RMS else 1) * g + 1)
                k = rsqrt(u, g, p, k, 0, 1, 8)
                scale = 8
                if u in RMS:
                    then(nc.vector.tensor_tensor(q(9), q(8), q(8), ALU.mult))
                    then(nc.vector.tensor_tensor(q(10), q(9), var, ALU.mult))
                    if l == 0:
                        then(nc.vector.tensor_scalar(q(6), q(10), float(D), 1e-24, ALU.mult, ALU.max))
                    else:
                        then(nc.vector.tensor_scalar(q(6), q(10), RMS_EPS, None, ALU.add))
                    dve.wait_ge(ln_a[u], 2 * g + 2)
                    k = rsqrt(u, g, p, k, 6, 7, 11)
                    if l == 0:
                        then(nc.vector.scalar_tensor_tensor(q(9), q(8), float(D) ** 0.5, q(11), ALU.mult, ALU.mult))
                        scale = 9
                if not (isinstance(g, int) and g < 2):
                    dve.wait_ge(xT_mm, GROUPS * u + g - 1)
                for t in range(4):
                    ins = nc.vector.tensor_scalar(xng[:, p, t, :], tile(t), mv[:, p, t, 0:1], sml[:, p, scale, t:t + 1],
                                                  ALU.subtract, ALU.mult)
                if u == 5:
                    then(ins)
                    then(nc.vector.scalar_tensor_tensor(
                        x_res[:, ds(4 * g, 4), :].rearrange("p t d -> p (t d)"),
                        xng[:, p].rearrange("p t d -> p (t d)"), tg[:, 4 + l:5 + l],
                        x_res[:, ds(4 * g, 4), :].rearrange("p t d -> p (t d)"), ALU.mult, ALU.add))
                    for t in range(4):
                        ins = nc.vector.tensor_scalar(xng[:, p, t, :], xng[:, p, t, :], sml[:, p, 11, t:t + 1], None,
                                                      ALU.mult)
                if u == 7:
                    then(ins)
                    then(nc.vector.tensor_reduce(q(6), xng[:, p], AX.X, ALU.max, apply_absolute_value=True))
                    then(nc.vector.tensor_scalar(q(7), q(6), 1e-5, 1.0 / 127.0, ALU.max, ALU.mult))
                    then(nc.vector.reciprocal(q(9), q(7)))
                    then(nc.vector.tensor_scalar(s1[:, ds(4 * g, 4)], q(7), q3[:, 2:3], None, ALU.mult))
                    for t in range(4):
                        ins = nc.vector.tensor_scalar(xng[:, p, t, :], xng[:, p, t, :], sml[:, p, 9, t:t + 1], MAGIC,
                                                      ALU.mult, ALU.add)
                    then(ins)
                    ins = nc.vector.tensor_scalar(xng[:, p], xng[:, p], MAGIC + 127.0, -MAGIC, ALU.min, ALU.add)
                ins.then_inc(xn_ready, 1)
                assert k == LNV[u], (u, k)

            def project(l, g, p):
                layernorm(l, 2 * l, g, p)
                at = ds(g * 512, 512)
                if l:
                    dve.wait_ge(khi_done, GROUPS * l + g + 1)
                    for oc in range(KC):
                        ins = nc.vector.scalar_tensor_tensor(
                            k_lo[:, oc, at], PS[:, 2 + oc, :], col(f"bk{l}", oc) if l != 2 else 0.0,
                            k_hi[:, oc, at].bitcast(F32), ALU.add, ALU.subtract)
                    ins.then_inc(klo_done, 1)
                    dve.wait_ge(v_mm[l], g + 1)
                    for t in range(2):
                        v = vall[:, ds(4 * g + 2 * t, 2), :]
                        ps = PS[:, 4 + t, :].rearrange("p (t d) -> p t d", d=D)
                        if l == 2:
                            ins = nc.vector.tensor_copy(v, ps)
                        else:
                            ins = nc.vector.tensor_tensor(v, ps, bvb[:].unsqueeze(1).broadcast_to([P, 2, D]), ALU.add)
                    ins.then_inc(v_done[l], 1)
                    dve.wait_ge(qhi_done, GROUPS * l + g + 1)
                    for oc in range(KC):
                        ins = nc.vector.scalar_tensor_tensor(
                            q_lo[:, oc, at], PS[:, 6 + oc, :], col(f"bq{l}", oc) if l != 2 else 0.0,
                            q_hi[:, oc, at].bitcast(F32), ALU.add, ALU.subtract)
                    ins.then_inc(qlo_done, 1)
                else:
                    dve.wait_ge(khi_done, g + 1)
                    nc.vector.tensor_tensor(k_lo[:, :, at], ctxg[:, p], k_hi[:, :, at].bitcast(F32), ALU.subtract
                                            ).then_inc(klo_done, 1)
                    dve.wait_ge(qhi_done, g + 1)
                    nc.vector.tensor_tensor(q_lo[:, :, at], PS[:, 0:2, :], q_hi[:, :, at].bitcast(F32), ALU.subtract
                                            ).then_inc(qlo_done, 1)

            def maxima(l, s, k):
                for h in range(2):
                    dve.wait_ge(nat_mm, 2 * s + h + 1)
                    if h == 0 and not (isinstance(s, int) and s < 2):
                        dve.wait_ge(maxT_mm, s - 1)
                    nc.vector.tensor_reduce(nm[:, k % 2, :, h], PS[:, 1 + h, :].rearrange("p (q n) -> p q n", q=2),
                                            AX.X, ALU.max, negate=True).then_inc(max_done, 1)

            def take_maxT(l, s, k):
                dve.wait_ge(maxT_mm, s + 1)
                if not (isinstance(s, int) and s < 2):
                    dve.wait_ge(sc_mm, 2 * s - 2)
                nc.vector.tensor_copy(nmT[:, k % 2, :], PS[0:2, 6, 0:256]).then_inc(maxT_done, 1)

            def take_pv(l, s, k, j):
                dve.wait_ge(pv_mm, s + 1)
                if not (isinstance(s, int) and s < 4):
                    dve.wait_ge(oT_mm, j - 1)
                nc.vector.tensor_copy(pvs[:, k // 2 % 2, :], PS[:, 5, 0:256]).then_inc(pv_done, 1)

            def divide(l, s, k, b, j):
                dve.wait_ge(oT_mm, j + 1)
                m = k // 2 % 2
                o = PS[:, 7, 0:256].rearrange("p (q h d) -> p q h d", q=2, h=4)
                nc.vector.reciprocal(rc[:, m], o[:, :, :, DH]).then_inc(rc_done, 1)
                dve.wait_ge(rc_done, j + 1)
                at = 64 * (k % PAIRS // 2)
                nc.vector.tensor_tensor(
                    onat[:, ds(2 * b, 2), at:at + 64].rearrange("p q (h d) -> p q h d", d=DH), o[:, :, :, 0:DH],
                    rc[:, m].unsqueeze(3).broadcast_to([P, 2, 4, DH]), ALU.mult).then_inc(o_done, 1)

            def make_mask(i, p):
                dve.wait_ge(mask_in[p], 32 * (i + 1))
                if not isinstance(i, int):
                    dve.wait_ge(sc_mm, 2 * PAIRS * (2 * i + p - 1))
                nc.vector.tensor_scalar(mask_b[:, p], stage_i[:, p], 0.0, None, ALU.is_equal).then_inc(mask_done, 1)

            def attend_turn(l, i, k, last=False):
                s0 = STEPS * (l + 1) if last else STEPS * l + 2 * PAIRS * i
                if l == 0 and not last and k in (0, 5):
                    make_mask(i, k // 5)
                for lag, stage in ((1, "max"), (2, "maxT"), (4, "pv"), (5, "divide")):
                    n = k - lag
                    if n < 0 and isinstance(i, int) and not last or last and n >= 0:
                        continue
                    m = n % (2 * PAIRS)
                    b = (B if last else 2 * i) + n // PAIRS
                    j = (QUADS * (l + 1) if last else QUADS * l + PAIRS * i) + n // 2
                    if stage == "max":
                        maxima(l, s0 + n, m)
                    elif stage == "maxT":
                        take_maxT(l, s0 + n, m)
                    elif stage == "pv" and n % 2:
                        take_pv(l, s0 + n, m, j)
                    elif stage == "divide" and n % 2:
                        divide(l, s0 + n, m, b, j)

            def add_out(l, b, p):
                dve.wait_ge(wo_mm, B * (l - 1) + b + 1)
                x = x_res[:, ds(2 * b, 2), :].rearrange("p t d -> p (t d)")
                nc.vector.scalar_tensor_tensor(x, PS[:, 2 + p, :], tg[:, l:l + 1], x, ALU.mult, ALU.add
                                               ).then_inc(xo_done[l], 1)

            def route(l, g, p):
                k = 5 * g

                def then(ins):
                    nonlocal k
                    k = k + 1
                    ins.then_inc(route_v[l], 1)
                    dve.wait_ge(route_v[l], k)
                dve.wait_ge(lgn_mm[l], g + 1)
                then(nc.vector.tensor_copy(lgs[:, p].rearrange("p t e -> p (t e)"), PS[:, 3, 0:32]))
                for t in range(4):
                    ins = nc.vector.max(mx8[:, p, t, :], lgs[:, p, t, :])
                then(ins)
                for t in range(4):
                    ins = nc.vector.max_index(ix8[:, p, t, :], mx8[:, p, t, :], lgs[:, p, t, :])
                then(ins)
                then(nc.vector.tensor_copy(gt[:, 0:2, ds(4 * g, 4)], ix8[:, p, :, 0:2].rearrange("p t k -> p k t")))
                then(nc.vector.tensor_tensor(gt[:, 2, ds(4 * g, 4)], mx8[:, p, :, 1], mx8[:, p, :, 0], ALU.subtract))

            def combine(l):
                k = 5 * GROUPS

                def then(ins):
                    nonlocal k
                    k += 1
                    ins.then_inc(route_v[l], 1)
                    dve.wait_ge(route_v[l], k)
                dve.wait_ge(route_e[l], 1)
                then(nc.vector.tensor_scalar(gt[:, 4, :], gt[:, 3, :], 1.0, None, ALU.add))
                then(nc.vector.reciprocal(gt[:, 5, :], gt[:, 4, :]))
                then(nc.vector.tensor_scalar(gt[:, 6, :], gt[:, 5, :], tg[:, 4 + l:5 + l], None, ALU.mult))
                then(nc.vector.tensor_tensor(gt[:, 7, :], gt[:, 6, :], gt[:, 3, :], ALU.mult))
                experts = cols[:, COLS["iota"][0]:COLS["iota"][0] + 8].unsqueeze(1).broadcast_to([P, TILES, 8])
                for m in range(2):
                    then(nc.vector.tensor_tensor(eq[:, m], experts, gt[:, m, :].unsqueeze(2).broadcast_to([P, TILES, 8]),
                                                 ALU.is_equal))
                    then(nc.vector.tensor_tensor(eq[:, m], eq[:, m],
                                                 gt[:, 6 + m, :].unsqueeze(2).broadcast_to([P, TILES, 8]), ALU.mult))
                nc.vector.tensor_tensor(cw[:], eq[:, 0], eq[:, 1], ALU.add).then_inc(prep[l], 1)

            def split_b2(l):
                ne = 2 if l == 0 else EXPERTS
                dve.wait_ge(b2_in[l], 16)
                nc.vector.tensor_copy(b2h[:, 0:ne], b2f[:, 0:ne]).then_inc(prep[l], 1)
                dve.wait_ge(prep[l], PREP[0] - 1 if l == 0 else 1)
                nc.vector.scalar_tensor_tensor(b2s[:, 0:ne], b2h[:, 0:ne].bitcast(F32), col("low", 0, 2), b2f[:, 0:ne],
                                               ALU.mult, ALU.add).then_inc(prep[l], 1)

            def add_feed(l, n, e, g, p):
                dve.wait_ge(y_mm[l], n + 1)
                if not (isinstance(n, int) and n < GROUPS):
                    dve.wait_ge(y_done[l], 4 * n - 12)
                for t in range(4):
                    x = x_res[:, ds(4 * g + t, 1), :].rearrange("p a d -> p (a d)")
                    w = tg[:, 4:5] if l == 0 else cw[:, ds(4 * g + t, 1), ds(e, 1)].rearrange("p a b -> p (a b)")
                    nc.vector.scalar_tensor_tensor(x, PS[:, 2 * p + t // 2, (t % 2) * D:(t % 2 + 1) * D], w, x,
                                                   ALU.mult, ALU.add).then_inc(y_done[l], 1)

            for l in lo_l:
                for p in range(2):
                    project(l, p, p)
                with dve.Fori(1, GROUPS // 2) as i:
                    for p in range(2):
                        project(l, 2 * i + p, p)
                for k in range(2 * PAIRS):
                    attend_turn(l, 0, k)
                with dve.Fori(1, B // 2) as i:
                    for k in range(2 * PAIRS):
                        attend_turn(l, i, k)
                for k in range(5):
                    attend_turn(l, B // 2, k, last=True)
                if l:
                    for p in range(2):
                        add_out(l, p, p)
                    with dve.Fori(1, B // 2) as i:
                        for p in range(2):
                            add_out(l, 2 * i + p, p)
                else:
                    dve.wait_ge(o_done, QUADS)
                    x = x_res[:].rearrange("p t d -> p (t d)")
                    nc.vector.scalar_tensor_tensor(x, wide[:], tg[:, 0:1], x, ALU.mult, ALU.add).then_inc(xo_done[0], 1)
                if not ffn(l):
                    continue
                u = 2 * l + 1
                if l == 0:
                    dve.wait_ge(w_in[0], 32)
                    w1 = wslots[:, 0:KC * NJ[0] * P].rearrange("p (c h) -> p c h", c=KC)
                    for c in range(KC):
                        nc.vector.tensor_scalar(w1[:, c, 0:P], w1[:, c, 0:P], col("gamma_l", c), None, ALU.mult
                                                ).then_inc(prep[0], 1)
                        nc.vector.tensor_scalar(w1[:, c, P:], w1[:, c, P:], col("gamma_h", c), None, ALU.mult
                                                ).then_inc(prep[0], 1)
                if l == 3:
                    k3 = 0

                    def then3(ins):
                        nonlocal k3
                        k3 += 1
                        ins.then_inc(q3_v, 1)
                        dve.wait_ge(q3_v, k3)
                    w1f, w2f = wslot[:, 0, 0:2048], wslot[:, 1, 0:2048]
                    dve.wait_ge(w3_in, 32)
                    nc.vector.tensor_reduce(q3[:, 0:1], w1f, AX.X, ALU.add, apply_absolute_value=True)
                    then3(nc.vector.tensor_reduce(q3[:, 1:2], w2f, AX.X, ALU.add, apply_absolute_value=True))
                    dve.wait_ge(q3_mm, 1)
                    then3(nc.vector.tensor_scalar(q3[:, 2:4], PS[:, 7, 0:2], 1.0 / (H3 * D), 1e-5, ALU.mult, ALU.max))
                    then3(nc.vector.reciprocal(q3[:, 4:6], q3[:, 2:4]))
                    then3(nc.vector.tensor_scalar(w1f, w1f, q3[:, 4:5], MAGIC, ALU.mult, ALU.add))
                    then3(nc.vector.tensor_scalar(w2f, w2f, q3[:, 5:6], MAGIC, ALU.mult, ALU.add))
                    then3(nc.vector.tensor_scalar(w1f, w1f, -MAGIC, 1.0, ALU.add, ALU.min))
                    then3(nc.vector.tensor_scalar(w2f, w2f, -MAGIC, 1.0, ALU.add, ALU.min))
                    then3(nc.vector.tensor_scalar(w1q[:].rearrange("p c h -> p (c h)"), w1f, -1.0, None, ALU.max))
                    then3(nc.vector.tensor_scalar(w2q[:].rearrange("p c h -> p (c h)"), w2f, -1.0, None, ALU.max))
                    then3(nc.vector.tensor_scalar(q3[:, 6:7], q3[:, 3:4], tg[:, 7:8], None, ALU.mult))

                def norm_pair(g):
                    for p in range(2):
                        layernorm(l, u, g + p, p)
                    if l in (1, 2):
                        for p in range(2):
                            route(l, g + p, p)
                norm_pair(0)
                with dve.Fori(1, GROUPS // 2) as i:
                    norm_pair(2 * i)
                if l < 3:
                    split_b2(l)
                if l in (1, 2):
                    combine(l)
                if l == 0:
                    for n in range(GROUPS):
                        add_feed(0, n, 0, n, n % 2)
                elif l < 3:
                    for n in range(GROUPS):
                        add_feed(l, n, 0, n, n % 2)
                    with dve.Fori(1, EXPERTS) as e:
                        for g in range(GROUPS):
                            add_feed(l, GROUPS * e + g, e, g, g % 2)
                else:
                    def quantised(g, p):
                        first = isinstance(g, int) and g == 0
                        k = Q3P * g
                        done = 0

                        def then(ins):
                            nonlocal done
                            done += 1
                            ins.then_inc(q3_p, 1)
                            dve.wait_ge(q3_p, k + done)
                        q = lambda n: q3g[:, p, n, :]
                        two = lambda ap: ap.rearrange("p (b t) -> p b t", b=2)
                        then(nc.vector.tensor_copy(q(0), s1[:, ds(4 * g, 4)]))
                        dve.wait_ge(bc_done, g + 1)
                        if not first:
                            dve.wait_ge(n2_done, g)
                        for c in range(NJ3 + 1):
                            if c < NJ3:
                                dve.wait_ge(h_mm[3], NJ3 * g + c + 1)
                                nc.vector.tensor_tensor(hT[:, 0, c, :], PS[:, 4 + c % 4, :], bcast[:, p, :], ALU.mult
                                                        ).then_inc(h_done[3], 1)
                            if c:
                                m = c - 1
                                dve.wait_ge(tap_done, NJ3 * g + c)
                                h, y = two(hT[:, 0, m, :]), two(hT[:, 1, m, :])
                                nc.vector.scalar_tensor_tensor(y[:, :, 1:S], h[:, :, 0:S - 1], col("conv_w", m),
                                                               y[:, :, 1:S], ALU.mult, ALU.add).then_inc(cv_v, 1)
                                dve.wait_ge(cv_v, NJ3 * g + c)
                                nc.vector.scalar_tensor_tensor(y[:, :, 0:S - 1], h[:, :, 1:S], col("conv_w", 2 * NJ3 + m),
                                                               y[:, :, 0:S - 1], ALU.mult, ALU.add).then_inc(cv_done, 1)
                        dve.wait_ge(silu_done, NJ3 * g + NJ3)
                        then(nc.vector.tensor_reduce(amx[:], hT[:, 1, 0:NJ3, :].rearrange("p c t -> p t c"), AX.X, ALU.max,
                                                     apply_absolute_value=True))
                        dve.wait_ge(mx3_mm, 3 * g + 2)
                        then(nc.vector.tensor_reduce(q(1), PS[:, 2, :].rearrange("p (t n) -> p t n", t=4), AX.X, ALU.max))
                        then(nc.vector.tensor_scalar(q(3), q(1), 1e-5, 1.0 / 127.0, ALU.max, ALU.mult))
                        then(nc.vector.reciprocal(q(2), q(3)))
                        then(nc.vector.tensor_scalar(q(1), q(3), q3[:, 6:7], None, ALU.mult))
                        dve.wait_ge(mx3_mm, 3 * g + 3)
                        h = hT[:, 0, 0:NJ3, :]
                        then(nc.vector.tensor_tensor(h, hT[:, 1, 0:NJ3, :],
                                                     PS[:, 3, :].unsqueeze(1).broadcast_to([P, NJ3, 512]), ALU.mult))
                        h = h.rearrange("p c t -> p (c t)")
                        then(nc.vector.tensor_scalar(h, h, 127.0, MAGIC, ALU.min, ALU.add))
                        assert done == Q3P
                        dve.wait_ge(y_mm[3], g + 1)
                        for t in range(4):
                            x = x_res[:, ds(4 * g + t, 1), :].rearrange("p a d -> p (a d)")
                            nc.vector.scalar_tensor_tensor(x, PS[:, t // 2, (t % 2) * D:(t % 2 + 1) * D],
                                                           q3g[:, p, 1, t:t + 1], x, ALU.mult, ALU.add
                                                           ).then_inc(y_done[3], 1)
                    for p in range(2):
                        quantised(p, p)
                    with dve.Fori(1, GROUPS // 2) as i:
                        for p in range(2):
                            quantised(2 * i + p, p)


def constants():
    sel = np.zeros((P, 4, 4, P), np.float32)
    rows = {0: (0, 2), 1: (1,), 2: (0, 1), 3: (2,)}
    for part, blocks in rows.items():
        for v in range(4):
            for h in range(2):
                for r in blocks:
                    for d in range(DH):
                        sel[32 * v + DH * h + d, part, v, 64 * h + DH * r + d] = 1.0
    pick = np.zeros((2, 2, P), np.float32)
    pick[0, 0] = pick[1, 1] = 1.0
    return {"sel": sel.reshape(P, 16 * P), "ident": np.eye(P, dtype=np.float32), "pick": pick.reshape(2, 2 * P)}


def layout(a):
    c = np.ascontiguousarray
    columns = lambda v: v.reshape(-1, P).T
    rows = lambda v, n: c(np.broadcast_to(v, (n,) + v.shape))
    table = [
        np.broadcast_to(np.concatenate([a["g_xattn"], a["g_ffn"]]), (P, 8)),
        columns(a["L1_xattn_bq"]), columns(a["L1_xattn_bk"]), columns(a["L3_xattn_bq"]),
        columns(a["L3_xattn_bkv"][:D]), columns(a["L0_ffn_light_gamma"]), columns(a["L0_ffn_heavy_gamma"]),
        columns(np.concatenate([a["L0_ffn_light_b1"], a["L0_ffn_heavy_b1"]])), columns(a["L1_ffn_b1"]),
        columns(a["L2_ffn_b1"]), columns(a["L2_ffn_norm_weight"]),
        *[columns(a["L3_ffn_conv_w"][:, 0, tap]) for tap in range(3)], columns(a["L3_ffn_conv_b"]),
        np.broadcast_to(np.arange(8, dtype=np.float32), (P, 8)),
        np.where(np.arange(P) == 1, -1.0, 0.0).astype(np.float32).reshape(P, 1),
    ]
    ctx = a["ctx_1024"].reshape(T, D)
    mask = a["mask_Bx1xSxS2_ik1"].reshape(B, S, S)
    wkv = a["L3_xattn_Wkv"]
    out = constants()
    out.update({
        "x": c(a["x"].reshape(T, D)), "ctx": c(ctx), "ctxT": c(ctx.T),
        "mask": c(mask.reshape(T, S)), "maskT": c(mask.transpose(0, 2, 1).reshape(T, S)),
        "cols": c(np.concatenate(table, axis=1)),
        "wproj_1": c(np.stack([a[f"L1_xattn_W{n}"].T for n in "qkvo"])),
        "wproj_2": c(np.stack([a[f"L2_xattn_W_{n}"] for n in "qkvo"])),
        "wproj_3": c(np.stack([a["L3_xattn_Wq"], wkv[:, :D], wkv[:, D:], a["L3_xattn_Wo"]])),
        "bo_1": c(a["L1_xattn_bo"].reshape(1, D)), "bo_2": c(a["L2_xattn_b_o"].reshape(1, D)),
        "bo_3": c(a["L3_xattn_bo"].reshape(1, D)),
        "bv_1": rows(a["L1_xattn_bv"], P), "bv_3": rows(a["L3_xattn_bkv"][D:], P),
        "W1_0": c(np.concatenate([a["L0_ffn_light_w1"], a["L0_ffn_heavy_w1"]], axis=1)),
        "W2_0": c(np.concatenate([a["L0_ffn_light_w2"], a["L0_ffn_heavy_w2"]], axis=0)),
        "b2_0": rows(np.stack([a["L0_ffn_light_b2"], a["L0_ffn_heavy_b2"]]), 2),
        "W1_1": c(a["L1_ffn_W1"].reshape(EXPERTS * D, -1)), "W2_1": c(a["L1_ffn_W2"].reshape(-1, D)),
        "wg_1": c(a["L1_ffn_Wr"]), "b2_1": rows(a["L1_ffn_b2"], 2),
        "W1_2": c(a["L2_ffn_w1"].transpose(0, 2, 1).reshape(EXPERTS * D, -1)),
        "W2_2": c(a["L2_ffn_w2"].transpose(0, 2, 1).reshape(-1, D)),
        "wg_2": c(a["L2_ffn_gate_w"].T), "b2_2": rows(a["L2_ffn_b2"], 2),
        "W1_3": c(a["L3_ffn_w1"].T), "W2_3": c(a["L3_ffn_w2"].T),
    })
    return out


def kernel(**inputs):
    import concourse.bacc as bacc
    from concourse.bass_utils import run_bass_kernel_spmd

    arrays = layout(inputs)
    nc = bacc.Bacc("TRN2", target_bir_lowering=False, num_devices=1)
    io = {name: nc.dram_tensor(name + "_dram", a.shape, mybir.dt.from_np(a.dtype), kind="ExternalInput").ap()
          for name, a in arrays.items()}
    io["out"] = nc.dram_tensor("out_dram", (T, D), F32, kind="ExternalOutput").ap()
    build(nc, io)
    got = run_bass_kernel_spmd(nc, [{name + "_dram": a for name, a in arrays.items()}], core_ids=[0])
    return got.results[0]["out_dram"].reshape(B, S, D)
```

```python
from contextlib import ExitStack

import numpy as np

import concourse.bass as bass
from concourse import mybir

F32 = mybir.dt.float32
F32R = mybir.dt.float32r
BF16 = mybir.dt.bfloat16
I32 = mybir.dt.int32
U32 = mybir.dt.uint32
ALU = mybir.AluOpType
ACT = mybir.ActivationFunctionType
AX = mybir.AxisListType
ds = bass.ds

P = 128
B, S, D = 8, 256, 256
HEADS, DH = 16, 16
T = B * S
TILES = T // P
KC = D // P
GROUPS = T // 512
PAIRS = HEADS // 2
STEPS = B * PAIRS
QUADS = STEPS // 2
LAYERS = 4
EXPERTS = 8
SCALE = 1.0 / DH ** 0.5
LN_EPS = 1e-5
RMS_EPS = 1e-6
MASKED = -2.0 ** 100
MAGIC = 1.5 * 2.0 ** 23
NJ = {0: 9, 1: 8, 2: 4}
NT = 2 * T // P + EXPERTS - 1
RING = 4096
FED = {0: T // P, 1: 2 * T // P, 2: 2 * T // P, 3: T // P}
PREP = 6
ROUTE = 5
RMS = (1, 5)
LNV = [8, 17, 8, 8, 8, 18, 8, 14]
RMS_AT = 11
Q3P = 8
H3 = 1024
NJ3 = H3 // P

COLS = {}


def _columns():
    at = 0
    for name, n in [("gate", 8), ("bq1", 2), ("bk1", 2), ("bq3", 2), ("bk3", 2), ("gamma_l", 2), ("gamma_h", 2),
                    ("b1_0", 9), ("norm_w", 2), ("conv_w", 24), ("conv_b", 8),
                    ("low", 1), ("low16", 1), ("expert16", 1)]:
        COLS[name] = (at, n)
        at += n
    return at


NCOL = _columns()


def build(nc, io, upto=8):
    ctx = ExitStack()
    with ctx:
        def sb(name, shape, dt=F32, stack=ctx):
            return stack.enter_context(nc.sbuf_tensor(name, shape, dt))

        def sem(name, n=None):
            if n is None:
                return ctx.enter_context(nc.semaphore(name))
            return [ctx.enter_context(nc.semaphore(f"{name}{i}")) for i in range(n)]

        x_res = sb("x_res", [P, TILES, D])
        wide = sb("wide", [P, KC * T])
        xnT = wide[:].rearrange("p (c t) -> p c t", c=KC)
        onat = wide[:].rearrange("p (t d) -> p t d", t=TILES)
        xng = sb("xng", [P, 2, 4, D])
        wslot = sb("wslot", [P, 2, 4096])
        wslots = wslot[:].rearrange("p s n -> p (s n)")
        wproj = sb("wproj", [P, 4, KC, D])
        sel = sb("sel", [P, 16, P], F32R)
        ident = sb("ident", [P, P])
        bar = sb("bar", [P, P], BF16)
        ones = sb("ones", [P, P])
        ones_r = sb("ones_r", [2, P], F32R)
        pick = sb("pick", [2, 2, P], F32R)
        cols = sb("cols", [P, NCOL])
        tg = sb("tg", [P, 8])
        st6 = sb("st6", [P, 2, 4, 6])
        mv = sb("mv", [P, 2, 4, 2])
        sml = sb("sml", [P, 2, 12, 4])
        s1 = sb("s1", [P, TILES])
        bvb = sb("bvb", [P, D])
        bo_row = sb("bo_row", [1, D])
        wg = sb("wg", [P, KC, EXPERTS])
        gt = sb("gt", [P, 16, TILES])
        lgs = sb("lgs", [P, 2, 4, 8])
        mx8 = sb("mx8", [P, 2, 4, 8])
        ix8 = sb("ix8", [P, 2, 4, 8], U32)
        eq = sb("eq", [P, 2, TILES, 8])
        picked = sb("picked", [P, TILES, 8])
        scan = sb("scan", [P, 2, TILES, 8])
        escan = sb("escan", [P, 4, 8])
        posf = sb("posf", [P, 2, TILES])
        pos = sb("pos", [P, 2, TILES], U32)
        tile_e = sb("tile_e", [P, 3, NT])
        table = sb("table", [1, 2, NT], I32)
        upto_e = sb("upto_e", [1, 8], I32)
        is_e = sb("is_e", [16, NT], F32R)
        iotas = sb("iotas", [P, NT + 1])
        tri = sb("tri", [P, P])
        zeros = sb("zeros", [P, D])
        yo = sb("yo", [P, 2, D])

        def col(name, i=0, parts=P):
            return cols[0:parts, COLS[name][0] + i:COLS[name][0] + i + 1]

        at = ExitStack()
        q_hi = sb("q_hi", [P, KC, T], F32R, at)
        q_lo = sb("q_lo", [P, KC, T], F32R, at)
        k_hi = sb("k_hi", [P, KC, T], F32R, at)
        k_lo = sb("k_lo", [P, KC, T], F32R, at)
        vall = sb("vall", [P, TILES, D], F32, at)
        vbuf = sb("vbuf", [P, 2, 2, HEADS * (DH + 1) + 15], F32, at)
        qk = sb("qk", [P, 4, 512], F32R, at)
        probs = sb("probs", [P, 4, 512], F32, at)
        pvs = sb("pvs", [P, 2, 256], F32, at)
        nm = sb("nm", [P, 2, 2, 2], F32, at)
        nmT = sb("nmT", [2, 2, 256], F32R, at)
        rc = sb("rc", [P, 2, 2, 4], F32, at)
        ctxg = probs[:].rearrange("p (g c) t -> p g c t", g=2)
        oTs = probs
        at.close()
        ft = ExitStack()
        hT = sb("hT", [P, 2, 9, 512], F32, ft)
        b2f = sb("b2f", [2, 2, D], F32, ft)
        b2h = sb("b2h", [2, 2, D], F32R, ft)
        b2s = sb("b2s", [2, 2, D], F32R, ft)
        nT = sb("nT", [P, KC, T], BF16, ft)
        w1q = sb("w1q", [P, KC, H3], BF16, ft)
        w2q = sb("w2q", [P, NJ3, D], BF16, ft)
        bcast = sb("bcast", [P, 2, 512], F32, ft)
        n2 = sb("n2", [P, NJ3, 512], BF16, ft)
        q3 = sb("q3", [P, 16], F32, ft)
        q3g = sb("q3g", [P, 2, 4, 4], F32, ft)
        amx = sb("amx", [P, 512], F32, ft)
        ft.close()
        fs = ExitStack()
        whi = sb("whi", [P, 2, RING], F32R, fs)
        wlo = sb("wlo", [P, 2, RING], F32R, fs)
        xn2 = sb("xn2", [P, 2, 4, D], F32, fs)
        lgT = sb("lgT", [8, 512], F32, fs)
        xg = sb("xg", [P, 2, D], F32, fs)
        xh = sb("xh", [P, 2, KC, P], F32R, fs)
        xl = sb("xl", [P, 2, KC, P], F32R, fs)
        hn = sb("hn", [P, 8 * P], F32, fs)
        hh = sb("hh", [P, 8, P], F32R, fs)
        hl = sb("hl", [P, 8, P], F32R, fs)
        b1f = sb("b1f", [16, 8 * P], F32, fs)
        b1s = sb("b1s", [16, 8 * P], F32R, fs)
        b2g = sb("b2g", [16, D], F32, fs)
        b2t = sb("b2t", [16, D], F32R, fs)
        of_e = sb("of_e", [16, 2, P], F32R, fs)
        fs.close()
        bh = hn[0:16, :].bitcast(F32R)
        yg = wslots.rearrange("p (r d) -> p r d", d=D)
        stage_i = wslots[:, 4608:4608 + 2048].bitcast(I32).rearrange("p (b m n) -> p b m n", b=2, m=2)
        mask_b = wslots[:, 6656:6656 + 1024].bitcast(BF16).rearrange("p (b m n) -> p b m n", b=2, m=2)

        xs = nc.dram_tensor("xs_sorted", (NT * P, D), F32, kind="Internal").ap()
        ys = nc.dram_tensor("ys_sorted", (NT * P, D), F32, kind="Internal").ap()

        PS = ctx.enter_context(nc.psum_tensor("PS", [P, 8, 512], F32))

        const_in = sem("const_in")
        x_in = sem("x_in")
        v0_in = sem("v0_in")
        consts = sem("consts")
        padded = sem("padded")
        gates = sem("gates")
        U = 2 * LAYERS
        ln_v, ln_a = sem("ln_v", U), sem("ln_a", U)
        xn_ready, xT_mm, xT_done = sem("xn_ready"), sem("xT_mm"), sem("xT_done")
        wproj_in, ctx_in = sem("wproj_in", LAYERS), sem("ctx_in", 2)
        k_mm, v_mm, q_mm = sem("k_mm", LAYERS), sem("v_mm", LAYERS), sem("q_mm", LAYERS)
        khi_done, klo_done = sem("khi_done"), sem("klo_done")
        qhi_done, qlo_done, v_done = sem("qhi_done"), sem("qlo_done"), sem("v_done", LAYERS)
        sel_mm, sel_done = sem("sel_mm"), sem("sel_done")
        nat_mm, max_done = sem("nat_mm"), sem("max_done")
        maxT_mm, maxT_done = sem("maxT_mm"), sem("maxT_done")
        sc_mm, exp_done = sem("sc_mm"), sem("exp_done")
        v_copied, pv_mm, pv_done = sem("v_copied"), sem("pv_mm"), sem("pv_done")
        oT_mm, rc_done, o_done = sem("oT_mm"), sem("rc_done"), sem("o_done")
        mask_in, mask_done = sem("mask_in", 2), sem("mask_done")
        o_staged, oTr_mm, oTr_done = sem("o_staged"), sem("oTr_mm"), sem("oTr_done")
        wo_mm, xo_done = sem("wo_mm"), sem("xo_done", LAYERS)
        lg_mm, lg_done = sem("lg_mm", LAYERS), sem("lg_done", LAYERS)
        lgn_mm, route_v, route_e = sem("lgn_mm", LAYERS), sem("route_v", LAYERS), sem("route_e", LAYERS)
        w0_in, w_in, wg_in, b2_in, prep = sem("w0_in"), sem("w_in", 2), sem("wg_in"), sem("b2_in"), sem("prep")
        h_mm, h_done = {0: sem("h0_mm"), 3: sem("h3_mm")}, {0: sem("h0_done"), 3: sem("h3_done")}
        y_mm, y_done = {0: sem("y0_mm"), 3: sem("y3_mm")}, sem("y_done", LAYERS)
        xs_zeroed, bias_in, pos_mm, placed, tables = sem("xs_zeroed"), sem("bias_in"), sem("pos_mm"), sem("placed"), sem("tables")
        bias_v, split_hi, split_done, scattered = sem("bias_v"), sem("split_hi"), sem("split_done"), sem("scattered")
        xg_in, xg_mm, xh_done, xl_done = sem("xg_in", 2), sem("xg_mm"), sem("xh_done"), sem("xl_done")
        e_done, hid_mm, gelu_done = sem("e_done"), sem("hid_mm"), sem("gelu_done")
        ht_mm, hh_done, hl_done = sem("ht_mm"), sem("hh_done"), sem("hl_done")
        tiles_done, yo_done, ys_out, yg_in = sem("tiles_done"), sem("yo_done"), sem("ys_out", 2), sem("yg_in", 8)
        w3_in = sem("w3_in")
        q3_mm, q3_v, q3_p = sem("q3_mm"), sem("q3_v"), sem("q3_p")
        mx3_mm, bc_done, tap_done, cv_v, cv_done = sem("mx3_mm"), sem("bc_done"), sem("tap_done"), sem("cv_v"), sem("cv_done")
        silu_done, n2_done = sem("silu_done"), sem("n2_done")
        out_done = sem("out_done")

        lo_l = [l for l in range(LAYERS) if 2 * l < upto]
        ffn = lambda l: 2 * l + 1 < upto

        def ln_ready(l, u):
            if u == 0:
                return x_in, 16
            if u % 2:
                return xo_done[l], (1 if l == 0 else B)
            return y_done[l - 1], FED[l - 1]

        def fed(l):
            return (yo_done, NT * l) if l in (1, 2) else (y_done[l], FED[l])

        def xn_slot(u, g, p):
            if u in (3, 5):
                return xng[:, g] if g < 2 else xn2[:, g - 2]
            return xng[:, p]

        block = ctx.enter_context(nc.Block())

        @block.sync
        def _(sp):
            sp.dma_start(x_res[:], io["x"].rearrange("(t p) d -> p t d", p=P)).then_inc(x_in, 16)
            for dst, name in ((xng[:].rearrange("p a b c -> p (a b c)"), "sel"), (ident[:], "ident"), (cols[:], "cols"),
                              (wproj[0:2, 0, 0, :], "pick"), (tri[:], "tri"), (iotas[:], "iotas")):
                sp.dma_start(dst, io[name]).then_inc(const_in, 16)
            sp.dma_start(vall[:], io["ctx"].rearrange("(t p) d -> p t d", p=P)).then_inc(v0_in, 16)

            for l in lo_l:
                if l >= 2:
                    sp.wait_ge(xo_done[l - 1], B)
                if l >= 1:
                    sp.dma_start(wproj[:], io[f"wproj_{l}"].rearrange("w (c p) n -> p w c n", p=P)
                                 ).then_inc(wproj_in[l], 16)
                    sp.dma_start(bo_row[:], io[f"bo_{l}"]).then_inc(wproj_in[l], 16)
                    if l != 2:
                        sp.dma_start(bvb[:], io[f"bv_{l}"]).then_inc(wproj_in[l], 16)
                if l == 0:
                    sp.dma_start(wslots[:, 0:KC * NJ[0] * P].rearrange("p (c h) -> p c h", c=KC),
                                 io["W1_0"].rearrange("(c p) h -> p c h", p=P)).then_inc(w0_in, 16)
                    sp.dma_start(wslots[:, 2304:2304 + NJ[0] * D].rearrange("p (j d) -> p j d", d=D),
                                 io["W2_0"].rearrange("(j p) d -> p j d", p=P)).then_inc(w0_in, 16)
                    sp.wait_ge(padded, 1)
                    sp.dma_start(xs.rearrange("(i p) d -> p i d", p=P), zeros[:].unsqueeze(1).broadcast_to([P, NT, D])
                                 ).then_inc(xs_zeroed, 16)
                if l in (1, 2):
                    if l == 2:
                        sp.wait_ge(lg_mm[1], GROUPS)
                    sp.dma_start(wg[:], io[f"wg_{l}"].rearrange("(c p) e -> p c e", p=P)).then_inc(wg_in, 16)
                if l == 3:
                    sp.wait_ge(y_done[2], FED[2])
                    sp.dma_start(wslot[:, 0, 0:2048].rearrange("p (c h) -> p c h", c=KC),
                                 io["W1_3"].rearrange("(c p) h -> p c h", p=P)).then_inc(w3_in, 16)
                    sp.dma_start(wslot[:, 1, 0:2048].rearrange("p (j d) -> p j d", d=D),
                                 io["W2_3"].rearrange("(j p) d -> p j d", p=P)).then_inc(w3_in, 16)
                if l >= 1:
                    sp.wait_ge(*fed(l - 1))
                for p in range(2):
                    sp.dma_start(ctxg[:, p], io["ctxT"][:, p * 512:(p + 1) * 512].rearrange("(c p) t -> p c t", p=P)
                                 ).then_inc(ctx_in[p], 16)
                with sp.Fori(1, GROUPS // 2) as i:
                    for p in range(2):
                        if l:
                            sp.wait_ge(v_mm[l], 2 * i + p - 1)
                        else:
                            sp.wait_ge(klo_done, 2 * i + p - 1)
                            sp.wait_ge(khi_done, 2 * i + p - 1)
                        sp.dma_start(ctxg[:, p], io["ctxT"][:, ds((2 * i + p) * 512, 512)].rearrange(
                            "(c p) t -> p c t", p=P)).then_inc(ctx_in[p], 16)
                if l == 0:
                    def load_mask(b, p):
                        for m, name in enumerate(("mask", "maskT")):
                            sp.dma_start(stage_i[:, p, m].rearrange("p (a n) -> p a n", a=2),
                                         io[name][ds(b * S, S), :].rearrange("(a p) n -> p a n", p=P)
                                         ).then_inc(mask_in[p], 16)
                    for p in range(2):
                        load_mask(p, p)
                    with sp.Fori(1, B // 2) as i:
                        for p in range(2):
                            sp.wait_ge(mask_done, 2 * i + p - 1)
                            load_mask(2 * i + p, p)
                if not ffn(l):
                    continue
                if l == 0:
                    sp.wait_ge(xo_done[0], 1)
                    sp.dma_start(b2f[:], io["b2_0"]).then_inc(b2_in, 16)
                if l in (1, 2):
                    sp.wait_ge(xo_done[l], B)
                    sp.dma_start(b1f[:, 0:NJ[l] * P], io[f"b1_{l}"]).then_inc(bias_in, 16)
                    sp.dma_start(b2g[:], io[f"b2_{l}"]).then_inc(bias_in, 16)

                    def load_tile(i, p):
                        if not (isinstance(i, int) and i < 2):
                            sp.wait_ge(xg_mm, NT * (l - 1) + i - 1)
                        sp.dma_start(xg[:, p], xs[ds(P * i, P), :]).then_inc(xg_in[p], 16)

                    def store_tile(i, p):
                        sp.wait_ge(yo_done, NT * (l - 1) + i + 1)
                        sp.dma_start(ys[ds(P * i, P), :], yo[:, p]).then_inc(ys_out[p], 16)
                    sp.wait_ge(scattered, 16 * FED[l] * l)
                    for i in range(3):
                        load_tile(i, i % 2)
                    with sp.Fori(0, (NT - 3) // 2) as k:
                        for q in range(2):
                            load_tile(2 * k + q + 3, (q + 1) % 2)
                            store_tile(2 * k + q, q)
                    for i in range(NT - 3, NT):
                        store_tile(i, i % 2)
            if upto == 8:
                for g in range(GROUPS):
                    sp.wait_ge(y_done[3], 4 * (g + 1))
                    sp.dma_start(io["out"].rearrange("(t p) d -> p t d", p=P)[:, 4 * g:4 * g + 4, :],
                                 x_res[:, 4 * g:4 * g + 4, :]).then_inc(out_done, 16)
                sp.wait_ge(out_done, 16 * GROUPS)
            else:
                if upto % 2:
                    sp.wait_ge(xo_done[upto // 2], 1 if upto == 1 else B)
                else:
                    sp.wait_ge(*ln_ready(upto // 2, upto))
                sp.dma_start(io["out"].rearrange("(t p) d -> p t d", p=P), x_res[:]).then_inc(out_done, 16)
                sp.wait_ge(out_done, 16)

        @block.gpsimd
        def _(pool):
            nc.gpsimd.memset(zeros[:], 0.0).then_inc(padded, 1)

            def heads(ap):
                return ap[..., 0:HEADS * (DH + 1)].rearrange("p t (h d) -> p t h d", d=DH + 1)

            def pad_v():
                for p in range(2):
                    nc.gpsimd.memset(heads(vbuf[:, p])[:, :, :, DH:DH + 1], 1.0).then_inc(padded, 1)
                nc.gpsimd.memset(vbuf[:, :, :, HEADS * (DH + 1):], 0.0).then_inc(padded, 1)
            pad_v()

            def load_expert(l, e):
                slot, h = e % 2, NJ[l] * P
                nc.gpsimd.dma_start(wslot[:, slot, 0:KC * h].rearrange("p (c h) -> p c h", c=KC),
                                    io[f"W1_{l}"][e * D:(e + 1) * D, :].rearrange("(c p) h -> p c h", p=P)
                                    ).then_inc(w_in[slot], 16)
                nc.gpsimd.dma_start(wslot[:, slot, KC * h:2 * KC * h].rearrange("p (j d) -> p j d", d=D),
                                    io[f"W2_{l}"][e * h:(e + 1) * h, :].rearrange("(j p) d -> p j d", p=P)
                                    ).then_inc(w_in[slot], 16)
            for l in lo_l:
                if l:
                    pool.wait_ge(*fed(l - 1))
                    pad_v()
                if l in (1, 2) and ffn(l):
                    if l == 1:
                        pool.wait_ge(y_mm[0], GROUPS)
                        pool.wait_ge(sc_mm, 2 * STEPS)
                    else:
                        pool.wait_ge(y_done[1], FED[1])
                    for e in range(2):
                        load_expert(l, e)

                def copy_v(b, p):
                    nc.gpsimd.tensor_copy(
                        heads(vbuf[:, p])[:, :, :, 0:DH],
                        vall[:, ds(2 * b, 2), :].rearrange("p t (h d) -> p t h d", d=DH)).then_inc(v_copied, 1)

                if l:
                    pool.wait_ge(v_done[l], GROUPS)
                else:
                    pool.wait_ge(v0_in, 16)
                for p in range(2):
                    copy_v(p, p)
                with pool.Fori(1, B // 2) as i:
                    for p in range(2):
                        b = 2 * i + p
                        pool.wait_ge(pv_mm, STEPS * l + PAIRS * (b - 1))
                        copy_v(b, p)
                if l:
                    def stage_o(b, p):
                        nc.gpsimd.tensor_copy(xng[:, p, 0:2, :], onat[:, ds(2 * b, 2), :]).then_inc(o_staged, 1)
                    pool.wait_ge(o_done, QUADS * (l + 1))
                    for p in range(2):
                        stage_o(p, p)
                    with pool.Fori(1, B // 2) as i:
                        for p in range(2):
                            pool.wait_ge(oTr_mm, B * (l - 1) + 2 * i + p - 1)
                            stage_o(2 * i + p, p)
                if l in (1, 2) and ffn(l):
                    n = 2 * KC * NJ[l] * P

                    def split(e):
                        slot = e % 2
                        w, wh, wl = wslot[:, slot, 0:n], whi[:, slot, 0:n], wlo[:, slot, 0:n]
                        if e >= 2:
                            pool.wait_ge(tiles_done, pool.value_load(upto_e[0:1, e - 2:e - 1], min_val=1, max_val=2 * NT + 2))
                        pool.wait_ge(w_in[slot], 32 * (EXPERTS // 2 * (l - 1) + e // 2 + 1))
                        nc.gpsimd.tensor_tensor(wh, w, zeros[:, 0:1].broadcast_to([P, n]), ALU.add).then_inc(split_hi, 1)
                        pool.wait_ge(split_hi, EXPERTS * (l - 1) + e + 1)
                        nc.gpsimd.tensor_tensor(wl, w, wh.bitcast(F32), ALU.subtract).then_inc(split_done, 1)
                        if e + 2 < EXPERTS:
                            pool.wait_ge(split_done, EXPERTS * (l - 1) + e + 1)
                            load_expert(l, e + 2)
                    pool.wait_ge(xo_done[l], B)
                    for e in range(2):
                        split(e)
                    pool.wait_ge(placed, l)
                    if l == 1:
                        pool.wait_ge(xs_zeroed, 16)
                    else:
                        pool.wait_ge(xg_in[0], 16 * ((NT + 1) // 2))
                        pool.wait_ge(xg_in[1], 16 * (NT // 2))
                    for t in range(TILES):
                        for m in range(2):
                            nc.gpsimd.indirect_dma_start(xs, bass.IndirectOffsetOnAxis(pos[:, m, t:t + 1], 0),
                                                         xn_slot(2 * l + 1, t // 4, 0)[:, t % 4, :], None
                                                         ).then_inc(scattered, 16)
                    pool.wait_ge(tables, l)
                    for e in range(2, EXPERTS):
                        split(e)
                    pool.wait_ge(split_done, EXPERTS * l)
                    pool.wait_ge(ys_out[0], 16 * ((NT + 1) // 2) * l)
                    pool.wait_ge(ys_out[1], 16 * (NT // 2) * l)
                    for k in range(FED[l]):
                        if k >= 8:
                            pool.wait_ge(y_done[l], k - 7)
                        nc.gpsimd.indirect_dma_start(yg[:, k, :], None, ys,
                                                     bass.IndirectOffsetOnAxis(pos[:, k % 2, k // 2:k // 2 + 1], 0)
                                                     ).then_inc(yg_in[k % 8], 16)

        @block.tensor
        def _(pe):
            pe.wait_ge(const_in, 96)
            pe.wait_ge(consts, 4)

            def transposes(u, g, p):
                pe.wait_ge(xn_ready, GROUPS * u + g + 1)
                if not (isinstance(g, int) and g == 0):
                    pe.wait_ge(*((qlo_done, g) if u == 0 else (xT_done, GROUPS * (u - 1) + g)))
                for c in range(KC):
                    for t in range(4):
                        mm = pe.transpose(PS[:, c, t * P:(t + 1) * P], xn_slot(u, g, p)[:, t, c * P:(c + 1) * P], ident[:])
                mm.then_inc(xT_mm, 1)

            def project(l, g, p, turn=1):
                u = 2 * l
                first = isinstance(g, int) and g == 0
                if l:
                    pe.wait_ge(ctx_in[p], 16 * (2 * l + turn))
                    if first:
                        pe.wait_ge(*fed(l - 1))
                        pe.wait_ge(wproj_in[l], 32 if l == 2 else 48)
                    else:
                        pe.wait_ge(klo_done, GROUPS * l + g)
                    for oc in range(KC):
                        for kc in range(KC):
                            mm = pe.matmul(PS[:, 2 + oc, :], wproj[:, 1, kc, oc * P:(oc + 1) * P], ctxg[:, p, kc, :],
                                           start=(kc == 0), stop=(kc == KC - 1))
                    mm.then_inc(k_mm[l], 1)
                    if not first:
                        pe.wait_ge(v_done[l], g)
                    for t in range(4):
                        for kc in range(KC):
                            mm = pe.matmul(PS[:, 4 + t // 2, (t % 2) * D:(t % 2 + 1) * D],
                                           ctxg[:, p, kc, t * P:(t + 1) * P], wproj[:, 2, kc, :],
                                           start=(kc == 0), stop=(kc == KC - 1))
                    mm.then_inc(v_mm[l], 1)
                transposes(u, g, p)
                if l:
                    pe.wait_ge(xT_done, GROUPS * (u - 1) + g + 1)
                    if not first:
                        pe.wait_ge(qlo_done, GROUPS * l + g)
                    for oc in range(KC):
                        for kc in range(KC):
                            mm = pe.matmul(PS[:, 6 + oc, :], wproj[:, 0, kc, oc * P:(oc + 1) * P],
                                           xnT[:, kc, ds(g * 512, 512)], start=(kc == 0), stop=(kc == KC - 1))
                    mm.then_inc(q_mm[l], 1)

            def attend(l, i):
                s0 = STEPS * l + 2 * PAIRS * i
                j0 = QUADS * l + PAIRS * i
                peeled = isinstance(i, int)
                for k in range(2 * PAIRS):
                    for stage, lag in ((select, 0), (scores_nat, 1), (max_rows, 2), (scores_key, 3), (times_v, 4),
                                       (back, 5)):
                        n = k - lag
                        if n >= 0 or not peeled:
                            stage(l, s0 + n, n % (2 * PAIRS), 2 * i + n // PAIRS, j0 + n // 2)

            def select(l, s, k, b, j):
                c = k % PAIRS
                oc, v = c // 4, c % 4
                if not (isinstance(s, int) and s == 0):
                    pe.wait_ge(sel_done, s)
                if isinstance(s, int) and s % STEPS == 0:
                    pe.wait_ge(qlo_done, GROUPS * (l + 1))
                    pe.wait_ge(klo_done, GROUPS * (l + 1))
                at = ds(b * S, S)
                pe.matmul(PS[:, 0, 0:256], sel[:, v, :], q_hi[:, oc, at], start=True, stop=False)
                pe.matmul(PS[:, 0, 0:256], sel[:, 4 + v, :], q_lo[:, oc, at], start=False, stop=True)
                pe.matmul(PS[:, 0, 256:512], sel[:, 8 + v, :], k_hi[:, oc, at], start=True, stop=False)
                pe.matmul(PS[:, 0, 256:512], sel[:, 12 + v, :], k_lo[:, oc, at], start=False, stop=True
                          ).then_inc(sel_mm, 1)

            def scores_nat(l, s, k, b, j):
                pe.wait_ge(sel_done, s + 1)
                if l == 0 and k % PAIRS == 0:
                    pe.wait_ge(mask_done, b + 1)
                for h in range(2):
                    rows = slice(64 * h, 64 * h + 3 * DH)
                    if not (isinstance(s, int) and s == 0):
                        pe.wait_ge(max_done, 2 * (s - 1) + h + 1)
                    for qt in range(2):
                        mm = pe.matmul(PS[:, 1 + h, qt * S:(qt + 1) * S], qk[rows, k % 4, qt * P:(qt + 1) * P],
                                       qk[rows, k % 4, 256:512], start=(l > 0 or qt == 0), stop=(l > 0),
                                       skip_group_check=(l == 0))
                    if l == 0:
                        mm = pe.matmul(PS[:, 1 + h, :], bar[:], mask_b[:, (k // PAIRS) % 2, 0], start=False,
                                       stop=True, skip_group_check=True)
                    mm.then_inc(nat_mm, 1)

            def max_rows(l, s, k, b, j):
                pe.wait_ge(max_done, 2 * s + 2)
                if not (isinstance(s, int) and s == 0):
                    pe.wait_ge(maxT_done, s)
                for qt in range(2):
                    mm = pe.transpose(PS[0:2, 6, qt * P:(qt + 1) * P], nm[:, k % 2, qt, :], ident[:])
                mm.then_inc(maxT_mm, 1)

            def scores_key(l, s, k, b, j):
                pe.wait_ge(maxT_done, s + 1)
                for h in range(2):
                    rows = slice(64 * h, 64 * h + 3 * DH)
                    if not (isinstance(s, int) and s == 0):
                        pe.wait_ge(exp_done, 2 * (s - 1) + h + 1)
                    for kt in range(2):
                        pe.matmul(PS[:, 3 + h, kt * S:(kt + 1) * S], qk[rows, k % 4, 256 + kt * P:256 + (kt + 1) * P],
                                  qk[rows, k % 4, 0:256], start=(kt == 0), stop=False, skip_group_check=True)
                    if l == 0:
                        pe.matmul(PS[:, 3 + h, :], bar[:], mask_b[:, (k // PAIRS) % 2, 1], start=False,
                                  stop=False, skip_group_check=True)
                    pe.matmul(PS[:, 3 + h, :], pick[:, h, :], nmT[:, k % 2, :].unsqueeze(1).broadcast_to([2, 2, 256]),
                              start=False, stop=True, skip_group_check=True).then_inc(sc_mm, 1)

            def times_v(l, s, k, b, j):
                pe.wait_ge(exp_done, 2 * s + 2)
                if k % PAIRS == 0:
                    pe.wait_ge(v_copied, B * l + b + 1)
                    if isinstance(s, int) and s % STEPS == 0:
                        pe.wait_ge(padded, 3 * (l + 1) + 1)
                if k % 2 == 0 and not (isinstance(s, int) and s < 2):
                    pe.wait_ge(pv_done, j)
                for h in range(2):
                    strip = 32 * (2 * (k % 2) + h)
                    head = 2 * (k % PAIRS) + h
                    for kt in range(2):
                        mm = pe.matmul(PS[strip:strip + 32, 5, 0:256],
                                       vbuf[:, (k // PAIRS) % 2, kt, (DH + 1) * head:(DH + 1) * head + 32],
                                       probs[:, 2 * (k % 2) + h, kt * S:(kt + 1) * S],
                                       start=(kt == 0), stop=(kt == 1))
                mm.then_inc(pv_mm, 1)

            def back(l, s, k, b, j):
                if k % 2 == 0:
                    return
                pe.wait_ge(pv_done, j + 1)
                if not (isinstance(s, int) and s < 2):
                    pe.wait_ge(o_done, j)
                for qt in range(2):
                    mm = pe.transpose(PS[:, 7, qt * P:(qt + 1) * P], pvs[:, k // 2 % 2, qt * P:(qt + 1) * P],
                                      ident[:])
                mm.then_inc(oT_mm, 1)

            def out_project(l, b, p):
                first = isinstance(b, int)
                b0 = B * (l - 1) + b
                pe.wait_ge(o_staged, b0 + 1)
                if not first:
                    pe.wait_ge(oTr_done, b0 - 1)
                for kc in range(KC):
                    for qt in range(2):
                        mm = pe.transpose(PS[:, p, kc * 256 + qt * P:kc * 256 + (qt + 1) * P],
                                          xng[:, p, qt, kc * P:(kc + 1) * P], ident[:])
                mm.then_inc(oTr_mm, 1)
                pe.wait_ge(oTr_done, b0 + 1)
                if not first:
                    pe.wait_ge(xo_done[l], b - 1)
                for qt in range(2):
                    o = PS[:, 2 + p, qt * D:(qt + 1) * D]
                    pe.matmul(o, ones[0:1, :], bo_row[:], start=True, stop=False)
                    for kc in range(KC):
                        mm = pe.matmul(o, oTs[:, p, kc * 256 + qt * P:kc * 256 + (qt + 1) * P], wproj[:, 3, kc, :],
                                       start=False, stop=(kc == KC - 1))
                mm.then_inc(wo_mm, 1)

            def router(l, g, p):
                first = isinstance(g, int) and g == 0
                if first:
                    pe.wait_ge(wg_in, 16 * l)
                else:
                    pe.wait_ge(lg_done[l], g)
                pe.wait_ge(xT_done, GROUPS * 2 * l + g + 1)
                for kc in range(KC):
                    mm = pe.matmul(PS[0:8, 2, :], wg[:, kc, :], xnT[:, kc, ds(g * 512, 512)],
                                   start=(kc == 0), stop=(kc == KC - 1))
                mm.then_inc(lg_mm[l], 1)
                pe.wait_ge(lg_done[l], g + 1)
                if not first:
                    pe.wait_ge(route_v[l], ROUTE * (g - 1) + 1)
                for t in range(4):
                    mm = pe.transpose(PS[:, 3, 8 * t:8 * t + 8], lgT[:, t * P:(t + 1) * P], ident[0:8, 0:8])
                mm.then_inc(lgn_mm[l], 1)

            def hidden(n, j):
                nj = NJ[0]
                if j >= 4:
                    pe.wait_ge(h_done[0], nj * n + j - 3)
                elif n:
                    last = max(x for x in range(nj) if x % 4 == j)
                    pe.wait_ge(h_done[0], nj * n - nj + last + 1)
                w1 = wslots[:, 0:KC * nj * P].rearrange("p (c h) -> p c h", c=KC)
                for kc in range(KC):
                    mm = pe.matmul(PS[:, 4 + j % 4, :], w1[:, kc, j * P:(j + 1) * P], xnT[:, kc, ds(n * 512, 512)],
                                   start=(kc == 0), stop=(kc == KC - 1))
                mm.then_inc(h_mm[0], 1)

            def outputs(n, j):
                nj, p = NJ[0], n % 2
                pe.wait_ge(h_done[0], nj * n + j + 1)
                if j == 0 and n >= 2:
                    pe.wait_ge(y_done[0], 4 * n - 4)
                w2 = wslots[:, KC * nj * P:KC * nj * P + nj * D].rearrange("p (j d) -> p j d", d=D)
                for t in range(4):
                    o = PS[:, 2 * p + t // 2, (t % 2) * D:(t % 2 + 1) * D]
                    mm = pe.matmul(o, hT[:, p, j, t * P:(t + 1) * P], w2[:, j, :],
                                   start=(j == 0 and t % 2 == 0), stop=(j == nj - 1), skip_group_check=True)
                    if j == 0:
                        for r in range(2):
                            pe.matmul(o, ones_r[:], b2s[:, r, :], start=False, stop=False, skip_group_check=True)
                if j == nj - 1:
                    mm.then_inc(y_mm[0], 1)

            def feed():
                todo = [(n, j) for n in range(GROUPS) for j in range(NJ[0])]
                hidden(0, 0)
                for at, (n, j) in enumerate(todo):
                    if at + 1 < len(todo):
                        hidden(*todo[at + 1])
                    outputs(n, j)

            def sparse(l):
                nj = NJ[l]
                nh = nj // 4
                n0, h0 = NT * (l - 1), NT * (NJ[1] // 4) * (l - 1)
                hi, lo = whi[:].rearrange("p s n -> p (s n)"), wlo[:].rearrange("p s n -> p (s n)")

                def ring(i):
                    return pe.value_load(table[0:1, 1, ds(i, 1)], min_val=0, max_val=RING)

                def a(i, p, turn):
                    pe.wait_ge(xg_in[p], 16 * (((NT + 1) // 2 if p == 0 else NT // 2) * (l - 1) + turn))
                    if not (isinstance(i, int) and n0 + i == 0):
                        pe.wait_ge(xl_done, n0 + i)
                    for c in range(KC):
                        mm = pe.transpose(PS[:, 0, c * P:(c + 1) * P], xg[:, p, c * P:(c + 1) * P], ident[:])
                    mm.then_inc(xg_mm, 1)

                def b(i, p):
                    off = ring(i)
                    pe.wait_ge(split_done, pe.value_load(table[0:1, 0, ds(i, 1)], min_val=1, max_val=2 * EXPERTS))
                    pe.wait_ge(xl_done, n0 + i + 1)
                    pe.wait_ge(e_done, n0 + i + 1)
                    for h in range(nh):
                        if not (isinstance(i, int) and n0 + i == 0):
                            pe.wait_ge(gelu_done, h0 + nh * i - nh + h + 1 if not (isinstance(i, int) and i == 0) else h0)
                        pe.matmul(PS[:, 1 + h, :], of_e[:, p, :], b1s[:, h * 512:(h + 1) * 512], start=True, stop=False)
                        for c in range(KC):
                            w = ds(off + (c * nj * P + h * 512), 512)
                            pe.matmul(PS[:, 1 + h, :], xh[:, p, c, :], hi[:, w], start=False, stop=False)
                            pe.matmul(PS[:, 1 + h, :], xl[:, p, c, :], hi[:, w], start=False, stop=False)
                            mm = pe.matmul(PS[:, 1 + h, :], xh[:, p, c, :], lo[:, w], start=False, stop=(c == KC - 1))
                        mm.then_inc(hid_mm, 1)

                def d(i):
                    for h in range(nh):
                        pe.wait_ge(gelu_done, h0 + nh * i + h + 1)
                        if not (isinstance(i, int) and n0 + i == 0):
                            pe.wait_ge(hl_done, h0 + nh * i - nh + h + 1 if not (isinstance(i, int) and i == 0) else h0)
                        for t in range(4):
                            mm = pe.transpose(PS[:, 3 + h, t * P:(t + 1) * P], hn[:, (4 * h + t) * P:(4 * h + t + 1) * P],
                                              ident[:])
                        mm.then_inc(ht_mm, 1)

                def e(i, p):
                    off = ring(i)
                    pe.wait_ge(hl_done, h0 + nh * i + nh)
                    if not (isinstance(i, int) and n0 + i == 0):
                        pe.wait_ge(yo_done, n0 + i)
                    o = PS[:, 5, 0:D]
                    pe.matmul(o, of_e[:, p, :], b2t[:], start=True, stop=False)
                    for j in range(nj):
                        w = ds(off + (KC * nj * P + j * D), D)
                        pe.matmul(o, hh[:, j, :], hi[:, w], start=False, stop=False)
                        pe.matmul(o, hl[:, j, :], hi[:, w], start=False, stop=False)
                        mm = pe.matmul(o, hh[:, j, :], lo[:, w], start=False, stop=(j == nj - 1))
                    mm.then_inc(tiles_done, 1)

                pe.wait_ge(route_v[l], ROUTE * GROUPS + 7)
                every = picked[:].rearrange("p t e -> p (t e)")
                pe.matmul(PS[:, 7, P:2 * P], ones[:], every, start=True, stop=True).then_inc(tiles_done, 1)
                pe.matmul(PS[:, 7, 0:P], tri[:], every, start=True, stop=True).then_inc(pos_mm, 1)
                pe.wait_ge(tables, l)
                pe.wait_ge(bias_v, 4 * l)
                a(0, 0, 1)
                b(0, 0)
                a(1, 1, 1)

                def turn(i):
                    d(i - 1)
                    if i < NT:
                        b(i, i % 2)
                    if i + 1 < NT:
                        a(i + 1, (i + 1) % 2, (i + 1) // 2 + 1)
                    e(i - 1, (i - 1) % 2)
                turn(1)
                turn(2)
                with pe.Fori(0, (NT - 5) // 2) as k:
                    for q in range(2):
                        i = 2 * k + q + 3
                        d(i - 1)
                        b(i, (q + 1) % 2)
                        a(i + 1, q, k + 3)
                        e(i - 1, q)
                for i in range(NT - 2, NT + 1):
                    turn(i)

            for l in lo_l:
                u = 2 * l
                for p in range(2):
                    project(l, p, p)
                with pe.Fori(1, GROUPS // 2) as i:
                    for p in range(2):
                        project(l, 2 * i + p, p, i + 1)
                attend(l, 0)
                with pe.Fori(1, B // 2) as i:
                    attend(l, i)
                for k in range(5):
                    for stage, lag in ((scores_nat, 1), (max_rows, 2), (scores_key, 3), (times_v, 4), (back, 5)):
                        n = k - lag
                        if n < 0:
                            stage(l, STEPS * (l + 1) + n, n % (2 * PAIRS), B + n // PAIRS, QUADS * (l + 1) + n // 2)
                if l:
                    pe.wait_ge(o_done, QUADS * (l + 1))
                    for p in range(2):
                        out_project(l, p, p)
                    with pe.Fori(1, B // 2) as i:
                        for p in range(2):
                            out_project(l, 2 * i + p, p)
                if not ffn(l):
                    continue
                u += 1
                if l:
                    pe.wait_ge(xo_done[l], B)

                if l == 3:
                    pe.wait_ge(q3_v, 1)
                    pe.matmul(PS[:, 7, 0:2], ones[:], q3[:, 0:2], start=True, stop=True).then_inc(q3_mm, 1)

                def norm(g, p):
                    transposes(u, g, p)
                    if l in (1, 2):
                        router(l, g, p)
                for g in range(GROUPS):
                    norm(g, g % 2)
                if l == 0:
                    pe.wait_ge(xT_done, GROUPS)
                    pe.wait_ge(prep, PREP)
                    feed()
                elif l < 3:
                    sparse(l)
                else:
                    def quantised(g, p):
                        first = isinstance(g, int) and g == 0
                        pe.wait_ge(q3_p, Q3P * g + 1)
                        for t in range(4):
                            mm = pe.transpose(PS[:, 2, t * P:(t + 1) * P],
                                              q3g[:, p, 0, t:t + 1].broadcast_to([P, P]), ident[:])
                        mm.then_inc(mx3_mm, 1)
                        for c in range(NJ3):
                            if c >= 4:
                                pe.wait_ge(h_done[3], NJ3 * g + c - 3)
                            elif not first:
                                pe.wait_ge(h_done[3], NJ3 * g + c - 3)
                            elif c == 0:
                                pe.wait_ge(xT_done, GROUPS * (u - 1) + GROUPS)
                                pe.wait_ge(q3_v, 10)
                            for kc in range(KC):
                                mm = pe.matmul(PS[:, 4 + c % 4, :], w1q[:, kc, c * P:(c + 1) * P],
                                               nT[:, kc, ds(g * 512, 512)], start=(kc == 0), stop=(kc == KC - 1))
                            mm.then_inc(h_mm[3], 1)
                        pe.wait_ge(q3_p, Q3P * g + 2)
                        for t in range(4):
                            mm = pe.transpose(PS[:, 2, t * P:(t + 1) * P], amx[:, t * P:(t + 1) * P], ident[:])
                        mm.then_inc(mx3_mm, 1)
                        pe.wait_ge(q3_p, Q3P * g + 5)
                        for t in range(4):
                            mm = pe.transpose(PS[:, 3, t * P:(t + 1) * P],
                                              q3g[:, p, 2, t:t + 1].broadcast_to([P, P]), ident[:])
                        mm.then_inc(mx3_mm, 1)
                        pe.wait_ge(n2_done, g + 1)
                        if not first:
                            pe.wait_ge(y_done[3], 4 * g)
                        for t in range(4):
                            for c in range(NJ3):
                                mm = pe.matmul(PS[:, t // 2, (t % 2) * D:(t % 2 + 1) * D], n2[:, c, t * P:(t + 1) * P],
                                               w2q[:, c, :], start=(c == 0), stop=(c == NJ3 - 1))
                        mm.then_inc(y_mm[3], 1)
                    for p in range(2):
                        quantised(p, p)
                    with pe.Fori(1, GROUPS // 2) as i:
                        for p in range(2):
                            quantised(2 * i + p, p)

        @block.scalar
        def _(act):
            act.wait_ge(const_in, 96)
            nc.scalar.activation(tg[:], cols[:, COLS["gate"][0]:COLS["gate"][0] + 8], ACT.Tanh).then_inc(gates, 1)

            def roots(u, g, p):
                act.wait_ge(ln_v[u], LNV[u] * g + 3)
                nc.scalar.activation(sml[:, p, 1, :], sml[:, p, 0, :], ACT.Sqrt).then_inc(ln_a[u], 1)
                if u in RMS:
                    act.wait_ge(ln_v[u], LNV[u] * g + RMS_AT)
                    nc.scalar.activation(sml[:, p, 7, :], sml[:, p, 6, :], ACT.Sqrt).then_inc(ln_a[u], 1)

            def project(l, g, p, turn=1):
                u = 2 * l
                roots(u, g, p)
                at = ds(g * 512, 512)
                if l:
                    act.wait_ge(k_mm[l], g + 1)
                    for oc in range(KC):
                        ins = nc.scalar.activation(k_hi[:, oc, at], PS[:, 2 + oc, :], ACT.Identity,
                                                   bias=col(f"bk{l}", oc) if l != 2 else 0.0)
                    ins.then_inc(khi_done, 1)
                    act.wait_ge(xT_mm, GROUPS * u + g + 1)
                    for c in range(KC):
                        ins = nc.scalar.activation(xnT[:, c, at], PS[:, c, :], ACT.Identity)
                    ins.then_inc(xT_done, 1)
                    act.wait_ge(q_mm[l], g + 1)
                    for oc in range(KC):
                        ins = nc.scalar.activation(q_hi[:, oc, at], PS[:, 6 + oc, :], ACT.Identity,
                                                   bias=col(f"bq{l}", oc) if l != 2 else 0.0)
                    ins.then_inc(qhi_done, 1)
                else:
                    act.wait_ge(ctx_in[p], 16 * turn)
                    for c in range(KC):
                        ins = nc.scalar.activation(k_hi[:, c, at], ctxg[:, p, c, :], ACT.Identity)
                    ins.then_inc(khi_done, 1)
                    act.wait_ge(xT_mm, g + 1)
                    for c in range(KC):
                        ins = nc.scalar.activation(q_hi[:, c, at], PS[:, c, :], ACT.Identity)
                    ins.then_inc(qhi_done, 1)

            def take_stack(l, s, k):
                act.wait_ge(sel_mm, s + 1)
                if not (isinstance(s, int) and s < 4):
                    act.wait_ge(sc_mm, 2 * s - 6)
                nc.scalar.activation(qk[:, k % 4, :], PS[:, 0, :], ACT.Identity).then_inc(sel_done, 1)

            def exps(l, s, k):
                for h in range(2):
                    act.wait_ge(sc_mm, 2 * s + h + 1)
                    if h == 0 and not (isinstance(s, int) and s < 2):
                        act.wait_ge(pv_mm, s - 1)
                    nc.scalar.activation(probs[:, 2 * (k % 2) + h, :], PS[:, 3 + h, :], ACT.Exp, scale=SCALE
                                         ).then_inc(exp_done, 1)

            def attend(l, i):
                for k in range(2 * PAIRS):
                    take_stack(l, STEPS * l + 2 * PAIRS * i + k, k)
                    n = k - 3
                    if n >= 0 or not isinstance(i, int):
                        exps(l, STEPS * l + 2 * PAIRS * i + n, n % (2 * PAIRS))

            def take_oT(l, b, p):
                b0 = B * (l - 1) + b
                act.wait_ge(oTr_mm, b0 + 1)
                if not isinstance(b, int):
                    act.wait_ge(wo_mm, b0 - 1)
                nc.scalar.activation(oTs[:, p, :], PS[:, p, :], ACT.Identity).then_inc(oTr_done, 1)

            def norm(l, g, p):
                u = 2 * l + 1
                at = ds(g * 512, 512)
                act.wait_ge(xT_mm, GROUPS * u + g + 1)
                for c in range(KC):
                    ins = nc.scalar.activation(nT[:, c, at] if l == 3 else xnT[:, c, at], PS[:, c, :], ACT.Identity,
                                               scale=col("norm_w", c) if l == 2 else 1.0)
                ins.then_inc(xT_done, 1)
                if l in (1, 2):
                    act.wait_ge(lg_mm[l], g + 1)
                    if not (isinstance(g, int) and g == 0):
                        act.wait_ge(lgn_mm[l], g)
                    nc.scalar.activation(lgT[:], PS[0:8, 2, :], ACT.Identity).then_inc(lg_done[l], 1)

            def feed(n):
                for j in range(NJ[0]):
                    act.wait_ge(h_mm[0], NJ[0] * n + j + 1)
                    if j == 0 and n >= 2:
                        act.wait_ge(y_mm[0], n - 1)
                    nc.scalar.activation(hT[:, n % 2, j, :], PS[:, 4 + j % 4, :], ACT.Gelu, bias=col("b1_0", j)
                                         ).then_inc(h_done[0], 1)

            def sparse(l):
                nh = NJ[l] // 4
                n0, h0 = NT * (l - 1), NT * (NJ[1] // 4) * (l - 1)

                def a(i, p):
                    act.wait_ge(xg_mm, n0 + i + 1)
                    if l == 1:
                        nc.scalar.activation(xh[:, p].rearrange("p c t -> p (c t)"), PS[:, 0, 0:D], ACT.Identity
                                             ).then_inc(xh_done, 1)
                    else:
                        for c in range(KC):
                            ins = nc.scalar.activation(xh[:, p, c], PS[:, 0, c * P:(c + 1) * P], ACT.Identity,
                                                       scale=col("norm_w", c))
                        ins.then_inc(xh_done, 1)

                def b(i):
                    for h in range(nh):
                        act.wait_ge(hid_mm, h0 + nh * i + h + 1)
                        nc.scalar.activation(hn[:, h * 512:(h + 1) * 512], PS[:, 1 + h, :], ACT.Gelu).then_inc(gelu_done, 1)

                def d(i):
                    for h in range(nh):
                        act.wait_ge(ht_mm, h0 + nh * i + h + 1)
                        nc.scalar.activation(hh[:, 4 * h:4 * h + 4, :].rearrange("p j t -> p (j t)"), PS[:, 3 + h, :],
                                             ACT.Identity).then_inc(hh_done, 1)
                a(0, 0)
                b(0)
                a(1, 1)

                def turn(i):
                    d(i - 1)
                    if i < NT:
                        b(i)
                    if i + 1 < NT:
                        a(i + 1, (i + 1) % 2)
                turn(1)
                turn(2)
                with act.Fori(0, (NT - 5) // 2) as k:
                    for q in range(2):
                        i = 2 * k + q + 3
                        d(i - 1)
                        b(i)
                        a(i + 1, q)
                for i in range(NT - 2, NT + 1):
                    turn(i)

            for l in lo_l:
                for p in range(2):
                    project(l, p, p)
                with act.Fori(1, GROUPS // 2) as i:
                    for p in range(2):
                        project(l, 2 * i + p, p, i + 1)
                attend(l, 0)
                with act.Fori(1, B // 2) as i:
                    attend(l, i)
                for n in range(-3, 0):
                    exps(l, STEPS * (l + 1) + n, n % (2 * PAIRS))
                if l:
                    for p in range(2):
                        take_oT(l, p, p)
                    with act.Fori(1, B // 2) as i:
                        for p in range(2):
                            take_oT(l, 2 * i + p, p)
                if not ffn(l):
                    continue
                u = 2 * l + 1

                def norm_pair(g):
                    for p in range(2):
                        roots(u, g + p, p)
                    for p in range(2):
                        norm(l, g + p, p)
                for g in range(0, GROUPS, 2):
                    norm_pair(g)
                if l == 0:
                    for n in range(GROUPS):
                        feed(n)
                elif l < 3:
                    act.wait_ge(route_v[l], ROUTE * GROUPS)
                    nc.scalar.activation(gt[:, 3, :], gt[:, 2, :], ACT.Exp).then_inc(route_e[l], 1)
                    sparse(l)
                else:
                    def quantised(g, p):
                        act.wait_ge(mx3_mm, 3 * g + 1)
                        nc.scalar.activation(bcast[:, p, :], PS[:, 2, :], ACT.Identity).then_inc(bc_done, 1)
                        for c in range(NJ3 + 1):
                            if c < NJ3:
                                act.wait_ge(h_done[3], NJ3 * g + c + 1)
                                nc.scalar.activation(hT[:, 1, c, :], hT[:, 0, c, :], ACT.Identity,
                                                     scale=col("conv_w", NJ3 + c), bias=col("conv_b", c)
                                                     ).then_inc(tap_done, 1)
                            if c:
                                act.wait_ge(cv_done, NJ3 * g + c)
                                nc.scalar.activation(hT[:, 1, c - 1, :], hT[:, 1, c - 1, :], ACT.Silu
                                                     ).then_inc(silu_done, 1)
                        act.wait_ge(q3_p, Q3P * g + Q3P)
                        if not (isinstance(g, int) and g == 0):
                            act.wait_ge(y_mm[3], g)
                        nc.scalar.activation(n2[:].rearrange("p c t -> p (c t)"),
                                             hT[:, 0, 0:NJ3, :].rearrange("p c t -> p (c t)"), ACT.Identity,
                                             bias=-MAGIC).then_inc(n2_done, 1)
                    for p in range(2):
                        quantised(p, p)
                    with act.Fori(1, GROUPS // 2) as i:
                        for p in range(2):
                            quantised(2 * i + p, p)

        @block.vector
        def _(dve):
            dve.wait_ge(const_in, 96)
            nc.vector.tensor_copy(sel[:].rearrange("p a b -> p (a b)"), xng[:].rearrange("p a b c -> p (a b c)")
                                  ).then_inc(consts, 1)
            nc.vector.tensor_scalar(bar[:], ident[:], MASKED, None, ALU.mult).then_inc(consts, 1)
            nc.vector.tensor_copy(pick[:].rearrange("p a b -> p (a b)"), wproj[0:2, 0, 0, :]).then_inc(consts, 1)
            nc.vector.memset(ones[:], 1.0)
            nc.vector.memset(ones_r[:].bitcast(F32), 1.0).then_inc(consts, 1)
            dve.wait_ge(consts, 4)
            dve.wait_ge(gates, 1)

            def rsqrt(u, g, p, k, v, root, r):
                q = lambda n: sml[:, p, n, :]

                def then(ins):
                    nonlocal k
                    k += 1
                    ins.then_inc(ln_v[u], 1)
                    dve.wait_ge(ln_v[u], LNV[u] * g + k)
                then(nc.vector.reciprocal(q(2), q(root)))
                then(nc.vector.tensor_tensor(q(3), q(2), q(2), ALU.mult))
                then(nc.vector.tensor_tensor(q(4), q(3), q(v), ALU.mult))
                then(nc.vector.tensor_scalar(q(5), q(4), -0.5, 1.5, ALU.mult, ALU.add))
                then(nc.vector.tensor_tensor(q(r), q(2), q(5), ALU.mult))
                return k

            def layernorm(l, u, g, p):
                q = lambda n: sml[:, p, n, :]
                first = isinstance(g, int) and g == 0
                k = 0

                def then(ins):
                    nonlocal k
                    k += 1
                    ins.then_inc(ln_v[u], 1)
                    dve.wait_ge(ln_v[u], LNV[u] * g + k)
                if first:
                    dve.wait_ge(*ln_ready(l, u))
                xn = xn_slot(u, g, p)
                tile = lambda t: x_res[:, ds(4 * g + t, 1), :].rearrange("p a d -> p (a d)")
                for t in range(4):
                    ins = nc.vector.bn_stats(st6[:, p, t, :], tile(t))
                then(ins)
                for t in range(4):
                    ins = nc.vector.bn_aggr(mv[:, p, t, :], st6[:, p, t, :])
                then(ins)
                var = mv[:, p, :, 1]
                then(nc.vector.tensor_scalar(q(0), var, LN_EPS, None, ALU.add))
                dve.wait_ge(ln_a[u], (2 if u in RMS else 1) * g + 1)
                k = rsqrt(u, g, p, k, 0, 1, 8)
                scale = 8
                if u in RMS:
                    then(nc.vector.tensor_tensor(q(9), q(8), q(8), ALU.mult))
                    then(nc.vector.tensor_tensor(q(10), q(9), var, ALU.mult))
                    if l == 0:
                        then(nc.vector.tensor_scalar(q(6), q(10), float(D), 1e-24, ALU.mult, ALU.max))
                    else:
                        then(nc.vector.tensor_scalar(q(6), q(10), RMS_EPS, None, ALU.add))
                    dve.wait_ge(ln_a[u], 2 * g + 2)
                    k = rsqrt(u, g, p, k, 6, 7, 11)
                    if l == 0:
                        then(nc.vector.scalar_tensor_tensor(q(9), q(8), float(D) ** 0.5, q(11), ALU.mult, ALU.mult))
                        scale = 9
                if u not in (3, 5) and not (isinstance(g, int) and g < 2):
                    dve.wait_ge(xT_mm, GROUPS * u + g - 1)
                for t in range(4):
                    ins = nc.vector.tensor_scalar(xn[:, t, :], tile(t), mv[:, p, t, 0:1], sml[:, p, scale, t:t + 1],
                                                  ALU.subtract, ALU.mult)
                if u == 5:
                    then(ins)
                    then(nc.vector.scalar_tensor_tensor(
                        x_res[:, ds(4 * g, 4), :].rearrange("p t d -> p (t d)"),
                        xn.rearrange("p t d -> p (t d)"), tg[:, 4 + l:5 + l],
                        x_res[:, ds(4 * g, 4), :].rearrange("p t d -> p (t d)"), ALU.mult, ALU.add))
                    for t in range(4):
                        ins = nc.vector.tensor_scalar(xn[:, t, :], xn[:, t, :], sml[:, p, 11, t:t + 1], None,
                                                      ALU.mult)
                if u == 7:
                    then(ins)
                    then(nc.vector.tensor_reduce(q(6), xn, AX.X, ALU.max, apply_absolute_value=True))
                    then(nc.vector.tensor_scalar(q(7), q(6), 1e-5, 1.0 / 127.0, ALU.max, ALU.mult))
                    then(nc.vector.reciprocal(q(9), q(7)))
                    then(nc.vector.tensor_scalar(s1[:, ds(4 * g, 4)], q(7), q3[:, 2:3], None, ALU.mult))
                    for t in range(4):
                        ins = nc.vector.tensor_scalar(xn[:, t, :], xn[:, t, :], sml[:, p, 9, t:t + 1], MAGIC,
                                                      ALU.mult, ALU.add)
                    then(ins)
                    ins = nc.vector.tensor_scalar(xn, xn, MAGIC + 127.0, -MAGIC, ALU.min, ALU.add)
                ins.then_inc(xn_ready, 1)
                assert k == LNV[u], (u, k)

            def project(l, g, p):
                layernorm(l, 2 * l, g, p)
                at = ds(g * 512, 512)
                if l:
                    dve.wait_ge(khi_done, GROUPS * l + g + 1)
                    for oc in range(KC):
                        ins = nc.vector.scalar_tensor_tensor(
                            k_lo[:, oc, at], PS[:, 2 + oc, :], col(f"bk{l}", oc) if l != 2 else 0.0,
                            k_hi[:, oc, at].bitcast(F32), ALU.add, ALU.subtract)
                    ins.then_inc(klo_done, 1)
                    dve.wait_ge(v_mm[l], g + 1)
                    for t in range(2):
                        v = vall[:, ds(4 * g + 2 * t, 2), :]
                        ps = PS[:, 4 + t, :].rearrange("p (t d) -> p t d", d=D)
                        if l == 2:
                            ins = nc.vector.tensor_copy(v, ps)
                        else:
                            ins = nc.vector.tensor_tensor(v, ps, bvb[:].unsqueeze(1).broadcast_to([P, 2, D]), ALU.add)
                    ins.then_inc(v_done[l], 1)
                    dve.wait_ge(qhi_done, GROUPS * l + g + 1)
                    for oc in range(KC):
                        ins = nc.vector.scalar_tensor_tensor(
                            q_lo[:, oc, at], PS[:, 6 + oc, :], col(f"bq{l}", oc) if l != 2 else 0.0,
                            q_hi[:, oc, at].bitcast(F32), ALU.add, ALU.subtract)
                    ins.then_inc(qlo_done, 1)
                else:
                    dve.wait_ge(khi_done, g + 1)
                    nc.vector.tensor_tensor(k_lo[:, :, at], ctxg[:, p], k_hi[:, :, at].bitcast(F32), ALU.subtract
                                            ).then_inc(klo_done, 1)
                    dve.wait_ge(qhi_done, g + 1)
                    nc.vector.tensor_tensor(q_lo[:, :, at], PS[:, 0:2, :], q_hi[:, :, at].bitcast(F32), ALU.subtract
                                            ).then_inc(qlo_done, 1)

            def maxima(l, s, k):
                for h in range(2):
                    dve.wait_ge(nat_mm, 2 * s + h + 1)
                    if h == 0 and not (isinstance(s, int) and s < 2):
                        dve.wait_ge(maxT_mm, s - 1)
                    nc.vector.tensor_reduce(nm[:, k % 2, :, h], PS[:, 1 + h, :].rearrange("p (q n) -> p q n", q=2),
                                            AX.X, ALU.max, negate=True).then_inc(max_done, 1)

            def take_maxT(l, s, k):
                dve.wait_ge(maxT_mm, s + 1)
                if not (isinstance(s, int) and s < 2):
                    dve.wait_ge(sc_mm, 2 * s - 2)
                nc.vector.tensor_copy(nmT[:, k % 2, :], PS[0:2, 6, 0:256]).then_inc(maxT_done, 1)

            def take_pv(l, s, k, j):
                dve.wait_ge(pv_mm, s + 1)
                if not (isinstance(s, int) and s < 4):
                    dve.wait_ge(oT_mm, j - 1)
                nc.vector.tensor_copy(pvs[:, k // 2 % 2, :], PS[:, 5, 0:256]).then_inc(pv_done, 1)

            def divide(l, s, k, b, j):
                dve.wait_ge(oT_mm, j + 1)
                m = k // 2 % 2
                o = PS[:, 7, 0:256].rearrange("p (q h d) -> p q h d", q=2, h=4)
                nc.vector.reciprocal(rc[:, m], o[:, :, :, DH]).then_inc(rc_done, 1)
                dve.wait_ge(rc_done, j + 1)
                at = 64 * (k % PAIRS // 2)
                nc.vector.tensor_tensor(
                    onat[:, ds(2 * b, 2), at:at + 64].rearrange("p q (h d) -> p q h d", d=DH), o[:, :, :, 0:DH],
                    rc[:, m].unsqueeze(3).broadcast_to([P, 2, 4, DH]), ALU.mult).then_inc(o_done, 1)

            def make_mask(i, p):
                dve.wait_ge(mask_in[p], 32 * (i + 1))
                if not isinstance(i, int):
                    dve.wait_ge(sc_mm, 2 * PAIRS * (2 * i + p - 1))
                nc.vector.tensor_scalar(mask_b[:, p], stage_i[:, p], 0.0, None, ALU.is_equal).then_inc(mask_done, 1)

            def attend_turn(l, i, k, last=False):
                s0 = STEPS * (l + 1) if last else STEPS * l + 2 * PAIRS * i
                if l == 0 and not last and k in (0, 5):
                    make_mask(i, k // 5)
                for lag, stage in ((1, "max"), (2, "maxT"), (4, "pv"), (5, "divide")):
                    n = k - lag
                    if n < 0 and isinstance(i, int) and not last or last and n >= 0:
                        continue
                    m = n % (2 * PAIRS)
                    b = (B if last else 2 * i) + n // PAIRS
                    j = (QUADS * (l + 1) if last else QUADS * l + PAIRS * i) + n // 2
                    if stage == "max":
                        maxima(l, s0 + n, m)
                    elif stage == "maxT":
                        take_maxT(l, s0 + n, m)
                    elif stage == "pv" and n % 2:
                        take_pv(l, s0 + n, m, j)
                    elif stage == "divide" and n % 2:
                        divide(l, s0 + n, m, b, j)

            def add_out(l, b, p):
                dve.wait_ge(wo_mm, B * (l - 1) + b + 1)
                x = x_res[:, ds(2 * b, 2), :].rearrange("p t d -> p (t d)")
                nc.vector.scalar_tensor_tensor(x, PS[:, 2 + p, :], tg[:, l:l + 1], x, ALU.mult, ALU.add
                                               ).then_inc(xo_done[l], 1)

            def route(l, g, p):
                k = ROUTE * g

                def then(ins):
                    nonlocal k
                    k = k + 1
                    ins.then_inc(route_v[l], 1)
                    dve.wait_ge(route_v[l], k)
                dve.wait_ge(lgn_mm[l], g + 1)
                then(nc.vector.tensor_copy(lgs[:, p].rearrange("p t e -> p (t e)"), PS[:, 3, 0:32]))
                for t in range(4):
                    ins = nc.vector.max(mx8[:, p, t, :], lgs[:, p, t, :])
                then(ins)
                for t in range(4):
                    ins = nc.vector.max_index(ix8[:, p, t, :], mx8[:, p, t, :], lgs[:, p, t, :])
                then(ins)
                then(nc.vector.tensor_copy(gt[:, 0:2, ds(4 * g, 4)], ix8[:, p, :, 0:2].rearrange("p t k -> p k t")))
                then(nc.vector.tensor_tensor(gt[:, 2, ds(4 * g, 4)], mx8[:, p, :, 1], mx8[:, p, :, 0], ALU.subtract))

            def plan(l):
                k = ROUTE * GROUPS

                def then(ins):
                    nonlocal k
                    k += 1
                    ins.then_inc(route_v[l], 1)
                    dve.wait_ge(route_v[l], k)
                tt, ts = nc.vector.tensor_tensor, nc.vector.tensor_scalar
                for m in range(2):
                    nc.vector.tensor_tensor(eq[:, m], iotas[:, 0:8].unsqueeze(1).broadcast_to([P, TILES, 8]),
                                            gt[:, m, :].unsqueeze(2).broadcast_to([P, TILES, 8]), ALU.is_equal
                                            ).then_inc(route_v[l], 1)
                k += 2
                dve.wait_ge(route_v[l], k)
                then(tt(picked[:], eq[:, 0], eq[:, 1], ALU.add))
                dve.wait_ge(route_e[l], 1)
                then(ts(gt[:, 4, :], gt[:, 3, :], 1.0, None, ALU.add))
                then(nc.vector.reciprocal(gt[:, 5, :], gt[:, 4, :]))
                then(ts(gt[:, 6, :], gt[:, 5, :], tg[:, 4 + l:5 + l], None, ALU.mult))
                then(tt(gt[:, 7, :], gt[:, 6, :], gt[:, 3, :], ALU.mult))
                assert k == ROUTE * GROUPS + 7
                dve.wait_ge(pos_mm, l)
                then(nc.vector.tensor_copy(scan[:, 0].rearrange("p t e -> p (t e)"), PS[:, 7, P:2 * P]))
                at = 0
                for step in (1, 2, 4, 8):
                    nc.vector.tensor_copy(scan[:, 1 - at, 0:step], scan[:, at, 0:step])
                    then(tt(scan[:, 1 - at, step:], scan[:, at, step:], scan[:, at, 0:TILES - step], ALU.add))
                    at = 1 - at
                total = scan[:, at, TILES - 1, :]
                then(ts(escan[:, 2, :], total, 1.0 / P, 63.5 / P, ALU.mult, ALU.add))
                then(ts(escan[:, 3, :], escan[:, 2, :], MAGIC, -MAGIC, ALU.add, ALU.add))
                then(nc.vector.tensor_copy(escan[:, 0, :], escan[:, 3, :]))
                es = 0
                for step in (1, 2, 4):
                    nc.vector.tensor_copy(escan[:, 1 - es, 0:step], escan[:, es, 0:step])
                    then(tt(escan[:, 1 - es, step:], escan[:, es, step:], escan[:, es, 0:8 - step], ALU.add))
                    es = 1 - es
                upto = escan[:, es, :]
                then(tt(escan[:, 2, :], upto, escan[:, 3, :], ALU.subtract))
                then(ts(escan[:, 2, :], escan[:, 2, :], float(P), None, ALU.mult))
                where = scan[:, 1 - at]
                flat = lambda ap: ap.rearrange("p t e -> p (t e)")
                then(tt(flat(where), flat(scan[:, at]), PS[:, 7, P:2 * P], ALU.subtract))
                then(tt(flat(where), flat(where), PS[:, 7, 0:P], ALU.add))
                then(tt(where, where, escan[:, 2, :].unsqueeze(1).broadcast_to([P, TILES, 8]), ALU.add))
                for m in range(2):
                    then(tt(eq[:, m], eq[:, m], where, ALU.mult))
                    then(nc.vector.tensor_reduce(posf[:, m, :], eq[:, m], AX.X, ALU.add))
                nc.vector.tensor_copy(pos[:], posf[:]).then_inc(placed, 1)
                for e in range(8):
                    if e == 0:
                        then(ts(tile_e[:, 0, :], iotas[:, 0:NT], escan[:, es, 0:1], None, ALU.is_ge))
                    else:
                        then(nc.vector.scalar_tensor_tensor(tile_e[:, e % 2, :], iotas[:, 0:NT], escan[:, es, e:e + 1],
                                                            tile_e[:, 1 - e % 2, :], ALU.is_ge, ALU.add))
                of, half, odd = tile_e[:, 0, :], tile_e[:, 1, :], tile_e[:, 2, :]
                then(ts(of, tile_e[:, 1, :], float(EXPERTS - 1), None, ALU.min))
                then(ts(half, of, 0.5, -0.25, ALU.mult, ALU.add))
                then(ts(half, half, MAGIC, -MAGIC, ALU.add, ALU.add))
                then(nc.vector.scalar_tensor_tensor(odd, half, -2.0, of, ALU.mult, ALU.add))
                ts(table[0:1, 0, :], of[0:1], 1.0 + EXPERTS * (l - 1), None, ALU.add)
                ts(table[0:1, 1, :], odd[0:1], float(RING), None, ALU.mult)
                ts(upto_e[:], upto[0:1], 1.0 + (NT + 1) * (l - 1), None, ALU.add)
                ts(is_e[:], of[0:16], col("expert16", 0, 16), None, ALU.is_equal).then_inc(tables, 1)

            def split_biases(l):
                n = NJ[l] * P
                dve.wait_ge(bias_in, 32 * l)
                for r, (v, h, o) in enumerate(((b1f[:, 0:n], bh[:, 0:n], b1s[:, 0:n]), (b2g[:], bh[:, 0:D], b2t[:]))):
                    nc.vector.tensor_copy(h, v).then_inc(bias_v, 1)
                    dve.wait_ge(bias_v, 4 * (l - 1) + 2 * r + 1)
                    nc.vector.scalar_tensor_tensor(o, h.bitcast(F32), col("low16", 0, 16), v, ALU.mult, ALU.add
                                                   ).then_inc(bias_v, 1)
                    dve.wait_ge(bias_v, 4 * (l - 1) + 2 * r + 2)

            def sparse(l):
                nh = NJ[l] // 4
                n0, h0 = NT * (l - 1), NT * (NJ[1] // 4) * (l - 1)
                t0 = (NT + 1) * (l - 1) + 1

                def a(i, p):
                    dve.wait_ge(xh_done, n0 + i + 1)
                    for c in range(KC):
                        ps, h, o = PS[:, 0, c * P:(c + 1) * P], xh[:, p, c].bitcast(F32), xl[:, p, c]
                        if l == 1:
                            ins = nc.vector.tensor_tensor(o, ps, h, ALU.subtract)
                        else:
                            ins = nc.vector.scalar_tensor_tensor(o, ps, col("norm_w", c), h, ALU.mult, ALU.subtract)
                    ins.then_inc(xl_done, 1)

                def b(i, p):
                    nc.vector.tensor_copy(of_e[:, p, :], is_e[:, ds(i, 1)].bitcast(F32).broadcast_to([16, P])).then_inc(e_done, 1)

                def d(i):
                    for h in range(nh):
                        dve.wait_ge(hh_done, h0 + nh * i + h + 1)
                        at = slice(4 * h, 4 * h + 4)
                        nc.vector.tensor_tensor(hl[:, at].rearrange("p j t -> p (j t)"), PS[:, 3 + h, :],
                                                hh[:, at].rearrange("p j t -> p (j t)").bitcast(F32), ALU.subtract
                                                ).then_inc(hl_done, 1)

                def e(i, p, turn):
                    dve.wait_ge(tiles_done, t0 + i + 1)
                    before = ((NT + 1) // 2 if p == 0 else NT // 2) * (l - 1) + turn - 1
                    if not (isinstance(turn, int) and before == 0):
                        dve.wait_ge(ys_out[p], 16 * before)
                    nc.vector.tensor_copy(yo[:, p], PS[:, 5, 0:D]).then_inc(yo_done, 1)
                dve.wait_ge(tables, l)
                b(0, 0)
                a(0, 0)
                b(1, 1)
                a(1, 1)

                def turn(i):
                    d(i - 1)
                    if i + 1 < NT:
                        a(i + 1, (i + 1) % 2)
                    e(i - 1, (i - 1) % 2, (i - 1) // 2 + 1)
                    if i + 1 < NT:
                        b(i + 1, (i + 1) % 2)
                turn(1)
                turn(2)
                with dve.Fori(0, (NT - 5) // 2) as k:
                    for q in range(2):
                        i = 2 * k + q + 3
                        d(i - 1)
                        a(i + 1, q)
                        e(i - 1, q, k + 2)
                        b(i + 1, q)
                for i in range(NT - 2, NT + 1):
                    turn(i)
                for k in range(FED[l]):
                    dve.wait_ge(yg_in[k % 8], 16 * (FED[l] // 8 * (l - 1) + k // 8 + 1))
                    if k % 2:
                        dve.wait_ge(y_done[l], k)
                    nc.vector.scalar_tensor_tensor(x_res[:, k // 2, :], yg[:, k, :], gt[:, 6 + k % 2, k // 2:k // 2 + 1],
                                                   x_res[:, k // 2, :], ALU.mult, ALU.add).then_inc(y_done[l], 1)

            def split_b2():
                dve.wait_ge(b2_in, 16)
                nc.vector.tensor_copy(b2h[:], b2f[:]).then_inc(prep, 1)
                dve.wait_ge(prep, PREP - 1)
                nc.vector.scalar_tensor_tensor(b2s[:], b2h[:].bitcast(F32), col("low", 0, 2), b2f[:],
                                               ALU.mult, ALU.add).then_inc(prep, 1)

            def add_feed(n):
                dve.wait_ge(y_mm[0], n + 1)
                for t in range(4):
                    x = x_res[:, 4 * n + t, :]
                    nc.vector.scalar_tensor_tensor(x, PS[:, 2 * (n % 2) + t // 2, (t % 2) * D:(t % 2 + 1) * D], tg[:, 4:5], x,
                                                   ALU.mult, ALU.add).then_inc(y_done[0], 1)

            for l in lo_l:
                for p in range(2):
                    project(l, p, p)
                with dve.Fori(1, GROUPS // 2) as i:
                    for p in range(2):
                        project(l, 2 * i + p, p)
                for k in range(2 * PAIRS):
                    attend_turn(l, 0, k)
                with dve.Fori(1, B // 2) as i:
                    for k in range(2 * PAIRS):
                        attend_turn(l, i, k)
                for k in range(5):
                    attend_turn(l, B // 2, k, last=True)
                if l:
                    for p in range(2):
                        add_out(l, p, p)
                    with dve.Fori(1, B // 2) as i:
                        for p in range(2):
                            add_out(l, 2 * i + p, p)
                else:
                    dve.wait_ge(o_done, QUADS)
                    x = x_res[:].rearrange("p t d -> p (t d)")
                    nc.vector.scalar_tensor_tensor(x, wide[:], tg[:, 0:1], x, ALU.mult, ALU.add).then_inc(xo_done[0], 1)
                if not ffn(l):
                    continue
                u = 2 * l + 1
                if l == 0:
                    dve.wait_ge(w0_in, 32)
                    w1 = wslots[:, 0:KC * NJ[0] * P].rearrange("p (c h) -> p c h", c=KC)
                    for c in range(KC):
                        nc.vector.tensor_scalar(w1[:, c, 0:P], w1[:, c, 0:P], col("gamma_l", c), None, ALU.mult
                                                ).then_inc(prep, 1)
                        nc.vector.tensor_scalar(w1[:, c, P:], w1[:, c, P:], col("gamma_h", c), None, ALU.mult
                                                ).then_inc(prep, 1)
                if l == 3:
                    k3 = 0

                    def then3(ins):
                        nonlocal k3
                        k3 += 1
                        ins.then_inc(q3_v, 1)
                        dve.wait_ge(q3_v, k3)
                    w1f, w2f = wslot[:, 0, 0:2048], wslot[:, 1, 0:2048]
                    dve.wait_ge(w3_in, 32)
                    nc.vector.tensor_reduce(q3[:, 0:1], w1f, AX.X, ALU.add, apply_absolute_value=True)
                    then3(nc.vector.tensor_reduce(q3[:, 1:2], w2f, AX.X, ALU.add, apply_absolute_value=True))
                    dve.wait_ge(q3_mm, 1)
                    then3(nc.vector.tensor_scalar(q3[:, 2:4], PS[:, 7, 0:2], 1.0 / (H3 * D), 1e-5, ALU.mult, ALU.max))
                    then3(nc.vector.reciprocal(q3[:, 4:6], q3[:, 2:4]))
                    then3(nc.vector.tensor_scalar(w1f, w1f, q3[:, 4:5], MAGIC, ALU.mult, ALU.add))
                    then3(nc.vector.tensor_scalar(w2f, w2f, q3[:, 5:6], MAGIC, ALU.mult, ALU.add))
                    then3(nc.vector.tensor_scalar(w1f, w1f, -MAGIC, 1.0, ALU.add, ALU.min))
                    then3(nc.vector.tensor_scalar(w2f, w2f, -MAGIC, 1.0, ALU.add, ALU.min))
                    then3(nc.vector.tensor_scalar(w1q[:].rearrange("p c h -> p (c h)"), w1f, -1.0, None, ALU.max))
                    then3(nc.vector.tensor_scalar(w2q[:].rearrange("p c h -> p (c h)"), w2f, -1.0, None, ALU.max))
                    then3(nc.vector.tensor_scalar(q3[:, 6:7], q3[:, 3:4], tg[:, 7:8], None, ALU.mult))

                def norm_pair(g):
                    for p in range(2):
                        layernorm(l, u, g + p, p)
                    if l in (1, 2):
                        for p in range(2):
                            route(l, g + p, p)
                if l in (1, 2):
                    split_biases(l)
                for g in range(0, GROUPS, 2):
                    norm_pair(g)
                if l == 0:
                    split_b2()
                    for n in range(GROUPS):
                        add_feed(n)
                elif l < 3:
                    plan(l)
                    sparse(l)
                else:
                    def quantised(g, p):
                        first = isinstance(g, int) and g == 0
                        k = Q3P * g
                        done = 0

                        def then(ins):
                            nonlocal done
                            done += 1
                            ins.then_inc(q3_p, 1)
                            dve.wait_ge(q3_p, k + done)
                        q = lambda n: q3g[:, p, n, :]
                        two = lambda ap: ap.rearrange("p (b t) -> p b t", b=2)
                        then(nc.vector.tensor_copy(q(0), s1[:, ds(4 * g, 4)]))
                        dve.wait_ge(bc_done, g + 1)
                        if not first:
                            dve.wait_ge(n2_done, g)
                        for c in range(NJ3 + 1):
                            if c < NJ3:
                                dve.wait_ge(h_mm[3], NJ3 * g + c + 1)
                                nc.vector.tensor_tensor(hT[:, 0, c, :], PS[:, 4 + c % 4, :], bcast[:, p, :], ALU.mult
                                                        ).then_inc(h_done[3], 1)
                            if c:
                                m = c - 1
                                dve.wait_ge(tap_done, NJ3 * g + c)
                                h, y = two(hT[:, 0, m, :]), two(hT[:, 1, m, :])
                                nc.vector.scalar_tensor_tensor(y[:, :, 1:S], h[:, :, 0:S - 1], col("conv_w", m),
                                                               y[:, :, 1:S], ALU.mult, ALU.add).then_inc(cv_v, 1)
                                dve.wait_ge(cv_v, NJ3 * g + c)
                                nc.vector.scalar_tensor_tensor(y[:, :, 0:S - 1], h[:, :, 1:S], col("conv_w", 2 * NJ3 + m),
                                                               y[:, :, 0:S - 1], ALU.mult, ALU.add).then_inc(cv_done, 1)
                        dve.wait_ge(silu_done, NJ3 * g + NJ3)
                        then(nc.vector.tensor_reduce(amx[:], hT[:, 1, 0:NJ3, :].rearrange("p c t -> p t c"), AX.X, ALU.max,
                                                     apply_absolute_value=True))
                        dve.wait_ge(mx3_mm, 3 * g + 2)
                        then(nc.vector.tensor_reduce(q(1), PS[:, 2, :].rearrange("p (t n) -> p t n", t=4), AX.X, ALU.max))
                        then(nc.vector.tensor_scalar(q(3), q(1), 1e-5, 1.0 / 127.0, ALU.max, ALU.mult))
                        then(nc.vector.reciprocal(q(2), q(3)))
                        then(nc.vector.tensor_scalar(q(1), q(3), q3[:, 6:7], None, ALU.mult))
                        dve.wait_ge(mx3_mm, 3 * g + 3)
                        h = hT[:, 0, 0:NJ3, :]
                        then(nc.vector.tensor_tensor(h, hT[:, 1, 0:NJ3, :],
                                                     PS[:, 3, :].unsqueeze(1).broadcast_to([P, NJ3, 512]), ALU.mult))
                        h = h.rearrange("p c t -> p (c t)")
                        then(nc.vector.tensor_scalar(h, h, 127.0, MAGIC, ALU.min, ALU.add))
                        assert done == Q3P
                        dve.wait_ge(y_mm[3], g + 1)
                        for t in range(4):
                            x = x_res[:, ds(4 * g + t, 1), :].rearrange("p a d -> p (a d)")
                            nc.vector.scalar_tensor_tensor(x, PS[:, t // 2, (t % 2) * D:(t % 2 + 1) * D],
                                                           q3g[:, p, 1, t:t + 1], x, ALU.mult, ALU.add
                                                           ).then_inc(y_done[3], 1)
                    for p in range(2):
                        quantised(p, p)
                    with dve.Fori(1, GROUPS // 2) as i:
                        for p in range(2):
                            quantised(2 * i + p, p)


def constants():
    sel = np.zeros((P, 4, 4, P), np.float32)
    rows = {0: (0, 2), 1: (1,), 2: (0, 1), 3: (2,)}
    for part, blocks in rows.items():
        for v in range(4):
            for h in range(2):
                for r in blocks:
                    for d in range(DH):
                        sel[32 * v + DH * h + d, part, v, 64 * h + DH * r + d] = 1.0
    pick = np.zeros((2, 2, P), np.float32)
    pick[0, 0] = pick[1, 1] = 1.0
    return {"sel": sel.reshape(P, 16 * P), "ident": np.eye(P, dtype=np.float32), "pick": pick.reshape(2, 2 * P),
            "tri": np.triu(np.ones((P, P), np.float32), 1),
            "iotas": np.ascontiguousarray(np.broadcast_to(np.arange(NT + 1, dtype=np.float32), (P, NT + 1)))}


def layout(a):
    c = np.ascontiguousarray
    columns = lambda v: v.reshape(-1, P).T
    rows = lambda v, n: c(np.broadcast_to(v, (n,) + v.shape))
    table = [
        np.broadcast_to(np.concatenate([a["g_xattn"], a["g_ffn"]]), (P, 8)),
        columns(a["L1_xattn_bq"]), columns(a["L1_xattn_bk"]), columns(a["L3_xattn_bq"]),
        columns(a["L3_xattn_bkv"][:D]), columns(a["L0_ffn_light_gamma"]), columns(a["L0_ffn_heavy_gamma"]),
        columns(np.concatenate([a["L0_ffn_light_b1"], a["L0_ffn_heavy_b1"]])), columns(a["L2_ffn_norm_weight"]),
        *[columns(a["L3_ffn_conv_w"][:, 0, tap]) for tap in range(3)], columns(a["L3_ffn_conv_b"]),
        np.where(np.arange(P) == 1, -1.0, 0.0).astype(np.float32).reshape(P, 1),
        np.where(np.arange(P) // 8 == 1, -1.0, 0.0).astype(np.float32).reshape(P, 1),
        (np.arange(P) % 8).astype(np.float32).reshape(P, 1),
    ]
    ctx = a["ctx_1024"].reshape(T, D)
    mask = a["mask_Bx1xSxS2_ik1"].reshape(B, S, S)
    wkv = a["L3_xattn_Wkv"]
    out = constants()
    out.update({
        "x": c(a["x"].reshape(T, D)), "ctx": c(ctx), "ctxT": c(ctx.T),
        "mask": c(mask.reshape(T, S)), "maskT": c(mask.transpose(0, 2, 1).reshape(T, S)),
        "cols": c(np.concatenate(table, axis=1)),
        "wproj_1": c(np.stack([a[f"L1_xattn_W{n}"].T for n in "qkvo"])),
        "wproj_2": c(np.stack([a[f"L2_xattn_W_{n}"] for n in "qkvo"])),
        "wproj_3": c(np.stack([a["L3_xattn_Wq"], wkv[:, :D], wkv[:, D:], a["L3_xattn_Wo"]])),
        "bo_1": c(a["L1_xattn_bo"].reshape(1, D)), "bo_2": c(a["L2_xattn_b_o"].reshape(1, D)),
        "bo_3": c(a["L3_xattn_bo"].reshape(1, D)),
        "bv_1": rows(a["L1_xattn_bv"], P), "bv_3": rows(a["L3_xattn_bkv"][D:], P),
        "W1_0": c(np.concatenate([a["L0_ffn_light_w1"], a["L0_ffn_heavy_w1"]], axis=1)),
        "W2_0": c(np.concatenate([a["L0_ffn_light_w2"], a["L0_ffn_heavy_w2"]], axis=0)),
        "b2_0": rows(np.stack([a["L0_ffn_light_b2"], a["L0_ffn_heavy_b2"]]), 2),
        "W1_1": c(a["L1_ffn_W1"].reshape(EXPERTS * D, -1)), "W2_1": c(a["L1_ffn_W2"].reshape(-1, D)),
        "wg_1": c(a["L1_ffn_Wr"]), "b2_1": c(np.tile(a["L1_ffn_b2"], (2, 1))),
        "b1_1": c(np.tile(a["L1_ffn_b1"], (2, 1))), "b1_2": c(np.tile(a["L2_ffn_b1"], (2, 1))),
        "W1_2": c(a["L2_ffn_w1"].transpose(0, 2, 1).reshape(EXPERTS * D, -1)),
        "W2_2": c(a["L2_ffn_w2"].transpose(0, 2, 1).reshape(-1, D)),
        "wg_2": c(a["L2_ffn_gate_w"].T), "b2_2": c(np.tile(a["L2_ffn_b2"], (2, 1))),
        "W1_3": c(a["L3_ffn_w1"].T), "W2_3": c(a["L3_ffn_w2"].T),
    })
    return out


def kernel(**inputs):
    import concourse.bacc as bacc
    from concourse.bass_utils import run_bass_kernel_spmd

    arrays = layout(inputs)
    nc = bacc.Bacc("TRN2", target_bir_lowering=False, num_devices=1)
    io = {name: nc.dram_tensor(name + "_dram", a.shape, mybir.dt.from_np(a.dtype), kind="ExternalInput").ap()
          for name, a in arrays.items()}
    io["out"] = nc.dram_tensor("out_dram", (T, D), F32, kind="ExternalOutput").ap()
    build(nc, io)
    got = run_bass_kernel_spmd(nc, [{name + "_dram": a for name, a in arrays.items()}], core_ids=[0])
    return got.results[0]["out_dram"].reshape(B, S, D)
```

```python
from contextlib import ExitStack

import numpy as np

import concourse.bass as bass
from concourse import mybir

F32 = mybir.dt.float32
F32R = mybir.dt.float32r
BF16 = mybir.dt.bfloat16
I32 = mybir.dt.int32
U32 = mybir.dt.uint32
ALU = mybir.AluOpType
ACT = mybir.ActivationFunctionType
AX = mybir.AxisListType
ds = bass.ds

P = 128
B, S, D = 8, 256, 256
HEADS, DH = 16, 16
T = B * S
TILES = T // P
KC = D // P
GROUPS = T // 512
PAIRS = HEADS // 2
STEPS = B * PAIRS
QUADS = STEPS // 2
LAYERS = 4
EXPERTS = 8
SCALE = 1.0 / DH ** 0.5
LN_EPS = 1e-5
RMS_EPS = 1e-6
STACK = 3 * DH + 1
MAXROW = 2 * DH
MASKED = -2.0 ** 100
MAGIC = 1.5 * 2.0 ** 23
NJ = {0: 9, 1: 8, 2: 4}
NT = 2 * T // P + EXPERTS - 1
RING = 4096
W0 = KC * 9 * P + 9 * D
FED = {0: T // P, 1: 2 * T // P, 2: 2 * T // P, 3: T // P}
AHEAD = 8
ROUTE = 14
RMS = (1, 5)
BY_GROUP = (0, 4, 6)
RMS_AT = 10
OUT = {0: B, 1: B, 2: B, 3: B}
Q3P = 9
H3 = 1024
NJ3 = H3 // P
CONV_PE, CONV_DVE = (0, 2, 3, 4, 5), (1, 6, 7)
SILU = (0, 2, 1, 3, 4, 5, 6, 7)

COLS = {}


def _columns():
    at = 0
    for name, n in [("gate", 8), ("bq1", 2), ("bk1", 2), ("bq3", 2), ("bk3", 2), ("gamma_l", 2), ("gamma_h", 2),
                    ("b1_0", 9), ("norm_w", 2), ("conv_w", 24), ("conv_b", 8),
                    ("low", 1), ("low16", 1), ("expert16", 1), ("max_row", 1), ("part", 1)]:
        COLS[name] = (at, n)
        at += n
    return at


NCOL = _columns()


def build(nc, io, upto=8):
    ctx = ExitStack()
    with ctx:
        def sb(name, shape, dt=F32, stack=ctx):
            return stack.enter_context(nc.sbuf_tensor(name, shape, dt))

        def sem(name, n=None):
            if n is None:
                return ctx.enter_context(nc.semaphore(name))
            return [ctx.enter_context(nc.semaphore(f"{name}{i}")) for i in range(n)]

        x_res = sb("x_res", [P, TILES, D])
        wide = sb("wide", [P, KC * T])
        xnT = wide[:].rearrange("p (c t) -> p c t", c=KC)
        onat = wide[:].rearrange("p (t d) -> p t d", t=TILES)
        xng = sb("xng", [P, 2, 4, D])
        wslot = sb("wslot", [P, 2, 4096])
        wslots = wslot[:].rearrange("p s n -> p (s n)")
        wproj = sb("wproj", [P, 4, KC, D])
        sel = sb("sel", [P, 16, P], F32R)
        ident = sb("ident", [P, P])
        bar = sb("bar", [P, P], BF16)
        ones = sb("ones", [P, P])
        ones_r = sb("ones_r", [2, P], F32R)
        nm = sb("nm", [P, 2, 2, P])
        cols = sb("cols", [P, NCOL])
        tg = sb("tg", [P, 8])
        st6 = sb("st6", [P, TILES, 6])
        mv = sb("mv", [P, TILES, 2])
        sml = sb("sml", [P, 12, TILES])
        s1 = sb("s1", [P, TILES])
        bvb = sb("bvb", [P, D])
        bo_f = sb("bo_f", [2, D])
        bo_s = sb("bo_s", [2, D], F32R)
        wg = sb("wg", [P, KC, EXPERTS])
        gt = sb("gt", [P, 16, TILES])
        eq = sb("eq", [P, 2, TILES, 8])
        picked = sb("picked", [P, TILES, 8])
        scan = sb("scan", [P, 2, TILES, 8])
        escan = sb("escan", [P, 4, 8])
        posf = sb("posf", [P, 2, TILES])
        pos = sb("pos", [P, 2, TILES], U32)
        tile_e = sb("tile_e", [P, 3, NT])
        table = sb("table", [1, 2, NT], I32)
        upto_e = sb("upto_e", [1, 8], I32)
        is_e = sb("is_e", [16, NT], F32R)
        iotas = sb("iotas", [P, P])
        tri = sb("tri", [P, P])
        zero = sb("zero", [P, 1])
        yo = sb("yo", [P, 2, D])
        q3 = sb("q3", [P, 8])

        def col(name, i=0, parts=P):
            return cols[0:parts, COLS[name][0] + i:COLS[name][0] + i + 1]

        at = ExitStack()
        q_hi = sb("q_hi", [P, KC, T], F32R, at)
        q_lo = sb("q_lo", [P, KC, T], F32R, at)
        k_hi = sb("k_hi", [P, KC, T], F32R, at)
        k_lo = sb("k_lo", [P, KC, T], F32R, at)
        vall = sb("vall", [P, TILES, D], F32, at)
        vbuf = sb("vbuf", [P, 2, 2, HEADS * (DH + 1) + 15], F32, at)
        qk = sb("qk", [P, 4, 512], F32R, at)
        probs = sb("probs", [P, 4, 512], F32, at)
        pvs = sb("pvs", [P, 2, 256], F32, at)
        rc = sb("rc", [P, 2, 2, 4], F32, at)
        oTs = probs
        at.close()
        ft = ExitStack()
        xn2f = sb("xn2f", [P, 2, 4, D], F32, ft)
        f0 = ExitStack()
        w0h = sb("w0h", [P, W0], F32R, f0)
        w0l = sb("w0l", [P, W0], F32R, f0)
        x0h = sb("x0h", [P, KC, T], F32R, f0)
        x0l = sb("x0l", [P, KC, T], F32R, f0)
        h0f = sb("h0f", [P, 2, 512], F32, f0)
        h0h = sb("h0h", [P, 3, 512], F32R, f0)
        h0l = sb("h0l", [P, 3, 512], F32R, f0)
        b2f = sb("b2f", [2, 2, D], F32, f0)
        b2h = sb("b2h", [2, 2, D], F32R, f0)
        b2s = sb("b2s", [2, 2, D], F32R, f0)
        f0.close()
        f3 = ExitStack()
        nT = sb("nT", [P, KC, T], BF16, f3)
        bcast = sb("bcast", [P, GROUPS, 512], F32, f3)
        hid = sb("hid", [P, 2, NJ3, 512], F32, f3)
        act3 = sb("act3", [P, 2, NJ3, 512], F32, f3)
        n2 = sb("n2", [P, NJ3, 512], BF16, f3)
        q3g = sb("q3g", [P, 2, 4, 4], F32, f3)
        amx = sb("amx", [P, 512], F32, f3)
        f3.close()
        ft.close()
        fs = ExitStack()
        whi = sb("whi", [P, 2, RING], F32R, fs)
        wlo = sb("wlo", [P, 2, RING], F32R, fs)
        xn2 = sb("xn2", [P, 2, 4, D], F32, fs)
        rs = ExitStack()
        lgT = sb("lgT", [8, 512], F32, rs)
        rs.close()
        of_e = sb("of_e", [16, 4, P], F32R, fs)
        xg = sb("xg", [P, 2, D], F32, fs)
        xh = sb("xh", [P, 2, KC, P], F32R, fs)
        xl = sb("xl", [P, 2, KC, P], F32R, fs)
        hn = sb("hn", [P, 8 * P], F32, fs)
        hh = sb("hh", [P, 8, P], F32R, fs)
        hl = sb("hl", [P, 8, P], F32R, fs)
        b1f = sb("b1f", [16, 8 * P], F32, fs)
        b1s = sb("b1s", [16, 8 * P], F32R, fs)
        b2g = sb("b2g", [16, D], F32, fs)
        b2t = sb("b2t", [16, D], F32R, fs)
        tile_of = sb("tile_of", [P, 2, TILES], F32, fs)
        row_of = sb("row_of", [P, 2, TILES], F32, fs)
        ids = sb("ids", [P, 2 * TILES, 2 * AHEAD], BF16, fs)
        idx = sb("idx", [P, AHEAD], U32, fs)
        fs.close()
        in_row = wide[:, 2048:4096].bitcast(BF16).rearrange("p (j n) -> p j n", n=P)

        def tile_in(i, p):
            if isinstance(i, int) and 2 <= i < AHEAD:
                return wide[:, T - (AHEAD - i) * D:T - (AHEAD - i - 1) * D]
            return xg[:, p]

        bh = hn[0:16, :].bitcast(F32R)
        lgs, mx8, ix8 = (hn[:, r * P:(r + 1) * P].bitcast(F32 if r < 2 else U32).rearrange("p (t e) -> p t e", e=8)
                         for r in range(3))
        w1q = wslot[:, 0, 2048:2048 + KC * H3 // 2].bitcast(BF16).rearrange("p (c h) -> p c h", c=KC)
        w2q = wslot[:, 1, 2048:2048 + NJ3 * D // 2].bitcast(BF16).rearrange("p (j d) -> p j d", d=D)
        diag = lambda j, tap: wslot[:, (3 * j + tap) // 8, 3072 + (3 * j + tap) % 8 * P:3072 + ((3 * j + tap) % 8 + 1) * P]
        yg = wslots.rearrange("p (r d) -> p r d", d=D)
        stage_i = wslots[:, 4608:4608 + 2048].bitcast(I32).rearrange("p (b m n) -> p b m n", b=2, m=2)
        mask_b = wslots[:, 6656:6656 + 1024].bitcast(BF16).rearrange("p (b m n) -> p b m n", b=2, m=2)

        sel_f = wslots[:, 0:2048]

        def ctx_at(g):
            return xnT[:, :, g * 512:(g + 1) * 512]

        xt = nc.dram_tensor("x_tokens", (T, D), F32, kind="Internal").ap()
        xs = nc.dram_tensor("xs_sorted", (NT * P, D), F32, kind="Internal").ap()
        ys = nc.dram_tensor("ys_sorted", (NT * P, D), F32, kind="Internal").ap()

        PS = ctx.enter_context(nc.psum_tensor("PS", [P, 8, 512], F32))

        const_in, sel_in, later_in = sem("const_in"), sem("sel_in"), sem("later_in")
        x_in = sem("x_in", GROUPS)
        v0_in = sem("v0_in")
        consts = sem("consts")
        padded = sem("padded")
        gates = sem("gates")
        U = 2 * LAYERS
        ln_s, ln_v, ln_a, ln_x = sem("ln_s"), sem("ln_v", U), sem("ln_a"), sem("ln_x")
        xn_ready, xT_mm, xT_done = sem("xn_ready"), sem("xT_mm"), sem("xT_done")
        wproj_in, ctx_in = sem("wproj_in", LAYERS), sem("ctx_in", GROUPS)
        k_mm, v_mm, q_mm = sem("k_mm"), sem("v_mm"), sem("q_mm")
        khi_done, klo_done = sem("khi_done"), sem("klo_done")
        qhi_done, qlo_done, v_done = sem("qhi_done"), sem("qlo_done"), sem("v_done")
        sel_mm, sel_done = sem("sel_mm"), sem("sel_done")
        nat_mm, max_done = sem("nat_mm"), sem("max_done")
        maxT_mm, maxT_done = sem("maxT_mm"), sem("maxT_done")
        sc_mm, exp_done = sem("sc_mm"), sem("exp_done")
        v_copied, pv_mm, pv_done = sem("v_copied"), sem("pv_mm"), sem("pv_done")
        oT_mm, rc_done, o_done = sem("oT_mm"), sem("rc_done"), sem("o_done")
        mask_in, mask_done = sem("mask_in", 2), sem("mask_done")
        oTr_mm, oTr_done = sem("oTr_mm"), sem("oTr_done")
        wo_mm, xo_done = sem("wo_mm"), sem("xo_done", LAYERS)
        lg_mm, lg_done, lgn_mm, route_v, route_e = ([None] + sem(name, 2) for name in (
            "lg_mm", "lg_done", "lgn_mm", "route_v", "route_e"))
        w0_in, w_in, wg_in, b2_in, prep = sem("w0_in"), sem("w_in", 2), sem("wg_in"), sem("b2_in"), sem("prep")
        h_mm, h_done = {0: sem("h0_mm"), 3: sem("h3_mm")}, {0: sem("h0_done"), 3: sem("h3_done")}
        x0l_done, w0_scaled, w0h_done, w0l_done = sem("x0l_done"), sem("w0_scaled"), sem("w0h_done"), sem("w0l_done")
        h0h_done, h0l_done = sem("h0h_done"), sem("h0l_done")
        y_mm, y_done = {0: sem("y0_mm"), 3: sem("y3_mm")}, sem("y_done", LAYERS)
        xs_zeroed, bias_in, pos_mm, placed, tables = sem("xs_zeroed"), sem("bias_in"), sem("pos_mm"), sem("placed"), sem("tables")
        bias_v, split_hi, split_done, scattered = sem("bias_v"), sem("split_hi"), sem("split_done"), sem("scattered")
        xt_out, hot_done, idx_mm, idx_done, xq_in = sem("xt_out"), sem("hot_done"), sem("idx_mm"), sem("idx_done"), sem("xq_in", 2 + (AHEAD - 2) // 2)
        xg_in, xg_mm, xh_done, xl_done = sem("xg_in", 2), sem("xg_mm"), sem("xh_done"), sem("xl_done")
        e_done, hid_mm, gelu_done = sem("e_done"), sem("hid_mm"), sem("gelu_done")
        ht_mm, hh_done, hl_done = sem("ht_mm"), sem("hh_done"), sem("hl_done")
        tiles_done, yo_done, ys_out, yg_in = sem("tiles_done"), sem("yo_done"), sem("ys_out", 2), sem("yg_in", 8)
        w3_in, bo_v = sem("w3_in"), sem("bo_v")
        q3_mm, q3_v, q3_p = sem("q3_mm"), sem("q3_v"), sem("q3_p")
        row_mm, bc_done, tap_done, cv_v, cv_done = sem("row_mm"), sem("bc_done"), sem("tap_done"), sem("cv_v"), sem("cv_done")
        diag_done, cv_mm = sem("diag_done"), sem("cv_mm")
        amx_mm, hrow_mm, q3_rows = sem("amx_mm"), sem("hrow_mm"), sem("q3_rows")
        silu_done, n2_done = sem("silu_done"), sem("n2_done")
        out_done = sem("out_done")

        lo_l = [l for l in range(LAYERS) if 2 * l < upto]
        ffn = lambda l: 2 * l + 1 < upto

        def ln_ready(l, u):
            if u == 0:
                return x_in[GROUPS - 1], 16
            if u % 2:
                return xo_done[l], OUT[l]
            return y_done[l - 1], FED[l - 1]

        def xT_bank(u, g):
            return 2 * g if u == 0 else 2 * (g % 2) if u % 2 else 0

        def q_bank(l, g):
            return 4 if (g % 2 if l == 1 else g == GROUPS - 1) else 6

        def fed(l):
            return (yo_done, NT * l) if l in (1, 2) else (y_done[l], FED[l])

        def xn_slot(u, g):
            if u % 2 and g >= 2:
                return (xn2 if u in (3, 5) else xn2f)[:, g - 2]
            return xng[:, g % 2]

        block = ctx.enter_context(nc.Block())

        @block.sync
        def _(sp):
            def load_ctx(g):
                sp.dma_start(ctx_at(g), io["ctxT"][:, g * 512:(g + 1) * 512].rearrange("(c p) t -> p c t", p=P)
                             ).then_inc(ctx_in[g], 16)
            for g in range(GROUPS):
                sp.dma_start(x_res[:, 4 * g:4 * g + 4, :],
                             io["x"][g * 512:(g + 1) * 512, :].rearrange("(t p) d -> p t d", p=P)).then_inc(x_in[g], 16)
                if g == 0:
                    sp.dma_start(ident[:], io["ident"]).then_inc(const_in, 16)
                    sp.dma_start(cols[:], io["cols"]).then_inc(const_in, 16)
                load_ctx(g)
            sp.dma_start(sel_f, io["sel"]).then_inc(sel_in, 16)

            def load_proj(l):
                sp.wait_ge(xo_done[l - 1], B)
                sp.dma_start(wproj[:], io[f"wproj_{l}"].rearrange("w (c p) n -> p w c n", p=P)
                             ).then_inc(wproj_in[l], 16)
                sp.dma_start(bo_f[:], io[f"bo_{l}"]).then_inc(wproj_in[l], 16)
                if l != 2:
                    sp.dma_start(bvb[:], io[f"bv_{l}"]).then_inc(wproj_in[l], 16)

            for l in lo_l:
                if l in (1, 2):
                    if l == 2:
                        sp.wait_ge(lg_mm[1], GROUPS)
                    sp.dma_start(wg[:], io[f"wg_{l}"].rearrange("(c p) e -> p c e", p=P)).then_inc(wg_in, 16)
                if l == 0:
                    def load_mask(b, p):
                        for m, name in enumerate(("mask", "maskT")):
                            sp.dma_start(stage_i[:, p, m].rearrange("p (a n) -> p a n", a=2),
                                         io[name][ds(b * S, S), :].rearrange("(a p) n -> p a n", p=P)
                                         ).then_inc(mask_in[p], 16)
                    for p in range(2):
                        load_mask(p, p)
                    sp.dma_start(vall[:], io["ctx"].rearrange("(t p) d -> p t d", p=P)).then_inc(v0_in, 16)
                if l == 0:
                    sp.dma_start(tri[:], io["tri"]).then_inc(later_in, 16)
                    sp.dma_start(iotas[:], io["iotas"]).then_inc(later_in, 16)
                if l == 3:
                    sp.wait_ge(y_done[2], FED[2])
                    sp.dma_start(wslot[:, 0, 0:2048].rearrange("p (c h) -> p c h", c=KC),
                                 io["W1_3"].rearrange("(c p) h -> p c h", p=P)).then_inc(w3_in, 16)
                    sp.dma_start(wslot[:, 1, 0:2048].rearrange("p (j d) -> p j d", d=D),
                                 io["W2_3"].rearrange("(j p) d -> p j d", p=P)).then_inc(w3_in, 16)
                if l == 0:
                    with sp.Fori(1, B // 2) as i:
                        for p in range(2):
                            sp.wait_ge(mask_done, 2 * i + p - 1)
                            load_mask(2 * i + p, p)
                    sp.dma_start(wslots[:, 0:KC * NJ[0] * P].rearrange("p (c h) -> p c h", c=KC),
                                 io["W1_0"].rearrange("(c p) h -> p c h", p=P)).then_inc(w0_in, 16)
                    sp.dma_start(wslots[:, KC * NJ[0] * P:W0].rearrange("p (j d) -> p j d", d=D),
                                 io["W2_0"].rearrange("(j p) d -> p j d", p=P)).then_inc(w0_in, 16)
                    sp.wait_ge(padded, 2)
                    sp.dma_start(xs.rearrange("(i p) d -> p i d", p=P), yo[:, 0:1, :].broadcast_to([P, NT, D])
                                 ).then_inc(xs_zeroed, 16)
                if not ffn(l):
                    continue
                if l == 0:
                    sp.wait_ge(xo_done[0], B)
                    sp.dma_start(b2f[:], io["b2_0"]).then_inc(b2_in, 16)
                    for g in range(GROUPS):
                        load_ctx(g)
                    load_proj(1)
                if l in (1, 2):
                    sp.wait_ge(xo_done[l], B)
                    sp.dma_start(b1f[:, 0:NJ[l] * P], io[f"b1_{l}"]).then_inc(bias_in, 16)
                    sp.dma_start(b2g[:], io[f"b2_{l}"]).then_inc(bias_in, 16)
                    for g in range(GROUPS):
                        sp.wait_ge(xn_ready, GROUPS * (2 * l + 1) + g + 1)
                        sp.dma_start(xt[g * 512:(g + 1) * 512, :].rearrange("(t p) d -> p t d", p=P), xn_slot(2 * l + 1, g)
                                     ).then_inc(xt_out, 16)
                    n0 = NT * (l - 1)

                    def load_tile(i, p):
                        sp.wait_ge(xg_mm, n0 + i - AHEAD + 1 if isinstance(i, int) and i < AHEAD + 2 else n0 + i - 1)
                        sp.dma_start(xg[:, p], xs[ds(P * i, P), :]).then_inc(xg_in[p], 16)

                    def store_tile(i, p):
                        sp.wait_ge(yo_done, n0 + i + 1)
                        sp.dma_start(ys[ds(P * i, P), :], yo[:, p]).then_inc(ys_out[p], 16)
                    for i in range(AHEAD - 3):
                        store_tile(i, i % 2)
                    sp.wait_ge(scattered, 16 * FED[l] * l)
                    for i in range(AHEAD, AHEAD + 2):
                        load_tile(i, i % 2)
                        store_tile(i - 3, (i - 3) % 2)
                    sp.wait_ge(xg_mm, n0 + AHEAD)
                    for g in range(GROUPS):
                        i = AHEAD + 2 + g
                        load_tile(i, i % 2)
                        load_ctx(g)
                        store_tile(i - 3, (i - 3) % 2)
                    with sp.Fori(0, (NT - AHEAD - 3 - GROUPS) // 2) as k:
                        for q in range(2):
                            load_tile(2 * k + q + AHEAD + 2 + GROUPS, q)
                            store_tile(2 * k + q + AHEAD - 1 + GROUPS, (q + 1) % 2)
                    load_tile(NT - 1, 0)
                    load_proj(l + 1)
                    for i in range(NT - 4, NT):
                        store_tile(i, i % 2)
            if upto == 8:
                for g in range(GROUPS):
                    sp.wait_ge(y_done[3], 4 * (g + 1))
                    sp.dma_start(io["out"].rearrange("(t p) d -> p t d", p=P)[:, 4 * g:4 * g + 4, :],
                                 x_res[:, 4 * g:4 * g + 4, :]).then_inc(out_done, 16)
                sp.wait_ge(out_done, 16 * GROUPS)
            else:
                if upto % 2:
                    sp.wait_ge(xo_done[upto // 2], OUT[upto // 2])
                else:
                    sp.wait_ge(*ln_ready(upto // 2, upto))
                sp.dma_start(io["out"].rearrange("(t p) d -> p t d", p=P), x_res[:]).then_inc(out_done, 16)
                sp.wait_ge(out_done, 16)

        @block.gpsimd
        def _(pool):
            nc.gpsimd.memset(zero[:], 0.0).then_inc(padded, 1)
            nc.gpsimd.memset(yo[:], 0.0).then_inc(padded, 1)

            def heads(ap):
                return ap[..., 0:HEADS * (DH + 1)].rearrange("p t (h d) -> p t h d", d=DH + 1)

            def pad_v():
                for p in range(2):
                    nc.gpsimd.memset(heads(vbuf[:, p])[:, :, :, DH:DH + 1], 1.0).then_inc(padded, 1)
                nc.gpsimd.memset(vbuf[:, :, :, HEADS * (DH + 1):], 0.0).then_inc(padded, 1)
            pad_v()

            def load_expert(l, e):
                slot, h = e % 2, NJ[l] * P
                nc.gpsimd.dma_start(wslot[:, slot, 0:KC * h].rearrange("p (c h) -> p c h", c=KC),
                                    io[f"W1_{l}"][e * D:(e + 1) * D, :].rearrange("(c p) h -> p c h", p=P)
                                    ).then_inc(w_in[slot], 16)
                nc.gpsimd.dma_start(wslot[:, slot, KC * h:2 * KC * h].rearrange("p (j d) -> p j d", d=D),
                                    io[f"W2_{l}"][e * h:(e + 1) * h, :].rearrange("(j p) d -> p j d", p=P)
                                    ).then_inc(w_in[slot], 16)
            for l in lo_l:
                if l:
                    pool.wait_ge(*fed(l - 1))
                    pad_v()
                if l in (1, 2) and ffn(l):
                    if l == 1:
                        pool.wait_ge(y_mm[0], GROUPS * NJ[0])
                        pool.wait_ge(sc_mm, 2 * STEPS)
                    else:
                        pool.wait_ge(y_done[1], FED[1])
                    for e in range(2):
                        load_expert(l, e)

                def copy_v(b, p):
                    nc.gpsimd.tensor_copy(
                        heads(vbuf[:, p])[:, :, :, 0:DH],
                        vall[:, ds(2 * b, 2), :].rearrange("p t (h d) -> p t h d", d=DH)).then_inc(v_copied, 1)

                if l:
                    pool.wait_ge(v_done, GROUPS * l)
                else:
                    for g in range(GROUPS):
                        pool.wait_ge(khi_done, g + 1)
                        at = ds(g * 512, 512)
                        nc.gpsimd.tensor_tensor(k_lo[:, :, at], ctx_at(g), k_hi[:, :, at].bitcast(F32), ALU.subtract
                                                ).then_inc(klo_done, 1)
                    pool.wait_ge(v0_in, 16)
                for p in range(2):
                    copy_v(p, p)
                with pool.Fori(1, B // 2) as i:
                    for p in range(2):
                        b = 2 * i + p
                        pool.wait_ge(pv_mm, STEPS * l + PAIRS * (b - 1))
                        copy_v(b, p)
                if l == 3 and ffn(3):
                    pool.wait_ge(o_done, QUADS * 4)
                    for j, c in enumerate(CONV_PE):
                        for tap in range(3):
                            nc.gpsimd.tensor_scalar(diag(j, tap), ident[:], col("conv_w", tap * NJ3 + c), None, ALU.mult
                                                    ).then_inc(diag_done, 1)
                if l == 0 and ffn(0):
                    pool.wait_ge(w0_in, 32)
                    w1 = wslots[:, 0:KC * NJ[0] * P].rearrange("p (c h) -> p c h", c=KC)
                    for c in range(KC):
                        nc.gpsimd.tensor_scalar(w1[:, c, 0:P], w1[:, c, 0:P], col("gamma_l", c), None, ALU.mult
                                                ).then_inc(w0_scaled, 1)
                        nc.gpsimd.tensor_scalar(w1[:, c, P:], w1[:, c, P:], col("gamma_h", c), None, ALU.mult
                                                ).then_inc(w0_scaled, 1)
                    for w in range(2):
                        pool.wait_ge(w0h_done, w + 1)
                        at = slice(w * W0 // 2, (w + 1) * W0 // 2)
                        nc.gpsimd.tensor_tensor(w0l[:, at], wslots[:, at], w0h[:, at].bitcast(F32), ALU.subtract
                                                ).then_inc(w0l_done, 1)
                if l in (1, 2) and ffn(l):
                    n = 2 * KC * NJ[l] * P

                    def split(e):
                        slot = e % 2
                        w, wh, wl = wslot[:, slot, 0:n], whi[:, slot, 0:n], wlo[:, slot, 0:n]
                        if e >= 2:
                            pool.wait_ge(tiles_done, pool.value_load(upto_e[0:1, e - 2:e - 1], min_val=1, max_val=2 * NT + 2))
                        pool.wait_ge(w_in[slot], 32 * (EXPERTS // 2 * (l - 1) + e // 2 + 1))
                        nc.gpsimd.tensor_tensor(wh, w, zero[:].broadcast_to([P, n]), ALU.add).then_inc(split_hi, 1)
                        pool.wait_ge(split_hi, EXPERTS * (l - 1) + e + 1)
                        nc.gpsimd.tensor_tensor(wl, w, wh.bitcast(F32), ALU.subtract).then_inc(split_done, 1)

                    def reload(e):
                        if e + 2 < EXPERTS:
                            pool.wait_ge(split_done, EXPERTS * (l - 1) + e + 1)
                            load_expert(l, e + 2)
                    pool.wait_ge(xo_done[l], B)
                    for e in range(2):
                        split(e)
                    pool.wait_ge(placed, l)
                    if l == 1:
                        pool.wait_ge(xs_zeroed, 16)
                    else:
                        pool.wait_ge(xg_in[0], 16 * ((NT + 1) // 2 - AHEAD // 2))
                        pool.wait_ge(xg_in[1], 16 * (NT // 2 - AHEAD // 2))
                    for t in range(TILES):
                        if t == 5:
                            pool.wait_ge(idx_done, l)
                            pool.wait_ge(xt_out, 16 * GROUPS * l)
                            for i in range(AHEAD):
                                nc.gpsimd.indirect_dma_start(tile_in(i, i % 2), None, xt,
                                                             bass.IndirectOffsetOnAxis(idx[:, i:i + 1], 0)
                                                             ).then_inc(xq_in[i if i < 2 else 1 + i // 2], 16)
                        for m in range(2):
                            nc.gpsimd.indirect_dma_start(xs, bass.IndirectOffsetOnAxis(pos[:, m, t:t + 1], 0),
                                                         xn_slot(2 * l + 1, t // 4)[:, t % 4, :], None
                                                         ).then_inc(scattered, 16)
                    pool.wait_ge(tables, l)
                    for e in range(2):
                        reload(e)
                    for e in range(2, EXPERTS):
                        split(e)
                        reload(e)
                    pool.wait_ge(split_done, EXPERTS * l)
                    pool.wait_ge(ys_out[0], 16 * ((NT + 1) // 2) * l)
                    pool.wait_ge(ys_out[1], 16 * (NT // 2) * l)
                    for k in range(FED[l]):
                        if k >= 8:
                            pool.wait_ge(y_done[l], k - 7)
                        nc.gpsimd.indirect_dma_start(yg[:, k, :], None, ys,
                                                     bass.IndirectOffsetOnAxis(pos[:, k % 2, k // 2:k // 2 + 1], 0)
                                                     ).then_inc(yg_in[k % 8], 16)

        @block.tensor
        def _(pe):
            pe.wait_ge(const_in, 32)

            def transposes(u, g):
                pe.wait_ge(xn_ready, GROUPS * u + g + 1)
                at = xT_bank(u, g)
                same = [n for n in range(g) if xT_bank(u, n) == at]
                if same:
                    pe.wait_ge(*((x0l_done, same[-1] + 1) if u == 1 else (xT_done, GROUPS * (u - 1) + same[-1] + 1)))
                for c in range(KC):
                    for t in range(4):
                        mm = pe.transpose(PS[:, at + c, t * P:(t + 1) * P],
                                          xn_slot(u, g)[:, t, c * P:(c + 1) * P], ident[:])
                mm.then_inc(xT_mm, 1)

            def keys_values(l, g):
                p = g % 2
                pe.wait_ge(ctx_in[g], 16 * (l + 1))
                if g == 0:
                    pe.wait_ge(*fed(l - 1))
                    pe.wait_ge(wproj_in[l], 32 if l == 2 else 48)
                else:
                    pe.wait_ge(klo_done, GROUPS * l + g)
                for oc in range(KC):
                    for kc in range(KC):
                        mm = pe.matmul(PS[:, 2 + oc, :], wproj[:, 1, kc, oc * P:(oc + 1) * P], ctx_at(g)[:, kc, :],
                                       start=(kc == 0), stop=(kc == KC - 1))
                mm.then_inc(k_mm, 1)
                if g:
                    pe.wait_ge(v_done, GROUPS * (l - 1) + g)
                for t in range(4):
                    for kc in range(KC):
                        mm = pe.matmul(PS[:, 4 + t // 2, (t % 2) * D:(t % 2 + 1) * D],
                                       ctx_at(g)[:, kc, t * P:(t + 1) * P], wproj[:, 2, kc, :],
                                       start=(kc == 0), stop=(kc == KC - 1))
                mm.then_inc(v_mm, 1)

            def queries(l, g):
                pe.wait_ge(xT_done, GROUPS * (2 * l - 1) + g + 1)
                if l == 1 and g + 1 < GROUPS:
                    transposes(2 * l, g + 1)
                at = q_bank(l, g)
                if at == 4:
                    pe.wait_ge(v_done, GROUPS * l)
                if g:
                    same = [n for n in range(g) if q_bank(l, n) == at]
                    if same:
                        pe.wait_ge(qlo_done, GROUPS * l + same[-1] + 1)
                for oc in range(KC):
                    for kc in range(KC):
                        mm = pe.matmul(PS[:, at + oc, :], wproj[:, 0, kc, oc * P:(oc + 1) * P],
                                       xnT[:, kc, ds(g * 512, 512)], start=(kc == 0), stop=(kc == KC - 1))
                mm.then_inc(q_mm, 1)

            def project(l):
                if l == 0:
                    for g in range(GROUPS):
                        transposes(0, g)
                    pe.wait_ge(consts, 4)
                    return
                if l == 1:
                    for g in range(GROUPS):
                        if g == GROUPS - 1:
                            transposes(2, 0)
                        keys_values(l, g)
                    for g in range(GROUPS):
                        queries(l, g)
                else:
                    keys_values(l, 0)
                    keys_values(l, 1)
                    for g in range(GROUPS):
                        if g + 2 < GROUPS:
                            keys_values(l, g + 2)
                        transposes(2 * l, g)
                        queries(l, g)

            def attend(l, i):
                s0 = STEPS * l + 2 * PAIRS * i
                j0 = QUADS * l + PAIRS * i
                peeled = isinstance(i, int)
                for k in range(2 * PAIRS):
                    for stage, lag in ((select, 0), (scores_nat, 1), (max_rows, 2), (scores_key, 3), (times_v, 4),
                                       (back, 5)):
                        n = k - lag
                        if n >= 0 or not peeled:
                            stage(l, s0 + n, n % (2 * PAIRS), 2 * i + n // PAIRS, j0 + n // 2)

            def select(l, s, k, b, j):
                c = k % PAIRS
                oc, v = c // 4, c % 4
                if not (isinstance(s, int) and s == 0):
                    pe.wait_ge(sel_done, s)
                if isinstance(s, int) and s % STEPS == 0:
                    pe.wait_ge(qlo_done, GROUPS * (l + 1))
                    pe.wait_ge(klo_done, GROUPS * (l + 1))
                at = ds(b * S, S)
                pe.matmul(PS[:, 0, 0:256], sel[:, v, :], q_hi[:, oc, at], start=True, stop=False)
                pe.matmul(PS[:, 0, 0:256], sel[:, 4 + v, :], q_lo[:, oc, at], start=False, stop=True)
                pe.matmul(PS[:, 0, 256:512], sel[:, 8 + v, :], k_hi[:, oc, at], start=True, stop=False)
                pe.matmul(PS[:, 0, 256:512], sel[:, 12 + v, :], k_lo[:, oc, at], start=False, stop=True
                          ).then_inc(sel_mm, 1)

            def scores_nat(l, s, k, b, j):
                pe.wait_ge(sel_done, s + 1)
                if l == 0 and k % PAIRS == 0:
                    pe.wait_ge(mask_done, b + 1)
                if not (isinstance(s, int) and s == 0):
                    pe.wait_ge(max_done, 2 * s)
                for qt in range(2):
                    for h in range(2):
                        rows = slice(64 * h, 64 * h + STACK)
                        mm = pe.matmul(PS[:, 1 + h, qt * S:(qt + 1) * S], qk[rows, k % 4, qt * P:(qt + 1) * P],
                                       qk[rows, k % 4, 256:512], start=(l > 0 or qt == 0), stop=(l > 0),
                                       skip_group_check=(l == 0))
                        if l and qt:
                            mm.then_inc(nat_mm, 1)
                if l == 0:
                    for h in range(2):
                        pe.matmul(PS[:, 1 + h, :], bar[:], mask_b[:, (k // PAIRS) % 2, 0], start=False,
                                  stop=True, skip_group_check=True).then_inc(nat_mm, 1)

            def max_rows(l, s, k, b, j):
                pe.wait_ge(max_done, 2 * s + 2)
                if not (isinstance(s, int) and s == 0):
                    pe.wait_ge(maxT_done, s)
                for qt in range(2):
                    mm = pe.transpose(PS[:, 6, qt * P:(qt + 1) * P], nm[:, k % 2, qt, :], ident[:])
                mm.then_inc(maxT_mm, 1)

            def scores_key(l, s, k, b, j):
                pe.wait_ge(maxT_done, s + 1)
                if not (isinstance(s, int) and s == 0):
                    pe.wait_ge(exp_done, 2 * s)
                for kt in range(2):
                    for h in range(2):
                        rows = slice(64 * h, 64 * h + STACK)
                        mm = pe.matmul(PS[:, 3 + h, kt * S:(kt + 1) * S], qk[rows, k % 4, 256 + kt * P:256 + (kt + 1) * P],
                                       qk[rows, k % 4, 0:256], start=(l > 0 or kt == 0), stop=(l > 0),
                                       skip_group_check=(l == 0))
                        if l and kt:
                            mm.then_inc(sc_mm, 1)
                if l == 0:
                    for h in range(2):
                        pe.matmul(PS[:, 3 + h, :], bar[:], mask_b[:, (k // PAIRS) % 2, 1], start=False,
                                  stop=True, skip_group_check=True).then_inc(sc_mm, 1)

            def times_v(l, s, k, b, j):
                pe.wait_ge(exp_done, 2 * s + 2)
                if k % PAIRS == 0:
                    pe.wait_ge(v_copied, B * l + b + 1)
                    if isinstance(s, int) and s % STEPS == 0:
                        pe.wait_ge(padded, 3 * (l + 1) + 2)
                if k % 2 == 0 and not (isinstance(s, int) and s < 2):
                    pe.wait_ge(pv_done, j)
                for h in range(2):
                    strip = 32 * (2 * (k % 2) + h)
                    head = 2 * (k % PAIRS) + h
                    for kt in range(2):
                        mm = pe.matmul(PS[strip:strip + 32, 5, 0:256],
                                       vbuf[:, (k // PAIRS) % 2, kt, (DH + 1) * head:(DH + 1) * head + 32],
                                       probs[:, 2 * (k % 2) + h, kt * S:(kt + 1) * S],
                                       start=(kt == 0), stop=(kt == 1))
                mm.then_inc(pv_mm, 1)

            def back(l, s, k, b, j):
                if k % 2 == 0:
                    return
                pe.wait_ge(pv_done, j + 1)
                if not (isinstance(s, int) and s < 2):
                    pe.wait_ge(o_done, j)
                for qt in range(2):
                    mm = pe.transpose(PS[:, 7, qt * P:(qt + 1) * P], pvs[:, k // 2 % 2, qt * P:(qt + 1) * P],
                                      ident[:])
                mm.then_inc(oT_mm, 1)

            def out_transposes(l, b):
                b0, p = B * (l - 1) + b, b % 2
                pe.wait_ge(o_done, QUADS * l + QUADS // B * (b + 1))
                if b >= 2:
                    pe.wait_ge(oTr_done, b0 - 1)
                for kc in range(KC):
                    for qt in range(2):
                        mm = pe.transpose(PS[:, p, kc * 256 + qt * P:kc * 256 + (qt + 1) * P],
                                          onat[:, 2 * b + qt, kc * P:(kc + 1) * P], ident[:])
                mm.then_inc(oTr_mm, 1)

            def out_project(l, b):
                b0, p = B * (l - 1) + b, b % 2
                if b == 0:
                    pe.wait_ge(bo_v, 2 * l)
                pe.wait_ge(oTr_done, b0 + 1)
                if b >= 2:
                    pe.wait_ge(xo_done[l], b - 1)
                for qt in range(2):
                    o = PS[:, 2 + p, qt * D:(qt + 1) * D]
                    pe.matmul(o, ones_r[:], bo_s[:], start=True, stop=False)
                    for kc in range(KC):
                        mm = pe.matmul(o, oTs[:, p, kc * 256 + qt * P:kc * 256 + (qt + 1) * P], wproj[:, 3, kc, :],
                                       start=False, stop=(kc == KC - 1))
                mm.then_inc(wo_mm, 1)

            def router(l, g):
                if g == 0:
                    pe.wait_ge(wg_in, 16 * l)
                else:
                    pe.wait_ge(lg_done[l], g)
                    to_tokens(l, g - 1)
                for kc in range(KC):
                    mm = pe.matmul(PS[0:8, 7, :], wg[:, kc, :], xnT[:, kc, ds(g * 512, 512)],
                                   start=(kc == 0), stop=(kc == KC - 1))
                mm.then_inc(lg_mm[l], 1)

            def to_tokens(l, g):
                pe.wait_ge(lg_done[l], g + 1)
                if g == 3:
                    pe.wait_ge(route_v[l], 1)
                for t in range(4):
                    mm = pe.transpose(PS[:, 4 + g % 3, 8 * t:8 * t + 8], lgT[:, t * P:(t + 1) * P], ident[0:8, 0:8])
                mm.then_inc(lgn_mm[l], 1)

            w0 = lambda w: (w[:, 0:KC * NJ[0] * P].rearrange("p (c h) -> p c h", c=KC),
                            w[:, KC * NJ[0] * P:].rearrange("p (j d) -> p j d", d=D))

            def hidden(n, j):
                q = NJ[0] * n + j
                if j == 0:
                    pe.wait_ge(x0l_done, n + 1)
                if q >= 4:
                    pe.wait_ge(h_done[0], q - 3)
                (wh, _), (wl, _) = w0(w0h), w0(w0l)
                at, cut = slice(n * 512, (n + 1) * 512), slice(j * P, (j + 1) * P)
                o = PS[:, 4 + q % 4, :]
                for c in range(KC):
                    pe.matmul(o, wh[:, c, cut], x0h[:, c, at], start=(c == 0), stop=False)
                    pe.matmul(o, wh[:, c, cut], x0l[:, c, at], start=False, stop=False)
                    mm = pe.matmul(o, wl[:, c, cut], x0h[:, c, at], start=False, stop=(c == KC - 1))
                mm.then_inc(h_mm[0], 1)

            def outputs(n, j):
                nj, p = NJ[0], n % 2
                q = nj * n + j
                if q == 0:
                    pe.wait_ge(w0l_done, 2)
                    pe.wait_ge(prep, 2)
                    pe.wait_ge(x0l_done, GROUPS)
                pe.wait_ge(h0l_done, q + 1)
                if j == 0 and n >= 2:
                    pe.wait_ge(y_done[0], 4 * n - 4)
                (_, wh), (_, wl) = w0(w0h), w0(w0l)
                for t in range(4):
                    o = PS[:, 2 * p + t // 2, (t % 2) * D:(t % 2 + 1) * D]
                    at = slice(t * P, (t + 1) * P)
                    pe.matmul(o, h0h[:, q % 3, at], wh[:, j, :], start=(j == 0 and t % 2 == 0), stop=False,
                              skip_group_check=True)
                    pe.matmul(o, h0h[:, q % 3, at], wl[:, j, :], start=False, stop=False, skip_group_check=True)
                    if j == 0:
                        for r in range(2):
                            pe.matmul(o, ones_r[:], b2s[:, r, :], start=False, stop=False, skip_group_check=True)
                    mm = pe.matmul(o, h0l[:, q % 3, at], wh[:, j, :], start=False, stop=(j == nj - 1), skip_group_check=True)
                mm.then_inc(y_mm[0], 1)

            def feed():
                todo = [(n, j) for n in range(GROUPS) for j in range(NJ[0])]
                pe.wait_ge(w0l_done, 1)
                hidden(*todo[0])
                hidden(*todo[1])
                for at, (n, j) in enumerate(todo):
                    if at + 2 < len(todo):
                        hidden(*todo[at + 2])
                    outputs(n, j)

            def sparse(l):
                nj = NJ[l]
                nh = nj // 4
                n0, h0 = NT * (l - 1), NT * (NJ[1] // 4) * (l - 1)
                hi, lo = whi[:].rearrange("p s n -> p (s n)"), wlo[:].rearrange("p s n -> p (s n)")

                def ring(i):
                    return pe.value_load(table[0:1, 1, ds(i, 1)], min_val=0, max_val=RING)

                def a(i, p, turn):
                    if isinstance(i, int) and i < AHEAD:
                        if i < 2:
                            pe.wait_ge(xq_in[i], 16 * l)
                        else:
                            pe.wait_ge(xq_in[1 + i // 2], 32 * l)
                    else:
                        n = ((NT + 1) // 2 if p == 0 else NT // 2) - AHEAD // 2
                        pe.wait_ge(xg_in[p], 16 * (n * (l - 1) + turn - AHEAD // 2))
                    if not (isinstance(i, int) and n0 + i == 0):
                        pe.wait_ge(xl_done, n0 + i)
                    for c in range(KC):
                        mm = pe.transpose(PS[:, 0, c * P:(c + 1) * P], tile_in(i, p)[:, c * P:(c + 1) * P], ident[:])
                    mm.then_inc(xg_mm, 1)

                def b(i, q, off):
                    p = q % 2
                    pe.wait_ge(xl_done, n0 + i + 1)
                    pe.wait_ge(e_done, n0 + i + 1)
                    for h in range(nh):
                        if not (isinstance(i, int) and n0 + i == 0):
                            pe.wait_ge(gelu_done, h0 + nh * i - nh + h + 1 if not (isinstance(i, int) and i == 0) else h0)
                        pe.matmul(PS[:, 1 + h, :], of_e[:, q, :], b1s[:, h * 512:(h + 1) * 512], start=True, stop=False)
                        for c in range(KC):
                            w = ds(off + (c * nj * P + h * 512), 512)
                            pe.matmul(PS[:, 1 + h, :], xh[:, p, c, :], hi[:, w], start=False, stop=False)
                            pe.matmul(PS[:, 1 + h, :], xl[:, p, c, :], hi[:, w], start=False, stop=False)
                            mm = pe.matmul(PS[:, 1 + h, :], xh[:, p, c, :], lo[:, w], start=False, stop=(c == KC - 1))
                        mm.then_inc(hid_mm, 1)

                def d(i):
                    for h in range(nh):
                        pe.wait_ge(gelu_done, h0 + nh * i + h + 1)
                        if not (isinstance(i, int) and n0 + i == 0):
                            pe.wait_ge(hl_done, h0 + nh * i - nh + h + 1 if not (isinstance(i, int) and i == 0) else h0)
                        for t in range(4):
                            mm = pe.transpose(PS[:, 3 + h, t * P:(t + 1) * P], hn[:, (4 * h + t) * P:(4 * h + t + 1) * P],
                                              ident[:])
                        mm.then_inc(ht_mm, 1)

                def e(i, q, off):
                    pe.wait_ge(hl_done, h0 + nh * i + nh)
                    if not (isinstance(i, int) and n0 + i == 0):
                        pe.wait_ge(yo_done, n0 + i)
                    o = PS[:, 5, 0:D]
                    pe.matmul(o, of_e[:, q, :], b2t[:], start=True, stop=False)
                    for j in range(nj):
                        w = ds(off + (KC * nj * P + j * D), D)
                        pe.matmul(o, hh[:, j, :], hi[:, w], start=False, stop=False)
                        pe.matmul(o, hl[:, j, :], hi[:, w], start=False, stop=False)
                        mm = pe.matmul(o, hh[:, j, :], lo[:, w], start=False, stop=(j == nj - 1))
                    mm.then_inc(tiles_done, 1)

                pe.wait_ge(route_v[l], ROUTE + 3)
                every = picked[:].rearrange("p t e -> p (t e)")
                pe.matmul(PS[:, 7, P:2 * P], ones[:], every, start=True, stop=True).then_inc(tiles_done, 1)
                pe.matmul(PS[:, 7, 0:P], tri[:], every, start=True, stop=True).then_inc(pos_mm, 1)
                pe.wait_ge(hot_done, l)
                for j in range(2 * TILES):
                    mm = pe.matmul(PS[:, 6, 0:2 * AHEAD], in_row[:, j, :], ids[:, j, :], start=(j == 0), stop=(j == 2 * TILES - 1))
                mm.then_inc(idx_mm, 1)
                pe.wait_ge(tables, l)
                pe.wait_ge(bias_v, 4 * l)
                a(0, 0, 1)
                offs = {0: ring(0)}
                b(0, 0, offs[0])
                a(1, 1, 1)

                def turn(i):
                    d(i - 1)
                    if i < NT:
                        offs[i] = ring(i)
                        b(i, i % 4, offs[i])
                    if i + 1 < NT:
                        a(i + 1, (i + 1) % 2, (i + 1) // 2 + 1)
                    e(i - 1, (i - 1) % 4, offs[i - 1])
                for i in range(1, AHEAD - 1):
                    turn(i)
                n = (NT - AHEAD) // 4
                with pe.Fori(0, n) as k:
                    before = ring(4 * k + AHEAD - 2)
                    for q in range(4):
                        i = 4 * k + q + AHEAD - 1
                        d(i - 1)
                        off = ring(i)
                        b(i, (q + AHEAD - 1) % 4, off)
                        a(i + 1, q % 2, 2 * k + q // 2 + AHEAD // 2 + 1)
                        e(i - 1, (q + AHEAD - 2) % 4, before)
                        before = off
                offs[4 * n + AHEAD - 2] = ring(4 * n + AHEAD - 2)
                for i in range(4 * n + AHEAD - 1, NT + 1):
                    turn(i)

            def to_rows(bank, column):
                for t in range(4):
                    mm = pe.transpose(PS[:, bank, t * P:(t + 1) * P], column(t).broadcast_to([P, P]), ident[:])
                return mm

            def quantised():
                def chunk(g, *cs):
                    for c in cs if g < GROUPS else ():
                        q = NJ3 * g + c
                        if q >= 2:
                            pe.wait_ge(h_done[3], q - 1)
                        if c == 0:
                            pe.wait_ge(xT_done, GROUPS * 6 + g + 1)
                        for kc in range(KC):
                            mm = pe.matmul(PS[:, 4 + q % 2, :], w1q[:, kc, c * P:(c + 1) * P],
                                           nT[:, kc, g * 512:(g + 1) * 512], start=(kc == 0), stop=(kc == KC - 1))
                        mm.then_inc(h_mm[3], 1)

                def conv(g, *cs):
                    two = lambda ap: ap.rearrange("p (b t) -> p b t", b=2)
                    for c in cs if g < GROUPS else ():
                        j = CONV_PE.index(c)
                        m = len(CONV_PE) * g + j
                        pe.wait_ge(h_done[3], NJ3 * g + c + 1)
                        if m == 0:
                            pe.wait_ge(diag_done, 3 * len(CONV_PE))
                        if m >= 2:
                            last = CONV_PE[(m - 2) % len(CONV_PE)]
                            pe.wait_ge(silu_done, NJ3 * ((m - 2) // len(CONV_PE)) + SILU.index(last) + 1)
                        y, h = two(PS[:, 6 + m % 2, :]), two(hid[:, g % 2, c, :])
                        pe.matmul(y, diag(j, 1), h, start=True, stop=False)
                        pe.matmul(y[:, :, 1:S], diag(j, 0), h[:, :, 0:S - 1], start=False, stop=False)
                        pe.matmul(y[:, :, 0:S - 1], diag(j, 2), h[:, :, 1:S], start=False, stop=True).then_inc(cv_mm, 1)

                def output(g):
                    for h in range(2):
                        pe.wait_ge(n2_done, 2 * g + h + 1)
                        if g:
                            pe.wait_ge(y_done[3], 4 * g - 2 + 2 * h)
                        for t in (2 * h, 2 * h + 1):
                            for c in range(NJ3):
                                mm = pe.matmul(PS[:, h, (t % 2) * D:(t % 2 + 1) * D], n2[:, c, t * P:(t + 1) * P],
                                               w2q[:, c, :], start=(c == 0), stop=(c == NJ3 - 1))
                        mm.then_inc(y_mm[3], 1)

                pe.wait_ge(q3_v, 9)
                pe.wait_ge(bc_done, GROUPS)
                chunk(0, 0, 1)
                for g in range(-1, GROUPS):
                    chunk(g + 1, 2, 3)
                    conv(g + 1, 0)
                    if g >= 0:
                        pe.wait_ge(q3_p, Q3P * g + 1)
                        if g == 0:
                            pe.wait_ge(xT_done, GROUPS * 7)
                        for t in range(4):
                            mm = pe.transpose(PS[:, 2, t * P:(t + 1) * P], amx[:, t * P:(t + 1) * P], ident[:])
                        mm.then_inc(amx_mm, 1)
                    chunk(g + 1, 4, 5)
                    conv(g + 1, 2)
                    chunk(g + 1, 6, 7)
                    if g >= 0:
                        pe.wait_ge(q3_p, Q3P * g + 4)
                        to_rows(3, lambda t: q3g[:, g % 2, 2, t:t + 1]).then_inc(hrow_mm, 1)
                    conv(g + 1, 3)
                    if g >= 1:
                        output(g - 1)
                    conv(g + 1, 4, 5)
                    chunk(g + 2, 0, 1)
                output(GROUPS - 1)

            for l in lo_l:
                u = 2 * l
                project(l)
                attend(l, 0)
                with pe.Fori(1, B // 2) as i:
                    attend(l, i)
                for k in range(5):
                    for stage, lag in ((scores_nat, 1), (max_rows, 2), (scores_key, 3), (times_v, 4), (back, 5)):
                        n = k - lag
                        if n < 0:
                            stage(l, STEPS * (l + 1) + n, n % (2 * PAIRS), B + n // PAIRS, QUADS * (l + 1) + n // 2)
                if l:
                    out_transposes(l, 0)
                    for b in range(B):
                        if b + 1 < B:
                            out_transposes(l, b + 1)
                        if b == 0 and l == 3:
                            pe.wait_ge(o_done, QUADS * (l + 1))
                            pe.wait_ge(q3_v, 1)
                            pe.matmul(PS[:, 7, 0:2], ones[:], q3[:, 0:2], start=True, stop=True).then_inc(q3_mm, 1)
                        out_project(l, b)
                if not ffn(l):
                    continue
                u += 1
                if l:
                    pe.wait_ge(xo_done[l], B)

                if l == 3:
                    pe.wait_ge(q3_rows, 1)
                    for g in range(GROUPS):
                        to_rows(4 + g, lambda t: s1[:, 4 * g + t:4 * g + t + 1]).then_inc(row_mm, 1)
                transposes(u, 0)
                for g in range(GROUPS):
                    if g + 1 < GROUPS:
                        transposes(u, g + 1)
                    if l in (1, 2):
                        pe.wait_ge(xT_done, GROUPS * 2 * l + g + 1)
                        router(l, g)
                if l in (1, 2):
                    to_tokens(l, GROUPS - 1)
                if l == 0:
                    feed()
                elif l < 3:
                    sparse(l)
                else:
                    quantised()

        @block.scalar
        def _(act):
            act.wait_ge(const_in, 32)
            nc.scalar.activation(tg[:], cols[:, COLS["gate"][0]:COLS["gate"][0] + 8], ACT.Tanh).then_inc(gates, 1)

            def roots(u):
                act.wait_ge(ln_v[u], 2)
                nc.scalar.activation(sml[:, 1, :], sml[:, 0, :], ACT.Sqrt).then_inc(ln_a, 1)
                if u in RMS:
                    act.wait_ge(ln_v[u], RMS_AT)
                    nc.scalar.activation(sml[:, 7, :], sml[:, 6, :], ACT.Sqrt).then_inc(ln_a, 1)

            def group_roots(u, g):
                act.wait_ge(ln_v[u], 7 * g + 2)
                nc.scalar.activation(sml[:, 1, 4 * g:4 * g + 4], sml[:, 0, 4 * g:4 * g + 4], ACT.Sqrt).then_inc(ln_a, 1)

            def keys(l, g):
                at = ds(g * 512, 512)
                if l:
                    act.wait_ge(k_mm, GROUPS * (l - 1) + g + 1)
                else:
                    act.wait_ge(ctx_in[g], 16)
                for oc in range(KC):
                    ins = nc.scalar.activation(k_hi[:, oc, at], PS[:, 2 + oc, :] if l else ctx_at(g)[:, oc, :],
                                               ACT.Identity, bias=col(f"bk{l}", oc) if l in (1, 3) else 0.0)
                ins.then_inc(khi_done, 1)

            def features(l, g):
                at = ds(g * 512, 512)
                act.wait_ge(xT_mm, GROUPS * 2 * l + g + 1)
                for c in range(KC):
                    ins = nc.scalar.activation((xnT if l else q_hi)[:, c, at], PS[:, xT_bank(2 * l, g) + c, :], ACT.Identity)
                ins.then_inc(xT_done if l else qhi_done, 1)

            def queries(l, g):
                act.wait_ge(q_mm, GROUPS * (l - 1) + g + 1)
                for oc in range(KC):
                    ins = nc.scalar.activation(q_hi[:, oc, ds(g * 512, 512)], PS[:, q_bank(l, g) + oc, :], ACT.Identity,
                                               bias=col(f"bq{l}", oc) if l != 2 else 0.0)
                ins.then_inc(qhi_done, 1)

            def project(l):
                if l == 0:
                    group_roots(0, 0)
                    keys(0, 0)
                    for g in range(GROUPS):
                        if g + 1 < GROUPS:
                            group_roots(0, g + 1)
                            keys(0, g + 1)
                        features(0, g)
                    return
                if l == 1:
                    roots(2)
                    for g in range(GROUPS):
                        keys(l, g)
                    features(l, 0)
                    for g in range(GROUPS):
                        if g + 1 < GROUPS:
                            features(l, g + 1)
                        queries(l, g)
                else:
                    keys(l, 0)
                    for g in range(GROUPS + 1):
                        if g < GROUPS:
                            group_roots(2 * l, g)
                            if g + 1 < GROUPS:
                                keys(l, g + 1)
                        if g:
                            features(l, g - 1)
                            queries(l, g - 1)

            def take_stack(l, s, k):
                act.wait_ge(sel_mm, s + 1)
                if not (isinstance(s, int) and s < 4):
                    act.wait_ge(sc_mm, 2 * s - 6)
                nc.scalar.activation(qk[:, k % 4, :], PS[:, 0, :], ACT.Identity, bias=col("max_row")).then_inc(sel_done, 1)

            def exps(l, s, k):
                for h in range(2):
                    act.wait_ge(sc_mm, 2 * s + h + 1)
                    if h == 0 and not (isinstance(s, int) and s < 2):
                        act.wait_ge(pv_mm, s - 1)
                    nc.scalar.activation(probs[:, 2 * (k % 2) + h, :], PS[:, 3 + h, :], ACT.Exp, scale=SCALE
                                         ).then_inc(exp_done, 1)

            def attend(l, i):
                for k in range(2 * PAIRS):
                    take_stack(l, STEPS * l + 2 * PAIRS * i + k, k)
                    n = k - 3
                    if n >= 0 or not isinstance(i, int):
                        exps(l, STEPS * l + 2 * PAIRS * i + n, n % (2 * PAIRS))

            def take_oT(l, b):
                b0 = B * (l - 1) + b
                act.wait_ge(oTr_mm, b0 + 1)
                if b >= 2:
                    act.wait_ge(wo_mm, b0 - 1)
                nc.scalar.activation(oTs[:, b % 2, :], PS[:, b % 2, :], ACT.Identity).then_inc(oTr_done, 1)

            def norm(l, g):
                u = 2 * l + 1
                at = ds(g * 512, 512)
                act.wait_ge(xT_mm, GROUPS * u + g + 1)
                for c in range(KC):
                    ins = nc.scalar.activation((x0h if l == 0 else nT if l == 3 else xnT)[:, c, at],
                                               PS[:, xT_bank(u, g) + c, :], ACT.Identity,
                                               scale=col("norm_w", c) if l == 2 else 1.0)
                ins.then_inc(xT_done, 1)

            def logits(l, g):
                act.wait_ge(lg_mm[l], g + 1)
                if g:
                    act.wait_ge(lgn_mm[l], g)
                nc.scalar.activation(lgT[:], PS[0:8, 7, :], ACT.Identity).then_inc(lg_done[l], 1)

            def feed():
                nj = NJ[0]
                for q in range(GROUPS * nj):
                    act.wait_ge(h_mm[0], q + 1)
                    if q >= 2:
                        act.wait_ge(h0l_done, q - 1)
                    nc.scalar.activation(h0f[:, q % 2, :], PS[:, 4 + q % 4, :], ACT.Gelu, bias=col("b1_0", q % nj)
                                         ).then_inc(h_done[0], 1)
                    act.wait_ge(h_done[0], q + 1)
                    if q >= 3:
                        act.wait_ge(y_mm[0], q - 2)
                    nc.scalar.activation(h0h[:, q % 3, :], h0f[:, q % 2, :], ACT.Identity).then_inc(h0h_done, 1)

            def sparse(l):
                nh = NJ[l] // 4
                n0, h0 = NT * (l - 1), NT * (NJ[1] // 4) * (l - 1)

                def a(i, p):
                    act.wait_ge(xg_mm, n0 + i + 1)
                    if l == 1:
                        nc.scalar.activation(xh[:, p].rearrange("p c t -> p (c t)"), PS[:, 0, 0:D], ACT.Identity
                                             ).then_inc(xh_done, 1)
                    else:
                        for c in range(KC):
                            ins = nc.scalar.activation(xh[:, p, c], PS[:, 0, c * P:(c + 1) * P], ACT.Identity,
                                                       scale=col("norm_w", c))
                        ins.then_inc(xh_done, 1)

                def b(i):
                    for h in range(nh):
                        act.wait_ge(hid_mm, h0 + nh * i + h + 1)
                        nc.scalar.activation(hn[:, h * 512:(h + 1) * 512], PS[:, 1 + h, :], ACT.Gelu).then_inc(gelu_done, 1)

                def d(i):
                    for h in range(nh):
                        act.wait_ge(ht_mm, h0 + nh * i + h + 1)
                        nc.scalar.activation(hh[:, 4 * h:4 * h + 4, :].rearrange("p j t -> p (j t)"), PS[:, 3 + h, :],
                                             ACT.Identity).then_inc(hh_done, 1)
                a(0, 0)
                b(0)
                a(1, 1)

                def turn(i):
                    d(i - 1)
                    if i < NT:
                        b(i)
                    if i + 1 < NT:
                        a(i + 1, (i + 1) % 2)
                turn(1)
                turn(2)
                with act.Fori(0, (NT - 5) // 2) as k:
                    for q in range(2):
                        i = 2 * k + q + 3
                        d(i - 1)
                        b(i)
                        a(i + 1, q)
                for i in range(NT - 2, NT + 1):
                    turn(i)

            def quantised():
                def middle(g, c):
                    act.wait_ge(h_done[3], NJ3 * g + c + 1)
                    nc.scalar.activation(act3[:, g % 2, c, :], hid[:, g % 2, c, :], ACT.Identity,
                                         scale=col("conv_w", NJ3 + c), bias=col("conv_b", c)).then_inc(tap_done, 1)

                def silu(g, *cs):
                    for c in cs:
                        a = act3[:, g % 2, c, :]
                        if c in CONV_PE:
                            m = len(CONV_PE) * g + CONV_PE.index(c)
                            act.wait_ge(cv_mm, m + 1)
                            nc.scalar.activation(a, PS[:, 6 + m % 2, :], ACT.Silu, bias=col("conv_b", c)).then_inc(silu_done, 1)
                        else:
                            act.wait_ge(cv_done, len(CONV_DVE) * g + CONV_DVE.index(c) + 1)
                            nc.scalar.activation(a, a, ACT.Silu).then_inc(silu_done, 1)

                def integers(g):
                    for h in range(2):
                        act.wait_ge(q3_p, Q3P * g + 8 + h)
                        if g:
                            act.wait_ge(y_mm[3], 2 * g - 1 + h)
                        at = slice(h * 256, (h + 1) * 256)
                        nc.scalar.activation(n2[:, :, at], act3[:, g % 2, :, at], ACT.Identity, bias=-MAGIC).then_inc(n2_done, 1)
                for g in range(GROUPS + 1):
                    if g < GROUPS:
                        silu(g, 0)
                        middle(g, 1)
                        silu(g, 2, 1)
                        middle(g, 6)
                        middle(g, 7)
                        silu(g, 3)
                    if g:
                        integers(g - 1)
                    if g < GROUPS:
                        silu(g, 4, 5, 6, 7)

            for l in lo_l:
                project(l)
                attend(l, 0)
                with act.Fori(1, B // 2) as i:
                    attend(l, i)
                for n in range(-3, 0):
                    exps(l, STEPS * (l + 1) + n, n % (2 * PAIRS))
                if l:
                    for b in range(B):
                        take_oT(l, b)
                if not ffn(l):
                    continue
                u = 2 * l + 1

                if l == 0:
                    act.wait_ge(w0_scaled, 4)
                    act.wait_ge(w0_in, 32)
                    act.wait_ge(o_done, QUADS)
                    for w in range(2):
                        at = slice(w * W0 // 2, (w + 1) * W0 // 2)
                        nc.scalar.activation(w0h[:, at], wslots[:, at], ACT.Identity).then_inc(w0h_done, 1)
                        if w == 0:
                            roots(u)
                else:
                    roots(u)
                if l == 3:
                    for g in range(GROUPS):
                        act.wait_ge(row_mm, g + 1)
                        nc.scalar.activation(bcast[:, g, :], PS[:, 4 + g, :], ACT.Identity).then_inc(bc_done, 1)
                norm(l, 0)
                for g in range(GROUPS):
                    if g + 1 < GROUPS:
                        norm(l, g + 1)
                    if l in (1, 2):
                        logits(l, g)
                if l == 0:
                    feed()
                elif l < 3:
                    act.wait_ge(route_v[l], ROUTE)
                    nc.scalar.activation(gt[:, 3, :], gt[:, 2, :], ACT.Exp).then_inc(route_e[l], 1)
                    sparse(l)
                else:
                    quantised()

        @block.vector
        def _(dve):
            nc.vector.memset(nm[:], 0.0).then_inc(consts, 1)
            nc.vector.memset(ones[:], 1.0)
            nc.vector.memset(ones_r[:].bitcast(F32), 1.0).then_inc(consts, 1)

            def stats(u, t):
                nc.vector.bn_stats(st6[:, t, :], x_res[:, t, :]).then_inc(ln_s, 1)

            def roots_before(u):
                return u + sum(w < u for w in RMS) + (GROUPS - 1) * sum(w < u for w in BY_GROUP)

            def group_variances(u, g):
                dve.wait_ge(ln_s, TILES * u + 4 * g + 4)
                for t in range(4 * g, 4 * g + 4):
                    ins = nc.vector.bn_aggr(mv[:, t, :], st6[:, t, :])
                ins.then_inc(ln_v[u], 1)
                dve.wait_ge(ln_v[u], 7 * g + 1)
                nc.vector.tensor_scalar(sml[:, 0, 4 * g:4 * g + 4], mv[:, 4 * g:4 * g + 4, 1], LN_EPS, None, ALU.add
                                        ).then_inc(ln_v[u], 1)

            def group_scales(u, g):
                q = lambda n: sml[:, n, 4 * g:4 * g + 4]
                k = 7 * g + 2

                def then(ins):
                    nonlocal k
                    k += 1
                    ins.then_inc(ln_v[u], 1)
                    dve.wait_ge(ln_v[u], k)
                dve.wait_ge(ln_a, roots_before(u) + g + 1)
                then(nc.vector.reciprocal(q(2), q(1)))
                then(nc.vector.tensor_tensor(q(3), q(2), q(2), ALU.mult))
                then(nc.vector.tensor_tensor(q(4), q(3), q(0), ALU.mult))
                then(nc.vector.tensor_scalar(q(5), q(4), -0.5, 1.5, ALU.mult, ALU.add))
                then(nc.vector.tensor_tensor(q(8), q(2), q(5), ALU.mult))

            def scales(l, u):
                q = lambda n: sml[:, n, :]
                k = 0

                def then(ins):
                    nonlocal k
                    k += 1
                    ins.then_inc(ln_v[u], 1)
                    dve.wait_ge(ln_v[u], k)

                def rsqrt(v, root, r):
                    then(nc.vector.reciprocal(q(2), q(root)))
                    then(nc.vector.tensor_tensor(q(3), q(2), q(2), ALU.mult))
                    then(nc.vector.tensor_tensor(q(4), q(3), q(v), ALU.mult))
                    then(nc.vector.tensor_scalar(q(5), q(4), -0.5, 1.5, ALU.mult, ALU.add))
                    then(nc.vector.tensor_tensor(q(r), q(2), q(5), ALU.mult))
                roots = roots_before(u)
                dve.wait_ge(ln_s, TILES * (u + 1))
                for t in range(TILES):
                    ins = nc.vector.bn_aggr(mv[:, t, :], st6[:, t, :])
                then(ins)
                var = mv[:, :, 1]
                then(nc.vector.tensor_scalar(q(0), var, LN_EPS, None, ALU.add))
                dve.wait_ge(ln_a, roots + 1)
                rsqrt(0, 1, 8)
                if u in RMS:
                    then(nc.vector.tensor_tensor(q(9), q(8), q(8), ALU.mult))
                    then(nc.vector.tensor_tensor(q(10), q(9), var, ALU.mult))
                    if l == 0:
                        then(nc.vector.tensor_scalar(q(6), q(10), float(D), 1e-24, ALU.mult, ALU.max))
                    else:
                        then(nc.vector.tensor_scalar(q(6), q(10), RMS_EPS, None, ALU.add))
                    assert k == RMS_AT
                    dve.wait_ge(ln_a, roots + 2)
                    rsqrt(6, 7, 11)
                    if l == 0:
                        then(nc.vector.scalar_tensor_tensor(q(9), q(8), float(D) ** 0.5, q(11), ALU.mult, ALU.mult))

            def normed(u, g):
                xn = xn_slot(u, g)
                for t in range(4):
                    at = 4 * g + t
                    ins = nc.vector.tensor_scalar(xn[:, t, :], x_res[:, at, :], mv[:, at, 0:1],
                                                  sml[:, 9 if u == 1 else 8, at:at + 1], ALU.subtract, ALU.mult)
                return xn, ins

            def layernorm(l, u, g):
                if u % 2 == 0 and g >= 2:
                    dve.wait_ge(xT_mm, GROUPS * u + g - 1)
                xn, ins = normed(u, g)
                if u == 5:
                    ins.then_inc(ln_x, 1)
                    dve.wait_ge(ln_x, 2 * g + 1)
                    x = x_res[:, 4 * g:4 * g + 4, :].rearrange("p t d -> p (t d)")
                    nc.vector.scalar_tensor_tensor(x, xn.rearrange("p t d -> p (t d)"), tg[:, 4 + l:5 + l], x,
                                                   ALU.mult, ALU.add).then_inc(ln_x, 1)
                    dve.wait_ge(ln_x, 2 * g + 2)
                    for t in range(4):
                        ins = nc.vector.tensor_scalar(xn[:, t, :], xn[:, t, :], sml[:, 11, 4 * g + t:4 * g + t + 1], None,
                                                      ALU.mult)
                ins.then_inc(xn_ready, 1)

            def layernorm_quantised(u):
                q = lambda n: sml[:, n, :]
                k = 2 * GROUPS

                def then(ins):
                    nonlocal k
                    k += 1
                    ins.then_inc(ln_x, 1)
                    dve.wait_ge(ln_x, k)
                xns = []
                for g in range(GROUPS):
                    xn, ins = normed(u, g)
                    xns.append(xn)
                then(ins)
                for g in range(GROUPS):
                    ins = nc.vector.tensor_reduce(sml[:, 6, 4 * g:4 * g + 4], xns[g], AX.X, ALU.max,
                                                  apply_absolute_value=True)
                then(ins)
                then(nc.vector.tensor_scalar(q(7), q(6), 1e-5, 1.0 / 127.0, ALU.max, ALU.mult))
                then(nc.vector.reciprocal(q(9), q(7)))
                nc.vector.tensor_scalar(s1[:], q(7), q3[:, 2:3], None, ALU.mult).then_inc(q3_rows, 1)
                for g in range(GROUPS):
                    xn = xns[g]
                    for t in range(4):
                        ins = nc.vector.tensor_scalar(xn[:, t, :], xn[:, t, :], sml[:, 9, 4 * g + t:4 * g + t + 1], MAGIC,
                                                      ALU.mult, ALU.add)
                    then(ins)
                    nc.vector.tensor_scalar(xn, xn, MAGIC + 127.0, -MAGIC, ALU.min, ALU.add).then_inc(xn_ready, 1)

            def keys_values(l, g):
                at = ds(g * 512, 512)
                dve.wait_ge(khi_done, GROUPS * l + g + 1)
                for oc in range(KC):
                    ins = nc.vector.scalar_tensor_tensor(
                        k_lo[:, oc, at], PS[:, 2 + oc, :], col(f"bk{l}", oc) if l != 2 else 0.0,
                        k_hi[:, oc, at].bitcast(F32), ALU.add, ALU.subtract)
                ins.then_inc(klo_done, 1)
                dve.wait_ge(v_mm, GROUPS * (l - 1) + g + 1)
                for t in range(2):
                    v = vall[:, 4 * g + 2 * t:4 * g + 2 * t + 2, :]
                    ps = PS[:, 4 + t, :].rearrange("p (t d) -> p t d", d=D)
                    if l == 2:
                        ins = nc.vector.tensor_copy(v, ps)
                    else:
                        ins = nc.vector.tensor_tensor(v, ps, bvb[:].unsqueeze(1).broadcast_to([P, 2, D]), ALU.add)
                ins.then_inc(v_done, 1)

            def queries(l, g):
                at = ds(g * 512, 512)
                dve.wait_ge(qhi_done, GROUPS * l + g + 1)
                if l == 0:
                    nc.vector.tensor_tensor(q_lo[:, :, at], PS[:, 2 * g:2 * g + 2, :], q_hi[:, :, at].bitcast(F32), ALU.subtract
                                            ).then_inc(qlo_done, 1)
                    return
                for oc in range(KC):
                    ins = nc.vector.scalar_tensor_tensor(
                        q_lo[:, oc, at], PS[:, q_bank(l, g) + oc, :], col(f"bq{l}", oc) if l != 2 else 0.0,
                        q_hi[:, oc, at].bitcast(F32), ALU.add, ALU.subtract)
                ins.then_inc(qlo_done, 1)

            def project(l):
                if l == 0:
                    for g in range(GROUPS + 2):
                        if g < GROUPS:
                            dve.wait_ge(x_in[g], 16)
                            for t in range(4 * g, 4 * g + 4):
                                stats(0, t)
                        if 1 <= g <= GROUPS:
                            group_scales(0, g - 1)
                            layernorm(0, 0, g - 1)
                        if g < GROUPS:
                            group_variances(0, g)
                        if g == GROUPS + 1:
                            dve.wait_ge(const_in, 32)
                            nc.vector.tensor_scalar(bar[:], ident[:], MASKED, None, ALU.mult).then_inc(consts, 1)
                            dve.wait_ge(sel_in, 16)
                            nc.vector.tensor_copy(sel[:].rearrange("p a b -> p (a b)"), sel_f).then_inc(consts, 1)
                        if g >= 2:
                            queries(0, g - 2)
                    dve.wait_ge(consts, 4)
                    dve.wait_ge(gates, 1)
                    dve.wait_ge(later_in, 32)
                elif l == 1:
                    scales(l, 2 * l)
                    layernorm(l, 2 * l, 0)
                    layernorm(l, 2 * l, 1)
                    for g in range(GROUPS):
                        keys_values(l, g)
                    for g in range(GROUPS):
                        if g + 2 < GROUPS:
                            layernorm(l, 2 * l, g + 2)
                        queries(l, g)

            def maxima(l, s, k):
                for h in range(2):
                    dve.wait_ge(nat_mm, 2 * s + h + 1)
                    if h == 0 and not (isinstance(s, int) and s < 2):
                        dve.wait_ge(maxT_mm, s - 1)
                    at = MAXROW + 64 * h
                    nc.vector.tensor_reduce(nm[:, k % 2, :, at:at + 1], PS[:, 1 + h, :].rearrange("p (q n) -> p q n", q=2),
                                            AX.X, ALU.max, negate=True).then_inc(max_done, 1)

            def take_maxT(l, s, k):
                dve.wait_ge(maxT_mm, s + 1)
                q = qk[:, k % 4, 0:256]
                nc.vector.tensor_tensor(q, PS[:, 6, 0:256], q.bitcast(F32), ALU.add).then_inc(maxT_done, 1)

            def take_pv(l, s, k, j):
                dve.wait_ge(pv_mm, s + 1)
                if not (isinstance(s, int) and s < 4):
                    dve.wait_ge(oT_mm, j - 1)
                nc.vector.tensor_copy(pvs[:, k // 2 % 2, :], PS[:, 5, 0:256]).then_inc(pv_done, 1)

            def divide(l, s, k, b, j):
                dve.wait_ge(oT_mm, j + 1)
                m = k // 2 % 2
                o = PS[:, 7, 0:256].rearrange("p (q h d) -> p q h d", q=2, h=4)
                nc.vector.reciprocal(rc[:, m], o[:, :, :, DH]).then_inc(rc_done, 1)
                dve.wait_ge(rc_done, j + 1)
                at = 64 * (k % PAIRS // 2)
                nc.vector.tensor_tensor(
                    onat[:, ds(2 * b, 2), at:at + 64].rearrange("p q (h d) -> p q h d", d=DH), o[:, :, :, 0:DH],
                    rc[:, m].unsqueeze(3).broadcast_to([P, 2, 4, DH]), ALU.mult).then_inc(o_done, 1)

            def make_mask(i, p):
                dve.wait_ge(mask_in[p], 32 * (i + 1))
                if not isinstance(i, int):
                    dve.wait_ge(sc_mm, 2 * PAIRS * (2 * i + p - 1))
                nc.vector.tensor_scalar(mask_b[:, p], stage_i[:, p], 0.0, None, ALU.is_equal).then_inc(mask_done, 1)

            def attend_turn(l, i, k, last=False):
                s0 = STEPS * (l + 1) if last else STEPS * l + 2 * PAIRS * i
                if l == 0 and not last and k in (0, 5):
                    make_mask(i, k // 5)
                for lag, stage in ((1, "max"), (2, "maxT"), (4, "pv"), (5, "divide")):
                    n = k - lag
                    if n < 0 and isinstance(i, int) and not last or last and n >= 0:
                        continue
                    m = n % (2 * PAIRS)
                    b = (B if last else 2 * i) + n // PAIRS
                    j = (QUADS * (l + 1) if last else QUADS * l + PAIRS * i) + n // 2
                    if stage == "max":
                        maxima(l, s0 + n, m)
                    elif stage == "maxT":
                        take_maxT(l, s0 + n, m)
                    elif stage == "pv" and n % 2:
                        take_pv(l, s0 + n, m, j)
                    elif stage == "divide" and n % 2:
                        divide(l, s0 + n, m, b, j)
                if l == 0 and not last:
                    if k in (5, 6) and not (isinstance(i, int) and i == 0):
                        (add_out0 if k == 5 else stats_out0)(2 * i - 1)
                    if k in (13, 14):
                        (add_out0 if k == 13 else stats_out0)(2 * i)

            def add_out(l, more):
                for b in range(B):
                    dve.wait_ge(wo_mm, B * (l - 1) + b + 1)
                    x = x_res[:, 2 * b:2 * b + 2, :].rearrange("p t d -> p (t d)")
                    nc.vector.scalar_tensor_tensor(x, PS[:, 2 + b % 2, :], tg[:, l:l + 1], x, ALU.mult, ALU.add
                                                   ).then_inc(xo_done[l], 1)
                    for step in more[2 * b:2 * b + 2]:
                        step()
                    if b:
                        dve.wait_ge(xo_done[l], b)
                        for t in range(2):
                            stats(2 * l + 1, 2 * b - 2 + t)
                dve.wait_ge(xo_done[l], B)
                for t in range(2):
                    stats(2 * l + 1, 2 * B - 2 + t)

            def split_bo(l):
                dve.wait_ge(wproj_in[l], 32 if l == 2 else 48)
                head = yo[0:2, 0, :]
                nc.vector.tensor_copy(head.bitcast(F32R), bo_f[:]).then_inc(bo_v, 1)
                dve.wait_ge(bo_v, 2 * l - 1)
                nc.vector.scalar_tensor_tensor(bo_s[:], head, col("low", 0, 2), bo_f[:], ALU.mult, ALU.add
                                               ).then_inc(bo_v, 1)

            def ternary():
                w1f, w2f = wslot[:, 0, 0:2048], wslot[:, 1, 0:2048]
                flat = lambda w: w.rearrange("p c h -> p (c h)")
                ts = nc.vector.tensor_scalar
                steps = [
                    lambda: nc.vector.tensor_scalar(q3[:, 2:4], PS[:, 7, 0:2], 1.0 / (H3 * D), 1e-5, ALU.mult, ALU.max),
                    lambda: nc.vector.reciprocal(q3[:, 4:6], q3[:, 2:4]),
                    lambda: ts(w1f, w1f, q3[:, 4:5], MAGIC, ALU.mult, ALU.add),
                    lambda: ts(w2f, w2f, q3[:, 5:6], MAGIC, ALU.mult, ALU.add),
                    lambda: ts(w1f, w1f, -MAGIC, 1.0, ALU.add, ALU.min),
                    lambda: ts(w2f, w2f, -MAGIC, 1.0, ALU.add, ALU.min),
                    lambda: ts(flat(w1q), w1f, -1.0, None, ALU.max),
                    lambda: ts(flat(w2q), w2f, -1.0, None, ALU.max),
                    lambda: ts(q3[:, 6:7], q3[:, 3:4], tg[:, 7:8], None, ALU.mult),
                ]

                def run(n):
                    if n == 0:
                        dve.wait_ge(q3_mm, 1)
                    else:
                        dve.wait_ge(q3_v, n + 1)
                    steps[n]().then_inc(q3_v, 1)
                return [lambda n=n: run(n) for n in range(len(steps))]

            def ternary_sums():
                dve.wait_ge(w3_in, 32)
                nc.vector.tensor_reduce(q3[:, 0:1], wslot[:, 0, 0:2048], AX.X, ALU.add, apply_absolute_value=True)
                nc.vector.tensor_reduce(q3[:, 1:2], wslot[:, 1, 0:2048], AX.X, ALU.add, apply_absolute_value=True
                                        ).then_inc(q3_v, 1)

            def add_out0(b):
                dve.wait_ge(o_done, QUADS // B * b + QUADS // B)
                x = x_res[:, ds(2 * b, 2), :].rearrange("p t d -> p (t d)")
                nc.vector.scalar_tensor_tensor(x, wide[:, ds(2 * D * b, 2 * D)], tg[:, 0:1], x, ALU.mult, ALU.add
                                               ).then_inc(xo_done[0], 1)

            def stats_out0(b):
                dve.wait_ge(xo_done[0], b + 1)
                for t in range(2):
                    nc.vector.bn_stats(st6[:, ds(2 * b + t, 1), :].rearrange("p t n -> p (t n)"),
                                       x_res[:, ds(2 * b + t, 1), :].rearrange("p t d -> p (t d)")).then_inc(ln_s, 1)

            def route(l):
                k = 0

                def then(ins):
                    nonlocal k
                    k = k + 1
                    ins.then_inc(route_v[l], 1)
                    dve.wait_ge(route_v[l], k)
                for g in range(GROUPS):
                    dve.wait_ge(lgn_mm[l], g + 1)
                    ts = range(4 * g, 4 * g + 4)
                    then(nc.vector.tensor_copy(lgs[:, 4 * g:4 * g + 4].rearrange("p t e -> p (t e)"), PS[:, 4 + g % 3, 0:32]))
                    for t in ts:
                        ins = nc.vector.max(mx8[:, t, :], lgs[:, t, :])
                    then(ins)
                    for t in ts:
                        ins = nc.vector.max_index(ix8[:, t, :], mx8[:, t, :], lgs[:, t, :])
                    then(ins)
                then(nc.vector.tensor_copy(gt[:, 0:2, :], ix8[:, :, 0:2].rearrange("p t k -> p k t")))
                then(nc.vector.tensor_tensor(gt[:, 2, :], mx8[:, :, 1], mx8[:, :, 0], ALU.subtract))
                assert k == ROUTE

            def plan(l):
                k = ROUTE

                def then(ins):
                    nonlocal k
                    k += 1
                    ins.then_inc(route_v[l], 1)
                    dve.wait_ge(route_v[l], k)
                tt, ts = nc.vector.tensor_tensor, nc.vector.tensor_scalar
                for m in range(2):
                    nc.vector.tensor_tensor(eq[:, m], iotas[:, 0:8].unsqueeze(1).broadcast_to([P, TILES, 8]),
                                            gt[:, m, :].unsqueeze(2).broadcast_to([P, TILES, 8]), ALU.is_equal
                                            ).then_inc(route_v[l], 1)
                k += 2
                dve.wait_ge(route_v[l], k)
                then(tt(picked[:], eq[:, 0], eq[:, 1], ALU.add))
                assert k == ROUTE + 3
                dve.wait_ge(pos_mm, l)
                then(nc.vector.tensor_copy(scan[:, 0].rearrange("p t e -> p (t e)"), PS[:, 7, P:2 * P]))
                at = 0
                for step in (1, 2, 4, 8):
                    nc.vector.tensor_copy(scan[:, 1 - at, 0:step], scan[:, at, 0:step])
                    then(tt(scan[:, 1 - at, step:], scan[:, at, step:], scan[:, at, 0:TILES - step], ALU.add))
                    at = 1 - at
                total = scan[:, at, TILES - 1, :]
                then(ts(escan[:, 2, :], total, 1.0 / P, 63.5 / P, ALU.mult, ALU.add))
                then(ts(escan[:, 1, :], escan[:, 2, :], 1.0, MAGIC, ALU.max, ALU.add))
                ts(escan[:, 3, :], escan[:, 1, :], -MAGIC, None, ALU.add)
                then(ts(escan[:, 0, :], escan[:, 1, :], -MAGIC, None, ALU.add))
                es = 0
                for step in (1, 2, 4):
                    nc.vector.tensor_copy(escan[:, 1 - es, 0:step], escan[:, es, 0:step])
                    then(tt(escan[:, 1 - es, step:], escan[:, es, step:], escan[:, es, 0:8 - step], ALU.add))
                    es = 1 - es
                upto = escan[:, es, :]
                then(tt(escan[:, 2, :], upto, escan[:, 3, :], ALU.subtract))
                then(ts(escan[:, 2, :], escan[:, 2, :], float(P), None, ALU.mult))
                where = scan[:, 1 - at]
                flat = lambda ap: ap.rearrange("p t e -> p (t e)")
                then(tt(flat(where), flat(scan[:, at]), PS[:, 7, P:2 * P], ALU.subtract))
                then(tt(flat(where), flat(where), PS[:, 7, 0:P], ALU.add))
                then(tt(where, where, escan[:, 2, :].unsqueeze(1).broadcast_to([P, TILES, 8]), ALU.add))
                for m in range(2):
                    then(tt(eq[:, m], eq[:, m], where, ALU.mult))
                    then(nc.vector.tensor_reduce(posf[:, m, :], eq[:, m], AX.X, ALU.add))
                nc.vector.tensor_copy(pos[:], posf[:]).then_inc(placed, 1)
                join = lambda ap: ap.rearrange("p m t -> p (m t)")
                n = 2 * TILES
                then(ts(tile_of[:], posf[:], 1.0 / P, -63.5 / P, ALU.mult, ALU.add))
                then(ts(tile_of[:], tile_of[:], MAGIC, -MAGIC, ALU.add, ALU.add))
                then(nc.vector.scalar_tensor_tensor(row_of[:], tile_of[:], -float(P), posf[:], ALU.mult, ALU.add))
                in_tile = eq[:].rearrange("p m t e -> p (m t) e")[:, :, 0:AHEAD]
                tt(in_tile, iotas[:, 0:AHEAD].unsqueeze(1).broadcast_to([P, n, AHEAD]),
                   join(tile_of[:]).unsqueeze(2).broadcast_to([P, n, AHEAD]), ALU.is_equal)
                then(tt(in_row[:], iotas[:].unsqueeze(1).broadcast_to([P, n, P]),
                        join(row_of[:]).unsqueeze(2).broadcast_to([P, n, P]), ALU.is_equal))
                ts(ids[:, :, 0:AHEAD], in_tile, col("part"), None, ALU.mult)
                for m in range(2):
                    at = slice(m * TILES, (m + 1) * TILES)
                    ins = tt(ids[:, at, AHEAD:], in_tile[:, at, :], iotas[:, 0:TILES].unsqueeze(2).broadcast_to([P, TILES, AHEAD]),
                             ALU.mult)
                ins.then_inc(hot_done, 1)
                dve.wait_ge(route_e[l], 1)
                then(ts(gt[:, 4, :], gt[:, 3, :], 1.0, None, ALU.add))
                then(nc.vector.reciprocal(gt[:, 5, :], gt[:, 4, :]))
                then(ts(gt[:, 6, :], gt[:, 5, :], tg[:, 4 + l:5 + l], None, ALU.mult))
                then(tt(gt[:, 7, :], gt[:, 6, :], gt[:, 3, :], ALU.mult))
                dve.wait_ge(idx_mm, l)
                then(nc.vector.tensor_copy(tile_of[:, 0, 0:AHEAD], PS[:, 6, 0:AHEAD]))
                nc.vector.scalar_tensor_tensor(idx[:], PS[:, 6, AHEAD:2 * AHEAD], float(P), tile_of[:, 0, 0:AHEAD],
                                               ALU.mult, ALU.add).then_inc(idx_done, 1)
                for e in range(8):
                    if e == 0:
                        then(ts(tile_e[:, 0, :], iotas[:, 0:NT], escan[:, es, 0:1], None, ALU.is_ge))
                    else:
                        then(nc.vector.scalar_tensor_tensor(tile_e[:, e % 2, :], iotas[:, 0:NT], escan[:, es, e:e + 1],
                                                            tile_e[:, 1 - e % 2, :], ALU.is_ge, ALU.add))
                of, half, odd = tile_e[:, 0, :], tile_e[:, 1, :], tile_e[:, 2, :]
                then(ts(of, tile_e[:, 1, :], float(EXPERTS - 1), None, ALU.min))
                then(ts(half, of, 0.5, -0.25, ALU.mult, ALU.add))
                then(ts(half, half, MAGIC, -MAGIC, ALU.add, ALU.add))
                then(nc.vector.scalar_tensor_tensor(odd, half, -2.0, of, ALU.mult, ALU.add))
                ts(table[0:1, 0, :], of[0:1], 1.0 + EXPERTS * (l - 1), None, ALU.add)
                ts(table[0:1, 1, :], odd[0:1], float(RING), None, ALU.mult)
                ts(upto_e[:], upto[0:1], 1.0 + (NT + 1) * (l - 1), None, ALU.add)
                ts(is_e[:], of[0:16], col("expert16", 0, 16), None, ALU.is_equal).then_inc(tables, 1)

            def split_biases(l):
                n = NJ[l] * P
                dve.wait_ge(bias_in, 32 * l)
                for r, (v, h, o) in enumerate(((b1f[:, 0:n], bh[:, 0:n], b1s[:, 0:n]), (b2g[:], bh[:, 0:D], b2t[:]))):
                    nc.vector.tensor_copy(h, v).then_inc(bias_v, 1)
                    dve.wait_ge(bias_v, 4 * (l - 1) + 2 * r + 1)
                    nc.vector.scalar_tensor_tensor(o, h.bitcast(F32), col("low16", 0, 16), v, ALU.mult, ALU.add
                                                   ).then_inc(bias_v, 1)
                    dve.wait_ge(bias_v, 4 * (l - 1) + 2 * r + 2)

            def sparse(l):
                nh = NJ[l] // 4
                n0, h0 = NT * (l - 1), NT * (NJ[1] // 4) * (l - 1)
                t0 = (NT + 1) * (l - 1) + 1

                def a(i, p):
                    dve.wait_ge(xh_done, n0 + i + 1)
                    for c in range(KC):
                        ps, h, o = PS[:, 0, c * P:(c + 1) * P], xh[:, p, c].bitcast(F32), xl[:, p, c]
                        if l == 1:
                            ins = nc.vector.tensor_tensor(o, ps, h, ALU.subtract)
                        else:
                            ins = nc.vector.scalar_tensor_tensor(o, ps, col("norm_w", c), h, ALU.mult, ALU.subtract)
                    ins.then_inc(xl_done, 1)

                def b(i, q):
                    dve.wait_ge(split_done, dve.value_load(table[0:1, 0, ds(i, 1)], min_val=1, max_val=2 * EXPERTS))
                    nc.vector.tensor_copy(of_e[:, q, :], is_e[:, ds(i, 1)].bitcast(F32).broadcast_to([16, P])).then_inc(e_done, 1)

                def d(i):
                    for h in range(nh):
                        dve.wait_ge(hh_done, h0 + nh * i + h + 1)
                        at = slice(4 * h, 4 * h + 4)
                        nc.vector.tensor_tensor(hl[:, at].rearrange("p j t -> p (j t)"), PS[:, 3 + h, :],
                                                hh[:, at].rearrange("p j t -> p (j t)").bitcast(F32), ALU.subtract
                                                ).then_inc(hl_done, 1)

                def e(i, p, turn):
                    dve.wait_ge(tiles_done, t0 + i + 1)
                    before = ((NT + 1) // 2 if p == 0 else NT // 2) * (l - 1) + turn - 1
                    if not (isinstance(turn, int) and before == 0):
                        dve.wait_ge(ys_out[p], 16 * before)
                    nc.vector.tensor_copy(yo[:, p], PS[:, 5, 0:D]).then_inc(yo_done, 1)
                dve.wait_ge(tables, l)
                b(0, 0)
                a(0, 0)
                b(1, 1)
                a(1, 1)

                def turn(i):
                    d(i - 1)
                    if i + 1 < NT:
                        b(i + 1, (i + 1) % 4)
                        a(i + 1, (i + 1) % 2)
                    e(i - 1, (i - 1) % 2, (i - 1) // 2 + 1)
                turn(1)
                turn(2)
                n = (NT - 4) // 4
                with dve.Fori(0, n) as k:
                    for q in range(4):
                        i = 4 * k + q + 3
                        d(i - 1)
                        b(i + 1, q)
                        a(i + 1, q % 2)
                        e(i - 1, q % 2, 2 * k + q // 2 + 2)
                for i in range(4 * n + 3, NT + 1):
                    turn(i)
                keys_values(l + 1, 0)
                for k in range(FED[l]):
                    t = k // 2
                    dve.wait_ge(yg_in[k % 8], 16 * (FED[l] // 8 * (l - 1) + k // 8 + 1))
                    if k % 2:
                        dve.wait_ge(y_done[l], k)
                    nc.vector.scalar_tensor_tensor(x_res[:, t, :], yg[:, k, :], gt[:, 6 + k % 2, t:t + 1], x_res[:, t, :],
                                                   ALU.mult, ALU.add).then_inc(y_done[l], 1)
                    if k % 8 > 1 and k % 2:
                        stats(2 * l + 2, t - 1)
                    if k % 8 == 7:
                        g = k // 8
                        dve.wait_ge(y_done[l], k + 1)
                        stats(2 * l + 2, t)
                        group_variances(2 * l + 2, g)
                        if g >= 2:
                            queries(l + 1, g - 2)
                        if g + 1 < GROUPS:
                            keys_values(l + 1, g + 1)
                        group_scales(2 * l + 2, g)
                        layernorm(l + 1, 2 * l + 2, g)
                for g in range(GROUPS - 2, GROUPS):
                    queries(l + 1, g)

            def split_b2():
                dve.wait_ge(b2_in, 16)
                nc.vector.tensor_copy(b2h[:], b2f[:]).then_inc(prep, 1)
                dve.wait_ge(prep, 1)
                nc.vector.scalar_tensor_tensor(b2s[:], b2h[:].bitcast(F32), col("low", 0, 2), b2f[:],
                                               ALU.mult, ALU.add).then_inc(prep, 1)

            def feed():
                for n in range(GROUPS):
                    for j in range(NJ[0]):
                        q = NJ[0] * n + j
                        dve.wait_ge(h0h_done, q + 1)
                        nc.vector.tensor_tensor(h0l[:, q % 3, :], h0f[:, q % 2, :], h0h[:, q % 3, :].bitcast(F32), ALU.subtract
                                                ).then_inc(h0l_done, 1)
                        if j == 2 and n:
                            add_feed(n - 1)
                        if j == 4 and n and 2 < upto:
                            feed_stats(n - 1)
                add_feed(GROUPS - 1)
                if 2 < upto:
                    feed_stats(GROUPS - 1)

            def feed_stats(n):
                dve.wait_ge(y_done[0], 4 * n + 4)
                for t in range(4):
                    stats(2, 4 * n + t)

            def add_feed(n):
                dve.wait_ge(y_mm[0], NJ[0] * (n + 1))
                for t in range(4):
                    x = x_res[:, 4 * n + t, :]
                    nc.vector.scalar_tensor_tensor(x, PS[:, 2 * (n % 2) + t // 2, (t % 2) * D:(t % 2 + 1) * D], tg[:, 4:5], x,
                                                   ALU.mult, ALU.add).then_inc(y_done[0], 1)

            def quantised():
                def chunks(g, cs):
                    if g >= GROUPS:
                        return
                    for c in cs:
                        if g == 0 and c == 0:
                            dve.wait_ge(bc_done, GROUPS)
                        if g >= 2 and c == 0:
                            dve.wait_ge(silu_done, NJ3 * (g - 1))
                        dve.wait_ge(h_mm[3], NJ3 * g + c + 1)
                        nc.vector.tensor_tensor(hid[:, g % 2, c, :], PS[:, 4 + c % 2, :], bcast[:, g, :], ALU.mult
                                                ).then_inc(h_done[3], 1)

                def taps(g, *cs):
                    if g == GROUPS:
                        return
                    two = lambda ap: ap.rearrange("p (b t) -> p b t", b=2)
                    for c in cs:
                        n = len(CONV_DVE) * g + CONV_DVE.index(c)
                        h, y = two(hid[:, g % 2, c, :]), two(act3[:, g % 2, c, :])
                        dve.wait_ge(tap_done, n + 1)
                        nc.vector.scalar_tensor_tensor(y[:, :, 1:S], h[:, :, 0:S - 1], col("conv_w", c), y[:, :, 1:S],
                                                       ALU.mult, ALU.add).then_inc(cv_v, 1)
                    for c in cs:
                        n = len(CONV_DVE) * g + CONV_DVE.index(c)
                        h, y = two(hid[:, g % 2, c, :]), two(act3[:, g % 2, c, :])
                        dve.wait_ge(cv_v, n + 1)
                        nc.vector.scalar_tensor_tensor(y[:, :, 0:S - 1], h[:, :, 1:S], col("conv_w", 2 * NJ3 + c),
                                                       y[:, :, 0:S - 1], ALU.mult, ALU.add).then_inc(cv_done, 1)
                k = 0

                def then(ins):
                    nonlocal k
                    k += 1
                    ins.then_inc(q3_p, 1)
                    dve.wait_ge(q3_p, k)

                def add(g):
                    for t in range(4):
                        x = x_res[:, 4 * g + t, :]
                        if t % 2 == 0:
                            dve.wait_ge(y_mm[3], 2 * g + t // 2 + 1)
                        nc.vector.scalar_tensor_tensor(x, PS[:, t // 2, (t % 2) * D:(t % 2 + 1) * D], q3g[:, g % 2, 1, t:t + 1],
                                                       x, ALU.mult, ALU.add).then_inc(y_done[3], 1)
                chunks(0, range(6))
                taps(0, 1)
                chunks(0, range(6, NJ3))
                taps(0, 6, 7)
                chunks(1, range(2))
                for g in range(GROUPS):
                    q = lambda n: q3g[:, g % 2, n, :]
                    a = act3[:, g % 2]
                    dve.wait_ge(silu_done, NJ3 * (g + 1))
                    then(nc.vector.tensor_reduce(amx[:], a.rearrange("p c t -> p t c"), AX.X, ALU.max,
                                                 apply_absolute_value=True))
                    chunks(g + 1, range(2, 4))
                    dve.wait_ge(amx_mm, g + 1)
                    then(nc.vector.tensor_reduce(q(1), PS[:, 2, :].rearrange("p (t n) -> p t n", t=4), AX.X, ALU.max))
                    then(nc.vector.tensor_scalar(q(3), q(1), 1e-5, 1.0 / 127.0, ALU.max, ALU.mult))
                    then(nc.vector.reciprocal(q(2), q(3)))
                    then(nc.vector.tensor_scalar(q(1), q(3), q3[:, 6:7], None, ALU.mult))
                    chunks(g + 1, range(4, NJ3))
                    taps(g + 1, 1)
                    dve.wait_ge(hrow_mm, g + 1)
                    for h in range(2):
                        at = slice(h * 256, (h + 1) * 256)
                        nc.vector.tensor_tensor(a[:, :, at], a[:, :, at], PS[:, 3, at].unsqueeze(1).broadcast_to([P, NJ3, 256]),
                                                ALU.mult).then_inc(q3_p, 1)
                    for h in range(2):
                        at = slice(h * 256, (h + 1) * 256)
                        dve.wait_ge(q3_p, k + h + 1)
                        nc.vector.tensor_scalar(a[:, :, at], a[:, :, at], 127.0, MAGIC, ALU.min, ALU.add).then_inc(q3_p, 1)
                    k += 4
                    assert k == Q3P * (g + 1)
                    taps(g + 1, 6, 7)
                    if g:
                        add(g - 1)
                    chunks(g + 2, range(2))
                add(GROUPS - 1)

            for l in lo_l:
                project(l)
                if l:
                    split_bo(l)
                if l == 3 and ffn(3):
                    ternary_sums()
                for k in range(2 * PAIRS):
                    attend_turn(l, 0, k)
                with dve.Fori(1, B // 2) as i:
                    for k in range(2 * PAIRS):
                        attend_turn(l, i, k)
                for k in range(5):
                    attend_turn(l, B // 2, k, last=True)
                if l == 0:
                    add_out0(B - 1)
                    stats_out0(B - 1)
                else:
                    add_out(l, ternary() if l == 3 and ffn(3) else [])
                if not ffn(l):
                    continue
                u = 2 * l + 1
                scales(l, u)
                if l == 3:
                    layernorm_quantised(u)
                elif l == 0:
                    split_b2()
                    layernorm(l, u, 0)
                    for g in range(GROUPS):
                        if g + 1 < GROUPS:
                            layernorm(l, u, g + 1)
                        dve.wait_ge(xT_done, g + 1)
                        at = slice(g * 512, (g + 1) * 512)
                        nc.vector.tensor_tensor(x0l[:, :, at], PS[:, xT_bank(1, g):xT_bank(1, g) + 2, :], x0h[:, :, at].bitcast(F32), ALU.subtract
                                                ).then_inc(x0l_done, 1)
                else:
                    for g in range(GROUPS):
                        layernorm(l, u, g)
                if l in (1, 2):
                    split_biases(l)
                    route(l)
                if l == 0:
                    feed()
                elif l < 3:
                    plan(l)
                    sparse(l)
                else:
                    quantised()


def constants():
    sel = np.zeros((P, 4, 4, P), np.float32)
    rows = {0: (0, 2), 1: (1,), 2: (0, 1), 3: (2,)}
    for part, blocks in rows.items():
        for v in range(4):
            for h in range(2):
                for r in blocks:
                    for d in range(DH):
                        sel[32 * v + DH * h + d, part, v, 64 * h + DH * r + (r == 2) + d] = 1.0
    return {"sel": sel.reshape(P, 16 * P), "ident": np.eye(P, dtype=np.float32),
            "tri": np.triu(np.ones((P, P), np.float32), 1),
            "iotas": np.ascontiguousarray(np.broadcast_to(np.arange(P, dtype=np.float32), (P, P)))}


def layout(a):
    c = np.ascontiguousarray
    columns = lambda v: v.reshape(-1, P).T
    rows = lambda v, n: c(np.broadcast_to(v, (n,) + v.shape))
    table = [
        np.broadcast_to(np.concatenate([a["g_xattn"], a["g_ffn"]]), (P, 8)),
        columns(a["L1_xattn_bq"]), columns(a["L1_xattn_bk"]), columns(a["L3_xattn_bq"]),
        columns(a["L3_xattn_bkv"][:D]), columns(a["L0_ffn_light_gamma"]), columns(a["L0_ffn_heavy_gamma"]),
        columns(np.concatenate([a["L0_ffn_light_b1"], a["L0_ffn_heavy_b1"]])), columns(a["L2_ffn_norm_weight"]),
        *[columns(a["L3_ffn_conv_w"][:, 0, tap]) for tap in range(3)], columns(a["L3_ffn_conv_b"]),
        np.where(np.arange(P) == 1, -1.0, 0.0).astype(np.float32).reshape(P, 1),
        np.where(np.arange(P) // 8 == 1, -1.0, 0.0).astype(np.float32).reshape(P, 1),
        (np.arange(P) % 8).astype(np.float32).reshape(P, 1),
        (np.arange(P) % 64 == MAXROW).astype(np.float32).reshape(P, 1),
        np.arange(P, dtype=np.float32).reshape(P, 1),
    ]
    ctx = a["ctx_1024"].reshape(T, D)
    mask = a["mask_Bx1xSxS2_ik1"].reshape(B, S, S)
    wkv = a["L3_xattn_Wkv"]
    out = constants()
    out.update({
        "x": c(a["x"].reshape(T, D)), "ctx": c(ctx), "ctxT": c(ctx.T),
        "mask": c(mask.reshape(T, S)), "maskT": c(mask.transpose(0, 2, 1).reshape(T, S)),
        "cols": c(np.concatenate(table, axis=1)),
        "wproj_1": c(np.stack([a[f"L1_xattn_W{n}"].T for n in "qkvo"])),
        "wproj_2": c(np.stack([a[f"L2_xattn_W_{n}"] for n in "qkvo"])),
        "wproj_3": c(np.stack([a["L3_xattn_Wq"], wkv[:, :D], wkv[:, D:], a["L3_xattn_Wo"]])),
        "bo_1": rows(a["L1_xattn_bo"], 2), "bo_2": rows(a["L2_xattn_b_o"], 2),
        "bo_3": rows(a["L3_xattn_bo"], 2),
        "bv_1": rows(a["L1_xattn_bv"], P), "bv_3": rows(a["L3_xattn_bkv"][D:], P),
        "W1_0": c(np.concatenate([a["L0_ffn_light_w1"], a["L0_ffn_heavy_w1"]], axis=1)),
        "W2_0": c(np.concatenate([a["L0_ffn_light_w2"], a["L0_ffn_heavy_w2"]], axis=0)),
        "b2_0": rows(np.stack([a["L0_ffn_light_b2"], a["L0_ffn_heavy_b2"]]), 2),
        "W1_1": c(a["L1_ffn_W1"].reshape(EXPERTS * D, -1)), "W2_1": c(a["L1_ffn_W2"].reshape(-1, D)),
        "wg_1": c(a["L1_ffn_Wr"]), "b2_1": c(np.tile(a["L1_ffn_b2"], (2, 1))),
        "b1_1": c(np.tile(a["L1_ffn_b1"], (2, 1))), "b1_2": c(np.tile(a["L2_ffn_b1"], (2, 1))),
        "W1_2": c(a["L2_ffn_w1"].transpose(0, 2, 1).reshape(EXPERTS * D, -1)),
        "W2_2": c(a["L2_ffn_w2"].transpose(0, 2, 1).reshape(-1, D)),
        "wg_2": c(a["L2_ffn_gate_w"].T), "b2_2": c(np.tile(a["L2_ffn_b2"], (2, 1))),
        "W1_3": c(a["L3_ffn_w1"].T), "W2_3": c(a["L3_ffn_w2"].T),
    })
    return out


def kernel(**inputs):
    import concourse.bacc as bacc
    from concourse.bass_utils import run_bass_kernel_spmd

    arrays = layout(inputs)
    nc = bacc.Bacc("TRN2", target_bir_lowering=False, num_devices=1)
    io = {name: nc.dram_tensor(name + "_dram", a.shape, mybir.dt.from_np(a.dtype), kind="ExternalInput").ap()
          for name, a in arrays.items()}
    io["out"] = nc.dram_tensor("out_dram", (T, D), F32, kind="ExternalOutput").ap()
    build(nc, io)
    got = run_bass_kernel_spmd(nc, [{name + "_dram": a for name, a in arrays.items()}], core_ids=[0])
    return got.results[0]["out_dram"].reshape(B, S, D)
```
